# Optimizing a Trainium2 kernel written in Bass

```python
import numpy as np
import jax
import jax.numpy as jnp

def _softmax(x, axis=-1):
    return jax.nn.softmax(x, axis=axis)

def _gelu(x):
    return jax.nn.gelu(x, approximate=True)

def _silu(x):
    return jax.nn.silu(x)

def _sigmoid(x):
    return jax.nn.sigmoid(x)

def _layernorm(x, axis=-1, eps=1e-05):
    m = jnp.mean(x, axis=axis, keepdims=True)
    v = jnp.var(x, axis=axis, keepdims=True)
    return (x - m) / jnp.sqrt(v + eps)

def _scatter_add(tgt, idx, src, axis=0):
    return tgt.at[idx].add(src)

def _segment_sum(src, seg, n):
    return jax.ops.segment_sum(src, seg, n)
kernel_name = 'mk_decoder_postln_d1_seqx_r4_9bcf09'

def setup_inputs(seed: int=0):
    np.random.seed(seed)
    _w = jnp.asarray

    def _rec_inputs():
        import jax
        import jax.numpy as jnp
        _rk = jax.random.key(seed)
        x = -0.0005207 + 1.001 * jax.random.normal(jax.random.fold_in(_rk, 1), (8, 256, 256), jnp.float32)
        _lenS = 256 - jax.random.randint(jax.random.fold_in(_rk, 7), (8,), 0, max(1, 256 // 4) + 1, jnp.int32)
        _lenS2 = 120 - jax.random.randint(jax.random.fold_in(_rk, 8), (8,), 0, max(1, 120 // 4) + 1, jnp.int32)
        _ctx_1024P = jax.random.normal(jax.random.fold_in(_rk, 11), (8, 16, 256), jnp.float32)
        _ctx_1024c = jax.random.dirichlet(jax.random.fold_in(_rk, 511), 0.3 * jnp.ones((16,), jnp.float32), (8, 120))
        _ctx_1024t = jnp.einsum('bsk,bkd->bsd', _ctx_1024c, _ctx_1024P)
        _ctx_1024t = _ctx_1024t * jax.lax.rsqrt(jnp.mean(jnp.square(_ctx_1024t)) + 1e-12) * 0.953939
        ctx_1024 = -5.72187e-05 + 0.999849 * (_ctx_1024t + 0.3 * jax.random.normal(jax.random.fold_in(_rk, 611), (8, 120, 256), jnp.float32))
        return (x, ctx_1024)
    x, ctx_1024 = _rec_inputs()

    def _L0_attn_setup():
        import jax, jax.numpy as jnp
        import numpy as np
        B, T, DIM = (2, 1024, 256)
        DEPTH, HEADS = (4, 8)
        DH = DIM // HEADS
        NLOCAL, WINDOW, BUCKET = (4, 128, 64)
        MULT = 4

        def layer_norm(x, g, b, eps=1e-05):
            m = jnp.mean(x, -1, keepdims=True)
            v = jnp.mean(jnp.square(x - m), -1, keepdims=True)
            return (x - m) * jax.lax.rsqrt(v + eps) * g + b

        def causal_linear_attn(q, k, v):
            b, h, n, e = q.shape
            u = n // BUCKET
            q = jax.nn.softmax(q, axis=-1)
            k = jax.nn.elu(k) + 1.0
            bq = q.reshape(b, h, u, BUCKET, e)
            bk = k.reshape(b, h, u, BUCKET, e)
            bv = v.reshape(b, h, u, BUCKET, e)
            k_cum = jnp.cumsum(bk.sum(axis=-2), axis=-2)
            ctx = jnp.einsum('bhund,bhune->bhude', bk, bv)
            ctx = jnp.cumsum(ctx, axis=2)
            ctx = ctx / (k_cum[..., None] + 1e-06)
            ctx = jnp.pad(ctx, ((0, 0), (0, 0), (1, 0), (0, 0), (0, 0)))[:, :, :-1]
            out = jnp.einsum('bhund,bhude->bhune', bq, ctx)
            return out.reshape(b, h, n, e)

        def local_attn(q, k, v):
            b, lh, t, e = q.shape
            bh = b * lh
            nb = t // WINDOW
            bq = q.reshape(bh, nb, WINDOW, e)
            bk = k.reshape(bh, nb, WINDOW, e)
            bv = v.reshape(bh, nb, WINDOW, e)

            def look_around(x):
                padded = jnp.pad(x, ((0, 0), (1, 0), (0, 0), (0, 0)))
                return jnp.concatenate([padded[:, :-1], padded[:, 1:]], axis=2)
            bk2 = look_around(bk)
            bv2 = look_around(bv)
            tix = jnp.arange(t).reshape(1, nb, WINDOW)
            tpad = jnp.pad(tix, ((0, 0), (1, 0), (0, 0)), constant_values=-1)
            kix = jnp.concatenate([tpad[:, :-1], tpad[:, 1:]], axis=2)
            dots = jnp.einsum('bwie,bwje->bwij', bq, bk2) * e ** (-0.5)
            mask_value = -jnp.finfo(dots.dtype).max
            causal_mask = tix[:, :, :, None] < kix[:, :, None, :]
            pad_mask = (kix == -1)[:, :, None, :]
            dots = jnp.where(causal_mask | pad_mask, mask_value, dots)
            attn = jax.nn.softmax(dots, axis=-1)
            out = jnp.einsum('bwij,bwje->bwie', attn, bv2)
            return out.reshape(b, lh, t, e)

        def self_attention(x, Wq, Wk, Wv, Wo, bo):
            b, t, _ = x.shape
            mh = lambda z: z.reshape(b, t, HEADS, DH).transpose(0, 2, 1, 3)
            q, k, v = (mh(x @ Wq), mh(x @ Wk), mh(x @ Wv))
            lo = local_attn(q[:, :NLOCAL], k[:, :NLOCAL], v[:, :NLOCAL])
            go = causal_linear_attn(q[:, NLOCAL:], k[:, NLOCAL:], v[:, NLOCAL:])
            out = jnp.concatenate([lo, go], axis=1)
            out = out.transpose(0, 2, 1, 3).reshape(b, t, DIM)
            return out @ Wo + bo
        key = jax.random.key(seed)
        ks = jax.random.split(key, 8)
        s = 0.02
        rn = lambda k, shape: jax.random.normal(k, shape, dtype=jnp.float32) * s
        return {'x': jax.random.normal(ks[0], (B, T, DIM), dtype=jnp.float32), 'Wq': rn(ks[1], (DEPTH, DIM, DIM)), 'Wk': rn(ks[2], (DEPTH, DIM, DIM)), 'Wv': rn(ks[3], (DEPTH, DIM, DIM)), 'Wo': rn(ks[4], (DEPTH, DIM, DIM)), 'bo': jnp.zeros((DEPTH, DIM), jnp.float32), 'ln1_g': jnp.ones((DEPTH, DIM), jnp.float32), 'ln1_b': jnp.zeros((DEPTH, DIM), jnp.float32), 'W1': rn(ks[5], (DEPTH, DIM, DIM * MULT)), 'b1': jnp.zeros((DEPTH, DIM * MULT), jnp.float32), 'W2': rn(ks[6], (DEPTH, DIM * MULT, DIM)), 'b2': jnp.zeros((DEPTH, DIM), jnp.float32), 'ln2_g': jnp.ones((DEPTH, DIM), jnp.float32), 'ln2_b': jnp.zeros((DEPTH, DIM), jnp.float32)}
    _L0_attn_all = _L0_attn_setup()
    _L0_attn_in = {k: v for k, v in _L0_attn_all.items() if k in ('Wq', 'Wk', 'Wv', 'Wo', 'bo', 'ln1_g', 'ln1_b', 'W1', 'b1', 'W2', 'b2', 'ln2_g', 'ln2_b')}
    del _L0_attn_all

    def _L0_xattn_setup():
        import jax, jax.numpy as jnp
        import numpy as np
        key = jax.random.key(seed)
        ks = jax.random.split(key, 5)
        b, n_q, n_kv = (16, 128, 1024)
        query_dim, context_dim, heads, dim_head = (256, 256, 16, 64)
        inner = heads * dim_head
        x = jax.random.normal(ks[0], (b, n_q, query_dim), dtype=jnp.float32)
        context = jax.random.normal(ks[1], (b, n_kv, context_dim), dtype=jnp.float32)
        Wq = jax.random.normal(ks[2], (query_dim, inner), dtype=jnp.float32) * query_dim ** (-0.5)
        Wkv = jax.random.normal(ks[3], (context_dim, 2 * inner), dtype=jnp.float32) * context_dim ** (-0.5)
        Wout = jax.random.normal(ks[4], (inner, query_dim), dtype=jnp.float32) * inner ** (-0.5)
        bout = jnp.zeros((query_dim,), dtype=jnp.float32)
        return {'x': x, 'context': context, 'Wq': Wq, 'Wkv': Wkv, 'Wout': Wout, 'bout': bout}
    _L0_xattn_all = _L0_xattn_setup()
    _L0_xattn_in = {k: v for k, v in _L0_xattn_all.items() if k in ('Wq', 'Wkv', 'Wout', 'bout')}
    del _L0_xattn_all

    def _L0_ffn_setup():
        import jax, jax.numpy as jnp
        import numpy as np
        TOP_K = 32
        TEMPERATURE = 1.0
        PARAM_SCALE = 0.02

        def _compose_weight(logits, A, B):
            vals, idx = jax.lax.top_k(logits, TOP_K)
            w = jax.nn.softmax(vals / TEMPERATURE)
            A_sel = A[idx]
            B_sel = B[idx]
            return jnp.einsum('k,kir,kro->io', w, A_sel, B_sel)
        key = jax.random.key(seed)
        ks = jax.random.split(key, 7)
        B, S, D, F, P, R = (2, 256, 256, 1024, 64, 64)
        x = jax.random.normal(ks[0], (B, S, D), dtype=jnp.float32)
        fc1_A = jax.random.normal(ks[1], (P, D, R), dtype=jnp.float32) * PARAM_SCALE
        fc1_B = jax.random.normal(ks[2], (P, R, F), dtype=jnp.float32) * PARAM_SCALE
        fc2_A = jax.random.normal(ks[3], (P, F, R), dtype=jnp.float32) * PARAM_SCALE
        fc2_B = jax.random.normal(ks[4], (P, R, D), dtype=jnp.float32) * PARAM_SCALE
        fc1_logits = jax.random.normal(ks[5], (P,), dtype=jnp.float32)
        fc2_logits = jax.random.normal(ks[6], (P,), dtype=jnp.float32)
        return {'x': x, 'fc1_A': fc1_A, 'fc1_B': fc1_B, 'fc2_A': fc2_A, 'fc2_B': fc2_B, 'fc1_logits': fc1_logits, 'fc2_logits': fc2_logits}
    _L0_ffn_all = _L0_ffn_setup()
    _L0_ffn_in = {k: v for k, v in _L0_ffn_all.items() if k in ('fc1_A', 'fc1_B', 'fc2_A', 'fc2_B', 'fc1_logits', 'fc2_logits')}
    del _L0_ffn_all
    return {'x': x, 'ctx_1024': ctx_1024, 'L0_attn_Wq': _L0_attn_in['Wq'], 'L0_attn_Wk': _L0_attn_in['Wk'], 'L0_attn_Wv': _L0_attn_in['Wv'], 'L0_attn_Wo': _L0_attn_in['Wo'], 'L0_attn_bo': _L0_attn_in['bo'], 'L0_attn_ln1_g': _L0_attn_in['ln1_g'], 'L0_attn_ln1_b': _L0_attn_in['ln1_b'], 'L0_attn_W1': _L0_attn_in['W1'], 'L0_attn_b1': _L0_attn_in['b1'], 'L0_attn_W2': _L0_attn_in['W2'], 'L0_attn_b2': _L0_attn_in['b2'], 'L0_attn_ln2_g': _L0_attn_in['ln2_g'], 'L0_attn_ln2_b': _L0_attn_in['ln2_b'], 'L0_xattn_Wq': _L0_xattn_in['Wq'], 'L0_xattn_Wkv': _L0_xattn_in['Wkv'], 'L0_xattn_Wout': _L0_xattn_in['Wout'], 'L0_xattn_bout': _L0_xattn_in['bout'], 'L0_ffn_fc1_A': _L0_ffn_in['fc1_A'], 'L0_ffn_fc1_B': _L0_ffn_in['fc1_B'], 'L0_ffn_fc2_A': _L0_ffn_in['fc2_A'], 'L0_ffn_fc2_B': _L0_ffn_in['fc2_B'], 'L0_ffn_fc1_logits': _L0_ffn_in['fc1_logits'], 'L0_ffn_fc2_logits': _L0_ffn_in['fc2_logits']}

def reference(x, ctx_1024, L0_attn_Wq, L0_attn_Wk, L0_attn_Wv, L0_attn_Wo, L0_attn_bo, L0_attn_ln1_g, L0_attn_ln1_b, L0_attn_W1, L0_attn_b1, L0_attn_W2, L0_attn_b2, L0_attn_ln2_g, L0_attn_ln2_b, L0_xattn_Wq, L0_xattn_Wkv, L0_xattn_Wout, L0_xattn_bout, L0_ffn_fc1_A, L0_ffn_fc1_B, L0_ffn_fc2_A, L0_ffn_fc2_B, L0_ffn_fc1_logits, L0_ffn_fc2_logits):
    import jax
    import jax.numpy as jnp

    def _L0_attn_ref(x, Wq, Wk, Wv, Wo, bo, ln1_g, ln1_b, W1, b1, W2, b2, ln2_g, ln2_b):
        import jax, jax.numpy as jnp
        import numpy as np
        B, T, DIM = (2, 1024, 256)
        DEPTH, HEADS = (4, 8)
        DH = DIM // HEADS
        NLOCAL, WINDOW, BUCKET = (4, 128, 64)
        MULT = 4

        def layer_norm(x, g, b, eps=1e-05):
            m = jnp.mean(x, -1, keepdims=True)
            v = jnp.mean(jnp.square(x - m), -1, keepdims=True)
            return (x - m) * jax.lax.rsqrt(v + eps) * g + b

        def causal_linear_attn(q, k, v):
            b, h, n, e = q.shape
            u = n // BUCKET
            q = jax.nn.softmax(q, axis=-1)
            k = jax.nn.elu(k) + 1.0
            bq = q.reshape(b, h, u, BUCKET, e)
            bk = k.reshape(b, h, u, BUCKET, e)
            bv = v.reshape(b, h, u, BUCKET, e)
            k_cum = jnp.cumsum(bk.sum(axis=-2), axis=-2)
            ctx = jnp.einsum('bhund,bhune->bhude', bk, bv)
            ctx = jnp.cumsum(ctx, axis=2)
            ctx = ctx / (k_cum[..., None] + 1e-06)
            ctx = jnp.pad(ctx, ((0, 0), (0, 0), (1, 0), (0, 0), (0, 0)))[:, :, :-1]
            out = jnp.einsum('bhund,bhude->bhune', bq, ctx)
            return out.reshape(b, h, n, e)

        def local_attn(q, k, v):
            b, lh, t, e = q.shape
            bh = b * lh
            nb = t // WINDOW
            bq = q.reshape(bh, nb, WINDOW, e)
            bk = k.reshape(bh, nb, WINDOW, e)
            bv = v.reshape(bh, nb, WINDOW, e)

            def look_around(x):
                padded = jnp.pad(x, ((0, 0), (1, 0), (0, 0), (0, 0)))
                return jnp.concatenate([padded[:, :-1], padded[:, 1:]], axis=2)
            bk2 = look_around(bk)
            bv2 = look_around(bv)
            tix = jnp.arange(t).reshape(1, nb, WINDOW)
            tpad = jnp.pad(tix, ((0, 0), (1, 0), (0, 0)), constant_values=-1)
            kix = jnp.concatenate([tpad[:, :-1], tpad[:, 1:]], axis=2)
            dots = jnp.einsum('bwie,bwje->bwij', bq, bk2) * e ** (-0.5)
            mask_value = -jnp.finfo(dots.dtype).max
            causal_mask = tix[:, :, :, None] < kix[:, :, None, :]
            pad_mask = (kix == -1)[:, :, None, :]
            dots = jnp.where(causal_mask | pad_mask, mask_value, dots)
            attn = jax.nn.softmax(dots, axis=-1)
            out = jnp.einsum('bwij,bwje->bwie', attn, bv2)
            return out.reshape(b, lh, t, e)

        def self_attention(x, Wq, Wk, Wv, Wo, bo):
            b, t, _ = x.shape
            mh = lambda z: z.reshape(b, t, HEADS, DH).transpose(0, 2, 1, 3)
            q, k, v = (mh(x @ Wq), mh(x @ Wk), mh(x @ Wv))
            lo = local_attn(q[:, :NLOCAL], k[:, :NLOCAL], v[:, :NLOCAL])
            go = causal_linear_attn(q[:, NLOCAL:], k[:, NLOCAL:], v[:, NLOCAL:])
            out = jnp.concatenate([lo, go], axis=1)
            out = out.transpose(0, 2, 1, 3).reshape(b, t, DIM)
            return out @ Wo + bo
        for i in range(DEPTH):
            x = x + self_attention(layer_norm(x, ln1_g[i], ln1_b[i]), Wq[i], Wk[i], Wv[i], Wo[i], bo[i])
            h = layer_norm(x, ln2_g[i], ln2_b[i])
            x = x + (jax.nn.gelu(h @ W1[i] + b1[i], approximate=False) @ W2[i] + b2[i])
        return x

    def _L0_xattn_ref(x, context, Wq, Wkv, Wout, bout):
        import jax, jax.numpy as jnp
        import numpy as np
        heads, dim_head = (16, 64)
        b, n_q, _ = x.shape
        n_kv = context.shape[1]
        scale = dim_head ** (-0.5)
        q = x @ Wq
        kv = context @ Wkv
        k, v = jnp.split(kv, 2, axis=-1)

        def split_heads(t):
            bb, n, _ = t.shape
            return t.reshape(bb, n, heads, dim_head).transpose(0, 2, 1, 3)
        q, k, v = map(split_heads, (q, k, v))
        i_idx = jnp.arange(n_q)[:, None]
        j_idx = jnp.arange(n_kv)[None, :]
        mask = j_idx % n_q == i_idx
        sim = jnp.einsum('bhid,bhjd->bhij', q, k) * scale
        max_neg = -jnp.finfo(sim.dtype).max
        sim = jnp.where(mask[None, None, :, :], sim, max_neg)
        attn = jax.nn.softmax(sim, axis=-1)
        out = jnp.einsum('bhij,bhjd->bhid', attn, v)
        out = out.transpose(0, 2, 1, 3).reshape(b, n_q, heads * dim_head)
        return out @ Wout + bout

    def _L0_ffn_ref(x, fc1_A, fc1_B, fc2_A, fc2_B, fc1_logits, fc2_logits):
        import jax, jax.numpy as jnp
        import numpy as np
        TOP_K = 32
        TEMPERATURE = 1.0
        PARAM_SCALE = 0.02

        def _compose_weight(logits, A, B):
            vals, idx = jax.lax.top_k(logits, TOP_K)
            w = jax.nn.softmax(vals / TEMPERATURE)
            A_sel = A[idx]
            B_sel = B[idx]
            return jnp.einsum('k,kir,kro->io', w, A_sel, B_sel)
        W1 = _compose_weight(fc1_logits, fc1_A, fc1_B)
        W2 = _compose_weight(fc2_logits, fc2_A, fc2_B)
        h = jax.nn.gelu(jnp.einsum('bsd,df->bsf', x, W1))
        return jnp.einsum('bsf,fd->bsd', h, W2)
    x = _layernorm(x + _L0_attn_ref(x, L0_attn_Wq, L0_attn_Wk, L0_attn_Wv, L0_attn_Wo, L0_attn_bo, L0_attn_ln1_g, L0_attn_ln1_b, L0_attn_W1, L0_attn_b1, L0_attn_W2, L0_attn_b2, L0_attn_ln2_g, L0_attn_ln2_b), axis=-1)
    x = _layernorm(x + _L0_xattn_ref(x, ctx_1024, L0_xattn_Wq, L0_xattn_Wkv, L0_xattn_Wout, L0_xattn_bout), axis=-1)
    x = _layernorm(x + _L0_ffn_ref(x, L0_ffn_fc1_A, L0_ffn_fc1_B, L0_ffn_fc2_A, L0_ffn_fc2_B, L0_ffn_fc1_logits, L0_ffn_fc2_logits), axis=-1)
    return x

_drawn_inputs = setup_inputs


def setup_inputs(seed=0):
    import zlib

    import numpy as np

    out = dict(_drawn_inputs(seed))
    spreads = {'L0_attn_bo': (0.0, 0.1),
     'L0_attn_ln1_g': (1.0, 0.6),
     'L0_attn_ln1_b': (0.0, 0.8),
     'L0_attn_b1': (0.0, 0.286),
     'L0_attn_b2': (0.0, 0.1),
     'L0_attn_ln2_g': (1.0, 0.6),
     'L0_attn_ln2_b': (0.0, 0.8),
     'L0_xattn_bout': (0.0, 0.1)}
    factors = {'L0_attn_Wq': 8.0,
     'L0_attn_Wk': 8.0,
     'L0_attn_Wv': 2.774,
     'L0_attn_Wo': 2.737,
     'L0_ffn_fc1_A': 8.0,
     'L0_ffn_fc1_B': 8.0,
     'L0_ffn_fc2_A': 8.0,
     'L0_ffn_fc2_B': 8.0,
     'L0_ffn_fc1_logits': 8.0,
     'L0_ffn_fc2_logits': 8.0}
    for name, (base, spread) in spreads.items():
        noise = np.random.default_rng([zlib.crc32(name.encode()), seed]).standard_normal(out[name].shape)
        drawn = base * np.exp(spread * noise) if base else spread * noise
        out[name] = jnp.asarray(drawn.astype(out[name].dtype))
    for name, factor in factors.items():
        out[name] = (out[name] * factor).astype(out[name].dtype)
    return out
```

```python
from contextlib import ExitStack

import concourse.bass as bass
from concourse import mybir

F32 = mybir.dt.float32
F32R = mybir.dt.float32r
BF16 = mybir.dt.bfloat16
I32 = mybir.dt.int32
ALU = mybir.AluOpType
ACT = mybir.ActivationFunctionType
AX_X = mybir.AxisListType.X

P = 128
B, T, D = 8, 256, 256
DC = D // P
DEPTH = 4
FF = 4 * D
FC = FF // P
E = 32
NH = 4
BUCKET = 64
TILES = 4
TOK = TILES * P
ITEMS = B * T // TOK
HB = E + 1
SCALE = float(E) ** -0.5
MASKED = -1.0e30
EPS = 1.0e-5
NKV = 120
CB = 128
PRIMS, TOPK, RANK = 64, 32, 64
PAIRS = TOPK // 2
PASSES = ((0, 0), (1, 0), (0, 1))


def build(nc, x_in, Wq, Wk, Wv, Wo, bo, ln1_g, ln1_b, W1, b1, W2, b2, ln2_g, ln2_b,
          ctx_in, Wkv, Wout, bout, fc1_A, fc1_B, fc2_A, fc2_B, fc1_logits, fc2_logits, out):
    with ExitStack() as ctx:
        def sb(name, shape, dt=F32):
            return ctx.enter_context(nc.sbuf_tensor(name, shape, dt))

        def sem(name):
            return ctx.enter_context(nc.semaphore(name))

        x = sb("x", [P, ITEMS * TILES, D])
        wa = sb("wa", [P, 2, DC, 768], F32R)
        wo = sb("wo", [P, 2, DC, D], F32R)
        w1 = sb("w1", [P, 2, DC, FF], F32R)
        w2 = sb("w2", [P, 2, FC, D], F32R)
        raw_a = sb("raw_a", [P, DC, 1024])
        raw_f = sb("raw_f", [P, 2048])
        vec_a = sb("vec_a", [P, 3, D])
        vec_f = sb("vec_f", [P, 3, D])
        b1c = sb("b1c", [P, DEPTH * FC])
        b1_now = sb("b1_now", [P, FC])
        carrier = sb("carrier", [P, 3])
        b1_rows = sb("b1_rows", [DEPTH * FC, P])
        slot_mark = sb("slot_mark", [P, 2])
        loaded_mark = sb("loaded_mark", [P, ITEMS * TILES])
        ident = sb("ident", [P, P])
        ident_bf = sb("ident_bf", [P, P], BF16)
        mask_bf = sb("mask_bf", [P, 3 * P], BF16)
        headmask = sb("headmask", [P, NH, E])
        ones = sb("ones", [P, 1])
        minus_half = sb("minus_half", [P, 4])
        xt = [sb("xt1", [P, 2, DC, TOK], F32R), sb("xt2", [P, 2, DC, TOK], F32R)]
        ht = sb("ht", [P, 2, FC, TOK], F32R)
        scratch = sb("scratch", [P, 9760])
        v8 = scratch[:, 0:1056].rearrange("p (t h e) -> p t h e", t=TILES, h=2 * NH)
        qk = scratch[:, 1056:2080].rearrange("p (t d) -> p t d", t=TILES)
        qexp = scratch[:, 2080:2592].rearrange("p (t d) -> p t d", t=TILES)
        kexp = scratch[:, 2592:3104].rearrange("p (t d) -> p t d", t=TILES)
        qnt = scratch[:, 3104:3616]
        prob = scratch[:, 3616:5152].rearrange("p (h k) -> p h k", h=NH)
        pt = scratch[:, 5152:6688].rearrange("p (r k) -> p r k", r=3)
        xh = [scratch[:, a:a + 1024].rearrange("p (t d) -> p t d", t=TILES) for a in (6688, 7712)]
        hf = scratch[:, 8736:9760].rearrange("p (s t) -> p s t", s=2)
        x0 = scratch[:, 0:4096].rearrange("p (t d) -> p t d", d=D)
        wvt = scratch[:, 0:2048].rearrange("p (j i) -> p j i", j=FC)
        wvo = scratch[:, 2048:2560].rearrange("p (c n) -> p c n", c=DC)
        wv_raw = scratch[:, 4096:6144].rearrange("p (c n) -> p c n", c=DC)
        ctxt = scratch[:, 4096:6144].rearrange("p (c b t) -> p c b t", c=DC, b=B)
        small_raw = scratch[:, 6144:6656].rearrange("p (r n) -> p r n", r=2)
        wout_raw = scratch[:, 6656:8704].rearrange("p (j n) -> p j n", j=FC)
        ctx_raw = raw_a[0:NKV, :, :].rearrange("p c n -> p (c n)").rearrange("p (b n) -> p b n", b=B)
        big_raw = raw_f[:, :].rearrange("p (r n) -> p r n", r=2)
        big = [[ht[:, i, 2 * r:2 * r + 2, :].rearrange("p c n -> p (c n)") for i in range(2)] for r in range(2)]
        small = [[xt[0][:, i, r, 0:D] for i in range(2)] for r in range(2)]
        ctx_mean = sb("ctx_mean", [P, DC, B])
        tstats, tmv = sb("tstats", [P, TILES, 6]), sb("tmv", [P, TILES, 2])
        tvar, trstd = sb("tvar", [P, TILES]), sb("trstd", [P, TILES])
        top = scratch[0:PRIMS, 8736:9760]
        lrow, tie, beats = (top[:, P * i:P * i + P].rearrange("p (f n) -> p f n", f=2) for i in range(3))
        lw_wide = top[:, 384:640].rearrange("p (f n) -> p f n", f=2)
        ones64, earlier = top[:, 640:768], top[:, 768:832]
        chosen = top[:, 832:896].rearrange("p (f n) -> p f n", f=2)
        lcol, lmax, lexp, rank, lsum, lw = (sb(n, [PRIMS, 2]) for n in ("lcol", "lmax", "lexp", "rank", "lsum", "lw"))
        places_i, places = sb("places_i", [PRIMS, TOPK], I32), sb("places", [PRIMS, TOPK])
        own_i, own = sb("own_i", [PRIMS, 1], I32), sb("own", [PRIMS, 1])
        index = sb("index", [1, 2 * TOPK], I32)
        wcol = sb("wcol", [P, 2, PAIRS])
        stats = [sb("stats1", [P, TILES, 6]), sb("stats2", [P, TILES, 6])]
        mv = [sb("mv1", [P, TILES, 2]), sb("mv2", [P, TILES, 2])]
        var = [sb("var1", [P, TILES]), sb("var2", [P, TILES])]
        rstd = [sb("rstd1", [P, TILES]), sb("rstd2", [P, TILES])]
        qm = sb("qm", [P, 2, NH, TOK], F32R)
        kt = sb("kt", [P, 2, TOK], F32R)
        qmax = sb("qmax", [P, TILES, NH])
        qsum = sb("qsum", [P, TILES, NH])
        kcum = sb("kcum", [P, 2, 3])
        ctxn = sb("ctxn", [P, 2, 3, P])
        smax = sb("smax", [P, 2, 2, NH])
        psum_r = sb("psum_r", [P, 8])
        aloc = qnt.rearrange("p (t d) -> p t d", t=TILES)
        at = sb("at", [P, 2, DC, TOK], F32R)
        A = ctx.enter_context(nc.psum_tensor("A", [P, 6, 512], F32))
        F = ctx.enter_context(nc.psum_tensor("F", [P, 2, 512], F32))

        x_loaded = [sem(f"x_loaded{p}") for p in range(ITEMS)]
        raw_a_loaded, raw_w1_loaded, raw_w2_loaded = sem("raw_a_loaded"), sem("raw_w1_loaded"), sem("raw_w2_loaded")
        vec_a_loaded, vec_f_loaded, b1_loaded = sem("vec_a_loaded"), sem("vec_f_loaded"), sem("b1_loaded")
        const_step, const_ready, zero_ready = sem("const_step"), sem("const_ready"), sem("zero_ready")
        wa_hi, wa_ready, wo_hi, wo_ready = sem("wa_hi"), sem("wa_ready"), sem("wo_hi"), sem("wo_ready")
        w1_hi, w1_ready, w2_hi, w2_ready = sem("w1_hi"), sem("w1_ready"), sem("w2_hi"), sem("w2_ready")
        ln_stats = [sem("ln1_stats"), sem("ln2_stats")]
        ln_mv = [sem("ln1_mv"), sem("ln2_mv")]
        ln_var = [sem("ln1_var"), sem("ln2_var")]
        ln_rstd = [sem("ln1_rstd"), sem("ln2_rstd")]
        ln_xhat = [sem("ln1_xhat"), sem("ln2_xhat")]
        ln_gain = [sem("ln1_gain"), sem("ln2_gain")]
        ln_ready = [sem("ln1_ready"), sem("ln2_ready")]
        biased = [sem("bo_added"), sem("b2_added")]
        xt_psum = [sem("xt1_psum"), sem("xt2_psum")]
        xt_hi = [sem("xt1_hi"), sem("xt2_hi")]
        xt_lo = [sem("xt1_lo"), sem("xt2_lo")]
        qk_psum, q_hi, k_hi, q_lo, k_lo = sem("qk_psum"), sem("q_hi"), sem("k_hi"), sem("q_lo"), sem("k_lo")
        tok_psum, tok_out = sem("tok_psum"), sem("tok_out")
        qmax_done, qsub_done, qexp_done, kexp_done = sem("qmax_done"), sem("qsub_done"), sem("qexp_done"), sem("kexp_done")
        qsum_done, qrec_done, qn_done, krelu_done, kf_done = (
            sem("qsum_done"), sem("qrec_done"), sem("qn_done"), sem("krelu_done"), sem("kf_done"))
        qnt_psum, qnt_out, ctx_psum, kcum_done, krec_done, ctxn_done, lin_psum, lin_hi, lin_lo = (
            sem("qnt_psum"), sem("qnt_out"), sem("ctx_psum"), sem("kcum_done"), sem("krec_done"),
            sem("ctxn_done"), sem("lin_psum"), sem("lin_hi"), sem("lin_lo"))
        s_psum, smax_done, nmax_done, exp_done = sem("s_psum"), sem("smax_done"), sem("nmax_done"), sem("exp_done")
        pt_psum, pt_out_act, pt_out_dve, pv_psum, prec_done, aloc_done = (
            sem("pt_psum"), sem("pt_out_act"), sem("pt_out_dve"), sem("pv_psum"), sem("prec_done"), sem("aloc_done"))
        al_psum, al_hi, al_lo, wo_psum, res1 = sem("al_psum"), sem("al_hi"), sem("al_lo"), sem("wo_psum"), sem("res1")
        h_psum, gelu_done, h_hi, h_lo, y_psum, res2 = (
            sem("h_psum"), sem("gelu_done"), sem("h_hi"), sem("h_lo"), sem("y_psum"), sem("res2"))
        top_wcol_psum = sem("top_wcol_psum")
        b1_turn = sem("b1_turn")
        stored, b1_psum, b1_ready = sem("stored"), sem("b1_psum"), sem("b1_ready")
        logits_loaded, top_const, top_step, top_exp, top_sum, top_w, top_idx, top_wcol, index_ready = (
            sem(n) for n in ("logits_loaded", "top_const", "top_step", "top_exp", "top_sum", "top_w", "top_idx",
                             "top_wcol", "index_ready"))
        x0_loaded, wv_loaded, wout_loaded, ctx_loaded, bout_loaded = (
            sem(n) for n in ("x0_loaded", "wv_loaded", "wout_loaded", "ctx_loaded", "bout_loaded"))
        big_loaded = [sem("big_loaded0"), sem("big_loaded1")]
        small_loaded = [sem("small_loaded0"), sem("small_loaded1")]
        t_sum, t_stats, t_mv, t_var, t_rstd, t_norm, t_bout = (
            sem(n) for n in ("t_sum", "t_stats", "t_mv", "t_var", "t_rstd", "t_norm", "t_bout"))
        wvt_psum, wvt_out, wvo_psum, wvo_out, ctxt_psum, ctxt_out, ctx_sum, ctxt_ready, cross_psum, cross_added = (
            sem(n) for n in ("wvt_psum", "wvt_out", "wvo_psum", "wvo_out", "ctxt_psum", "ctxt_out", "ctx_sum",
                             "ctxt_ready", "cross_psum", "cross_added"))
        at_psum, big_hi, big_lo, small_hi, small_lo, pair_done, comp_hi, comp_lo = (
            sem(n) for n in ("at_psum", "big_hi", "big_lo", "small_hi", "small_lo", "pair_done", "comp_hi", "comp_lo"))
        f_xt_psum, f_xt_hi, f_xt_lo, f_h_psum, f_gelu, f_h_hi, f_h_lo, f_y_psum, f_res = (
            sem(n) for n in ("f_xt_psum", "f_xt_hi", "f_xt_lo", "f_h_psum", "f_gelu", "f_h_hi", "f_h_lo", "f_y_psum",
                             "f_res"))
        H_LO_0 = 2
        RES2_0 = 4 * ITEMS

        def slot(p):
            return slice(TILES * p, TILES * p + TILES)

        def w1_part(k):
            c, s = k // 2, k % 2

            def dst(i):
                return w1[:, i, c, :].rearrange("q (m p) -> q p m", p=P)[:, 64 * s:64 * s + 64, :]
            return dst, A[:, k, :].rearrange("q (p m) -> q p m", m=FC)

        def w2_part(k):
            def dst(i):
                return w2[:, i, 2 * k:2 * k + 2, :].rearrange("p m n -> p (m n)")
            return dst, A[:, k, :]


        def load_a(sp, l, first=False):
            if not first:
                sp.wait_ge(wo_ready, l)
            for i, (w, lo, hi, at_col) in enumerate((
                    (Wq, 0, P, 0), (Wk, 0, P, P), (Wv, 0, D, 2 * P), (Wq, P, D, 4 * P), (Wk, P, D, 5 * P),
                    (Wo, 0, D, 6 * P))):
                src = w[bass.ds(l, 1)].rearrange("a (c p) n -> p (a c) n", p=P)[:, :, lo:hi]
                sp.dma_start(raw_a[:, :, at_col:at_col + hi - lo], src).then_inc(raw_a_loaded, 16)

        def load_w1(sp, l, first=False):
            if not first:
                sp.wait_ge(w2_ready, l)
            sp.dma_start(raw_f[:, :].rearrange("p (c n) -> p c n", c=DC),
                         W1[bass.ds(l, 1)].rearrange("a (c p) n -> p (a c) n", p=P)).then_inc(raw_w1_loaded, 16)

        def load_w2(sp, l):
            sp.wait_ge(w1_ready, l + 1)
            sp.dma_start(raw_f[:, :].rearrange("p (c n) -> p c n", c=FC),
                         W2[bass.ds(l, 1)].rearrange("a (c p) n -> p (a c) n", p=P)).then_inc(raw_w2_loaded, 16)

        def load_vec(sp, l, which, n=None):
            dst, src, loaded = ((vec_a, (ln1_g, ln1_b, bo), vec_a_loaded), (vec_f, (ln2_g, ln2_b, b2), vec_f_loaded))[which]
            if n is not None:
                sp.wait_ge(biased[which], n + 1)
                sp.wait_ge(ln_ready[which], n + 1)
            for i, s in enumerate(src):
                row = s[bass.ds(l, 1)]
                sp.dma_start(dst[:, i, :], row.broadcast_to([P, D])).then_inc(loaded, 16)

        block = ctx.enter_context(nc.Block())

        @block.sync
        def _(sp):
            sp.dma_start(x[:, slot(0), :], x_in[0:2].rearrange("b (s p) d -> p (b s) d", p=P)).then_inc(x_loaded[0], 16)
            load_vec(sp, 0, 0)
            load_a(sp, 0, first=True)
            for p in range(1, ITEMS):
                sp.dma_start(x[:, slot(p), :],
                             x_in[2 * p:2 * p + 2].rearrange("b (s p) d -> p (b s) d", p=P)).then_inc(x_loaded[p], 16)
            sp.dma_start(b1_rows[:, :], b1.rearrange("l (m p) -> (l m) p", p=P)).then_inc(b1_loaded, 16)
            load_w1(sp, 0, first=True)
            load_vec(sp, 0, 1)
            load_w2(sp, 0)
            for f, lg in enumerate((fc1_logits, fc2_logits)):
                sp.dma_start(lrow[:, f, :], lg.rearrange("(a n) -> a n", a=1).broadcast_to([PRIMS, PRIMS])).then_inc(logits_loaded, 16)
                sp.dma_start(lcol[:, f:f + 1], lg.rearrange("(p o) -> p o", o=1)).then_inc(logits_loaded, 16)
            with sp.Fori(0, DEPTH - 1) as l:
                load_a(sp, l + 1)
                load_w1(sp, l + 1)
                load_vec(sp, l + 1, 0, 4 * l + 3)
                load_vec(sp, l + 1, 1, 4 * l + 3)
                load_w2(sp, l + 1)
            sp.wait_ge(wo_ready, DEPTH)
            sp.dma_start(ctx_raw, ctx_in.rearrange("b t d -> t b d")).then_inc(ctx_loaded, 16)
            sp.wait_ge(biased[0], 4 * DEPTH)
            sp.wait_ge(ln_ready[0], 4 * DEPTH)
            sp.dma_start(vec_a[:, 0, :], bout.rearrange("(a n) -> a n", a=1).broadcast_to([P, D])).then_inc(bout_loaded, 16)
            sp.wait_ge(wo_psum, 16 * DEPTH)
            sp.wait_ge(xt_psum[1], 8 * DEPTH)
            sp.dma_start(x0, x_in.rearrange("b (s p) d -> p (b s) d", p=P)).then_inc(x0_loaded, 16)
            sp.dma_start(wv_raw, Wkv.rearrange("(c p) n -> p c n", p=P)[:, :, 1024:2048]).then_inc(wv_loaded, 16)
            sp.dma_start(wout_raw, Wout.rearrange("(j p) n -> p j n", p=P)).then_inc(wout_loaded, 16)
            sp.wait_ge(w2_ready, DEPTH)
            sp.wait_ge(index_ready, 1)

            def load_pair(f, g, kk, r, peel):
                if not peel:
                    sp.wait_ge(big_lo, g - 1)
                    sp.wait_ge(small_lo, g - 1)
                for j in range(2):
                    k = sp.value_load(index[0:1, bass.ds(f * TOPK + 2 * kk + j, 1)], min_val=0, max_val=PRIMS - 1)
                    rows = slice(RANK * j, RANK * j + RANK)
                    if f == 0:
                        sp.dma_start(small_raw[:, r, :].rearrange("p (c n) -> p c n", c=DC)[:, :, rows],
                                     fc1_A[bass.ds(k, 1)].rearrange("a (c p) r -> p (a c) r", p=P)).then_inc(small_loaded[r], 16)
                        sp.dma_start(big_raw[rows, r, :],
                                     fc1_B[bass.ds(k, 1)].rearrange("a r n -> (a r) n")).then_inc(big_loaded[r], 16)
                    else:
                        sp.dma_start(big_raw[:, r, :].rearrange("p (m n) -> p m n", m=FC)[:, :, rows],
                                     fc2_A[bass.ds(k, 1)].rearrange("a (p m) r -> p (a m) r", p=P)).then_inc(big_loaded[r], 16)
                        sp.dma_start(small_raw[rows, r, :],
                                     fc2_B[bass.ds(k, 1)].rearrange("a r n -> (a r) n")).then_inc(small_loaded[r], 16)

            for r in range(2):
                load_pair(0, r, r, r, True)
            with sp.Fori(1, PAIRS // 2) as i:
                for r in range(2):
                    load_pair(0, 2 * i + r, 2 * i + r, r, False)
            with sp.Fori(0, PAIRS // 2) as i:
                for r in range(2):
                    load_pair(1, PAIRS + 2 * i + r, 2 * i + r, r, False)
            for p in range(ITEMS):
                sp.wait_ge(t_norm, 2 * ITEMS + p + 1)
                sp.dma_start(out[2 * p:2 * p + 2].rearrange("b (s p) d -> p (b s) d", p=P), x[:, slot(p), :]).then_inc(stored, 16)
            sp.wait_ge(stored, 16 * ITEMS)

        def split(pool, dst, src, hi_sem, ready, l):
            one = ones[:, :].broadcast_to([P, 2048]) if len(src.shape) == 2 else ones[:, :].rearrange(
                "p (a o) -> p a o", a=1).broadcast_to(list(src.shape))
            pool.tensor_tensor(dst[0], src, one, ALU.mult).then_inc(hi_sem, 1)
            pool.wait_ge(hi_sem, l + 1)
            pool.tensor_tensor(dst[1], src, dst[0].bitcast(F32), ALU.subtract).then_inc(ready, 1)

        def split_wa(pool, l, n=None):
            pool.wait_ge(raw_a_loaded, 96 * (l + 1))
            if n is not None:
                pool.wait_ge(tok_psum, 4 * n + 4)
            split(pool, [wa[:, i] for i in range(2)], raw_a[:, :, 0:768], wa_hi, wa_ready, l)

        def split_wo(pool, l, n=None):
            pool.wait_ge(raw_a_loaded, 96 * (l + 1))
            if n is not None:
                pool.wait_ge(wo_psum, 4 * n + 4)
            split(pool, [wo[:, i] for i in range(2)], raw_a[:, :, 768:1024], wo_hi, wo_ready, l)

        def split_w1(pool, l, n=None):
            pool.wait_ge(raw_w1_loaded, 16 * (l + 1))
            if n is not None:
                pool.wait_ge(h_psum, FC * n + FC)
            split(pool, [w1[:, i].rearrange("p c n -> p (c n)") for i in range(2)], raw_f[:, :], w1_hi, w1_ready, l)

        def split_w2(pool, l, n=None):
            pool.wait_ge(raw_w2_loaded, 16 * (l + 1))
            if n is not None:
                pool.wait_ge(y_psum, 4 * n + 4)
            split(pool, [w2[:, i].rearrange("p c n -> p (c n)") for i in range(2)], raw_f[:, :], w2_hi, w2_ready, l)

        def pool_ln(pool, i, n, p, l):
            vec, loaded = ((vec_a, vec_a_loaded), (vec_f, vec_f_loaded))[i]
            pool.wait_ge(ln_var[i], n + 1)
            pool.tensor_tensor(rstd[i][:, :], var[i][:, :], minus_half[:, :], ALU.pow).then_inc(ln_rstd[i], 1)
            pool.wait_ge(ln_xhat[i], n + 1)
            pool.wait_ge(loaded, 48 * (l + 1))
            def every(k):
                return vec[:, k:k + 1, :].broadcast_to([P, TILES, D])
            pool.tensor_tensor(xh[i][:, :, :], xh[i][:, :, :], every(0), ALU.mult).then_inc(ln_gain[i], 1)
            pool.wait_ge(ln_gain[i], n + 1)
            pool.tensor_tensor(xh[i][:, :, :], xh[i][:, :, :], every(1), ALU.add).then_inc(ln_ready[i], 1)
            pool.tensor_tensor(x[:, slot(p), :], x[:, slot(p), :], every(2), ALU.add).then_inc(biased[i], 1)

        def pool_h_lo(pool, n, m):
            pool.wait_ge(h_hi, FC * n + m + 1)
            pool.tensor_tensor(ht[:, 1, m, :], hf[:, m % 2, :], ht[:, 0, m, :].bitcast(F32),
                               ALU.subtract).then_inc(h_lo, 1)

        @block.gpsimd
        def _(pool):
            pool.memset(ones[:, :], 1.0).then_inc(const_step, 1)
            pool.memset(minus_half[:, :], -0.5).then_inc(const_step, 1)
            pool.memset(ident[:, :], 0.0).then_inc(const_step, 1)
            pool.memset(ident_bf[:, :], 0.0).then_inc(const_step, 1)
            pool.memset(mask_bf[:, :], 0.0).then_inc(const_step, 1)
            pool.memset(headmask[:, :, :], 1.0).then_inc(const_step, 1)
            pool.memset(v8[:, :, :, :], 1.0).then_inc(const_step, 1)
            for i in range(H_LO_0):
                pool.memset(slot_mark[:, i:i + 1], 0.0).then_inc(h_lo, 1)
            pool.wait_ge(const_step, 7)
            for m in (ident, ident_bf):
                pool.affine_select(out=m[:, :], in_=m[:, :], compare_op=ALU.not_equal, fill=1.0, base=0,
                                   pattern=[[-1, P]], channel_multiplier=1).then_inc(const_step, 1)
            for col in (0, 2 * P):
                m = mask_bf[:, col:col + P]
                pool.affine_select(out=m, in_=m, compare_op=ALU.is_ge, fill=MASKED, base=0,
                                   pattern=[[-1, P]], channel_multiplier=1).then_inc(const_step, 1)
            pool.affine_select(out=headmask[:, :, :], in_=headmask[:, :, :], compare_op=ALU.is_ge, fill=0.0, base=0,
                               pattern=[[-E, NH], [0, E]], channel_multiplier=1).then_inc(const_step, 1)
            pool.wait_ge(const_step, 12)
            pool.affine_select(out=headmask[:, :, :], in_=headmask[:, :, :], compare_op=ALU.is_ge, fill=0.0, base=E - 1,
                               pattern=[[E, NH], [0, E]], channel_multiplier=-1).then_inc(const_ready, 1)
            pool.wait_ge(const_ready, 1)
            pool_ln(pool, 0, 0, 0, 0)
            pool.iota(places_i[:, :], pattern=[[1, TOPK]], base=0, channel_multiplier=0).then_inc(top_const, 1)
            pool.iota(own_i[:, :], pattern=[[0, 1]], base=0, channel_multiplier=1).then_inc(top_const, 1)
            pool.memset(ones64[:, :], 1.0).then_inc(top_const, 1)
            pool.memset(earlier[:, :], 1.0).then_inc(top_const, 1)
            pool.wait_ge(top_const, 4)
            pool.affine_select(out=earlier[:, :], in_=earlier[:, :], compare_op=ALU.is_gt, fill=0.0, base=0,
                               pattern=[[-1, PRIMS]], channel_multiplier=1).then_inc(top_const, 1)
            split_wa(pool, 0)
            split_wo(pool, 0)
            split_w1(pool, 0)
            split_w2(pool, 0)
            pool_ln(pool, 0, 1, 1, 0)
            pool_ln(pool, 1, 0, 0, 0)

            def step(l, p, last):
                n = 4 * l + p + 1
                attn = not (last and p == ITEMS - 1)
                la = l + 1 if p == ITEMS - 1 else l
                for m in range(FC):
                    pool_h_lo(pool, n - 1, m)
                    if m == 1 and p == ITEMS - 2 and not last:
                        split_wa(pool, l + 1, n)
                if p == ITEMS - 1 and not last:
                    split_wo(pool, l + 1, n - 1)
                    split_w1(pool, l + 1, n - 1)
                if not (last and p >= ITEMS - 2):
                    pool_ln(pool, 0, n + 1, (p + 2) % ITEMS, l + 1 if p >= ITEMS - 2 else l)
                if attn:
                    pool_ln(pool, 1, n, (p + 1) % ITEMS, la)
                if p == ITEMS - 1 and not last:
                    split_w2(pool, l + 1, n - 1)

            with pool.Fori(0, DEPTH - 1) as l:
                for p in range(ITEMS):
                    step(l, p, False)
            for p in range(ITEMS):
                step(DEPTH - 1, p, True)

            def inverse_std(q):
                pool.wait_ge(t_var, q + 1)
                pool.tensor_tensor(trstd[:, :], tvar[:, :], minus_half[:, :], ALU.pow).then_inc(t_rstd, 1)

            pool.wait_ge(bout_loaded, 16)
            for p in range(ITEMS):
                inverse_std(p)
                pool.wait_ge(t_norm, p + 1)
                pool.tensor_tensor(x[:, slot(p), :], x[:, slot(p), :],
                                   vec_a[:, 0:1, :].broadcast_to([P, TILES, D]), ALU.add).then_inc(t_bout, 1)
            for p in range(ITEMS):
                inverse_std(ITEMS + p)
            for p in range(ITEMS):
                for m in range(FC):
                    pool.wait_ge(f_h_hi, FC * p + m + 1)
                    pool.tensor_tensor(ht[:, 1, m, :], hf[:, m % 2, :], ht[:, 0, m, :].bitcast(F32),
                                       ALU.subtract).then_inc(f_h_lo, 1)
                inverse_std(2 * ITEMS + p)

        def ln(dve, i, n, p):
            for t in range(TILES):
                last = dve.bn_stats(stats[i][:, t, :], x[:, TILES * p + t, :])
            last.then_inc(ln_stats[i], 1)
            dve.wait_ge(ln_stats[i], n + 1)
            dve.memset(carrier[:, 0:1], 0.0)
            for t in range(TILES):
                last = dve.bn_aggr(mv[i][:, t, :], stats[i][:, t, :])
            last.then_inc(ln_mv[i], 1)
            dve.wait_ge(ln_mv[i], n + 1)
            dve.tensor_scalar(var[i][:, :], mv[i][:, :, 1], EPS, None, ALU.add).then_inc(ln_var[i], 1)
            dve.wait_ge(ln_rstd[i], n + 1)
            for t in range(TILES):
                last = dve.tensor_scalar(xh[i][:, t, :], x[:, TILES * p + t, :], mv[i][:, t, 0:1],
                                         rstd[i][:, t:t + 1], ALU.subtract, ALU.mult)
            last.then_inc(ln_xhat[i], 1)

        def lo(dve, dst, src, hi):
            return dve.tensor_tensor(dst, src, hi.bitcast(F32), ALU.subtract)

        def dve_xt_lo(dve, i, n):
            for c in range(DC):
                dve.wait_ge(xt_hi[i], 2 * n + c + 1)
                lo(dve, xt[i][:, 1, c, :], A[:, (0, 2)[i] + c, :], xt[i][:, 0, c, :]).then_inc(xt_lo[i], 1)

        def dve_qk_lo(dve, n):
            dve.wait_ge(q_hi, n + 1)
            for h in range(NH):
                r = slice(E * h, E * h + E)
                last = lo(dve, qm[r, 1, h, :], A[r, 2, :], qm[r, 0, h, :])
            last.then_inc(q_lo, 1)
            dve.wait_ge(k_hi, n + 1)
            lo(dve, kt[:, 1, :], A[:, 3, :], kt[:, 0, :]).then_inc(k_lo, 1)

        def heads(ap):
            return ap.rearrange("p t (h e) -> p t h e", h=NH)

        def over_e(ap):
            return ap.rearrange("p t (h o) -> p t h o", o=1).broadcast_to([P, TILES, NH, E])

        def dve_features(dve, n):
            dve.wait_ge(tok_out, 4 * n + 4)
            q = qk[:, :, 0:P]
            dve.tensor_reduce(qmax[:, :, :], heads(q), AX_X, ALU.max).then_inc(qmax_done, 1)
            dve.wait_ge(qmax_done, n + 1)
            dve.tensor_tensor(heads(qexp[:, :, :]), heads(q), over_e(qmax[:, :, :]), ALU.subtract).then_inc(qsub_done, 1)

        def dve_features2(dve, n):
            k = qk[:, :, P:2 * P]
            dve.wait_ge(kexp_done, n + 1)
            dve.tensor_scalar(k, k, 0.0, None, ALU.max).then_inc(krelu_done, 1)
            dve.wait_ge(krelu_done, n + 1)
            dve.scalar_tensor_tensor(out=kexp[:, :, :], in0=kexp[:, :, :], scalar=1.0, in1=k,
                                     op0=ALU.min, op1=ALU.add).then_inc(kf_done, 1)
            dve.wait_ge(qexp_done, n + 1)
            dve.tensor_reduce(qsum[:, :, :], heads(qexp[:, :, :]), AX_X, ALU.add).then_inc(qsum_done, 1)
            dve.wait_ge(qsum_done, n + 1)
            dve.reciprocal(qsum[:, :, :], qsum[:, :, :]).then_inc(qrec_done, 1)
            dve.wait_ge(qrec_done, n + 1)
            dve.tensor_tensor(heads(qexp[:, :, :]), heads(qexp[:, :, :]), over_e(qsum[:, :, :]),
                              ALU.mult).then_inc(qn_done, 1)

        def dve_ctx(dve, n, b):
            dve.wait_ge(ctx_psum, 2 * n + b + 1)
            ps = A[:, 1 - b, 0:3 * NH * HB].rearrange("p (j h e) -> p j h e", j=3, h=NH)
            dve.tensor_scalar(kcum[:, b, :], ps[:, :, 0, E], 1e-6, None, ALU.add).then_inc(kcum_done, 1)
            dve.wait_ge(kcum_done, 2 * n + b + 1)
            dve.reciprocal(kcum[:, b, :], kcum[:, b, :]).then_inc(krec_done, 1)
            dve.wait_ge(krec_done, 2 * n + b + 1)
            for j in range(3):
                last = dve.scalar_tensor_tensor(
                    out=ctxn[:, b, j, :].rearrange("p (h e) -> p h e", h=NH), in0=ps[:, j, :, 0:E],
                    scalar=kcum[:, b, j:j + 1], in1=headmask[:, :, :], op0=ALU.mult, op1=ALU.mult)
            last.then_inc(ctxn_done, 1)

        def later_buckets(ap):
            return ap.rearrange("p (b t) -> p b t", b=2)[:, :, BUCKET:T]

        def dve_lin_lo(dve, n):
            dve.wait_ge(lin_hi, n + 1)
            lo(dve, later_buckets(at[:, 1, 1, :]), later_buckets(A[:, 1, :]),
               later_buckets(at[:, 0, 1, :])).then_inc(lin_lo, 1)

        def dve_max(dve, n, b):
            dve.wait_ge(s_psum, 2 * n + b + 1)
            dve.tensor_reduce(smax[:, b, 0, :], A[:, 2:6, 0:P], AX_X, ALU.max)
            dve.tensor_reduce(smax[:, b, 1, :], A[:, 2:6, P:3 * P], AX_X, ALU.max).then_inc(smax_done, 1)
            dve.wait_ge(smax_done, 2 * n + b + 1)
            dve.tensor_scalar(smax[:, b, :, :], smax[:, b, :, :], -SCALE, None, ALU.mult).then_inc(nmax_done, 1)

        def dve_pt(dve, n, b):
            for r in (1, 2):
                dve.wait_ge(pt_psum, 6 * n + 3 * b + r + 1)
                dve.tensor_copy(pt[:, r, :], A[:, r % 2, :]).then_inc(pt_out_dve, 1)

        def dve_aloc(dve, n, b):
            dve.wait_ge(pv_psum, 2 * n + b + 1)
            ps = A[:, 1, 0:8 * HB].rearrange("p (w e) -> p w e", w=8)
            dve.reciprocal(psum_r[:, :], ps[:, :, E]).then_inc(prec_done, 1)
            dve.wait_ge(prec_done, 2 * n + b + 1)
            dve.tensor_tensor(aloc[:, 2 * b:2 * b + 2, :].rearrange("p t (h e) -> p (t h) e", h=NH), ps[:, :, 0:E],
                              psum_r[:, :].rearrange("p (w o) -> p w o", o=1).broadcast_to([P, 8, E]),
                              ALU.mult).then_inc(aloc_done, 1)

        def dve_al_lo(dve, n):
            dve.wait_ge(al_hi, n + 1)
            lo(dve, at[:, 1, 0, :], A[:, 0, :], at[:, 0, 0, :]).then_inc(al_lo, 1)

        def dve_res1(dve, n, p):
            dve.wait_ge(biased[0], n + 1)
            for t in range(TILES):
                dve.wait_ge(wo_psum, 4 * n + t + 1)
                xs = x[:, TILES * p + t, :]
                dve.tensor_tensor(xs, A[:, 2 + t, 0:D], xs, ALU.add).then_inc(res1, 1)
            dve.wait_ge(res1, 4 * n + 4)

        def dve_h_hi(dve, n, m):
            dve.wait_ge(gelu_done, FC * n + m + 1)
            dve.tensor_copy(ht[:, 0, m, :], hf[:, m % 2, :]).then_inc(h_hi, 1)

        def dve_res2(dve, n, p, t):
            if t == 0:
                dve.wait_ge(biased[1], n + 1)
            dve.wait_ge(y_psum, 4 * n + t + 1)
            xs = x[:, TILES * p + t, :]
            dve.tensor_tensor(xs, F[:, t % 2, 0:D], xs, ALU.add).then_inc(res2, 1)

        @block.vector
        def _(dve):
            dve.memset(qm[:, :, :, :].bitcast(F32), 0.0)
            for i in range(2):
                last = dve.memset(at[:, i, 1, :].bitcast(F32), 0.0)
            last.then_inc(zero_ready, 1)
            dve.wait_ge(x_loaded[0], 16)
            ln(dve, 0, 0, 0)
            for p in range(ITEMS):
                dve.wait_ge(x_loaded[p], 16)
                for t in range(TILES):
                    dve.memset(loaded_mark[:, TILES * p + t:TILES * p + t + 1], 0.0).then_inc(res2, 1)

            def attn_only():
                dve_xt_lo(dve, 0, 0)
                dve_qk_lo(dve, 0)
                dve_features(dve, 0)
                dve_max(dve, 0, 0)
                dve_features2(dve, 0)
                for b in range(2):
                    dve_ctx(dve, 0, b)
                dve_lin_lo(dve, 0)
                dve_pt(dve, 0, 0)
                dve_max(dve, 0, 1)
                dve_aloc(dve, 0, 0)
                dve_pt(dve, 0, 1)
                dve_aloc(dve, 0, 1)
                dve_al_lo(dve, 0)
                dve_wait_x(1)
                ln(dve, 0, 1, 1)
                dve_res1(dve, 0, 0)
                ln(dve, 1, 0, 0)

            def dve_wait_x(n):
                dve.wait_ge(res2, 4 * n + 4)

            def step(l, p, last):
                n = 4 * l + p + 1
                pa = (p + 1) % ITEMS
                attn = not (last and p == ITEMS - 1)
                nxt = not (last and p >= ITEMS - 2)
                if attn:
                    dve_xt_lo(dve, 0, n)
                    dve_qk_lo(dve, n)
                    dve_features(dve, n)
                dve_xt_lo(dve, 1, n - 1)
                dve_h_hi(dve, n - 1, 0)
                if attn:
                    dve_max(dve, n, 0)
                dve_h_hi(dve, n - 1, 1)
                if attn:
                    dve_features2(dve, n)
                dve_h_hi(dve, n - 1, 2)
                dve_h_hi(dve, n - 1, 3)
                if attn:
                    dve_ctx(dve, n, 0)
                    dve_ctx(dve, n, 1)
                dve_h_hi(dve, n - 1, 4)
                if attn:
                    dve_lin_lo(dve, n)
                    dve_pt(dve, n, 0)
                    dve_max(dve, n, 1)
                dve_h_hi(dve, n - 1, 5)
                if attn:
                    dve_aloc(dve, n, 0)
                dve_h_hi(dve, n - 1, 6)
                dve_h_hi(dve, n - 1, 7)
                if attn:
                    dve_pt(dve, n, 1)
                dve_res2(dve, n - 1, p, 0)
                if attn:
                    dve_aloc(dve, n, 1)
                dve_res2(dve, n - 1, p, 1)
                if attn:
                    dve_al_lo(dve, n)
                if nxt:
                    dve_wait_x(n + 1)
                    ln(dve, 0, n + 1, (pa + 1) % ITEMS)
                dve_res2(dve, n - 1, p, 2)
                if attn:
                    dve_res1(dve, n, pa)
                    ln(dve, 1, n, pa)
                dve_res2(dve, n - 1, p, 3)

            def top_k():
                dve.wait_ge(logits_loaded, 64)
                dve.wait_ge(top_const, 5)
                dve.tensor_copy(places[:, :], places_i[:, :])
                dve.tensor_copy(own[:, :], own_i[:, :])
                for f in range(2):
                    dve.scalar_tensor_tensor(out=tie[:, f, :], in0=lrow[:, f, :], scalar=lcol[:, f:f + 1],
                                             in1=earlier[:, :], op0=ALU.is_equal, op1=ALU.mult)
                dve.tensor_reduce(lmax[:, :], lrow[:, :, :], AX_X, ALU.max).then_inc(top_step, 1)
                dve.wait_ge(top_step, 1)
                dve.tensor_scalar(lmax[:, :], lmax[:, :], -1.0, None, ALU.mult).then_inc(top_step, 1)
                for f in range(2):
                    last = dve.scalar_tensor_tensor(out=beats[:, f, :], in0=lrow[:, f, :], scalar=lcol[:, f:f + 1],
                                                    in1=tie[:, f, :], op0=ALU.is_gt, op1=ALU.add)
                last.then_inc(top_step, 1)
                dve.wait_ge(top_step, 3)
                dve.tensor_reduce(rank[:, :], beats[:, :, :], AX_X, ALU.add).then_inc(top_step, 1)
                dve.wait_ge(top_step, 4)
                dve.wait_ge(top_exp, 1)
                dve.scalar_tensor_tensor(out=lexp[:, :], in0=rank[:, :], scalar=TOPK - 0.5, in1=lexp[:, :],
                                         op0=ALU.is_lt, op1=ALU.mult).then_inc(top_step, 1)
                for f in range(2):
                    last = dve.tensor_scalar(chosen[:, f, :], places[:, :], rank[:, f:f + 1], None, ALU.is_equal)
                last.then_inc(top_step, 1)
                dve.wait_ge(top_sum, 1)
                dve.reciprocal(lsum[:, :], F[0:PRIMS, 1, 0:2]).then_inc(top_step, 1)
                dve.wait_ge(top_step, 7)
                dve.tensor_tensor(lw[:, :], lexp[:, :], lsum[:, :], ALU.mult).then_inc(top_step, 1)
                dve.wait_ge(top_step, 8)
                for f in range(2):
                    last = dve.tensor_scalar(lw_wide[:, f, :], ones64[:, :], lw[:, f:f + 1], None, ALU.mult)
                last.then_inc(top_w, 1)
                dve.wait_ge(top_idx, 1)
                dve.tensor_copy(index[:, :], F[0:1, 1, 64:64 + 2 * TOPK]).then_inc(index_ready, 1)
                dve.wait_ge(top_wcol_psum, 1)
                for j in range(2):
                    rows = slice(RANK * j, RANK * j + RANK)
                    last = dve.tensor_copy(wcol[rows, :, :], F[rows, 1, 128 + 32 * j:160 + 32 * j].rearrange(
                        "p (f k) -> p f k", f=2))
                last.then_inc(top_wcol, 1)

            top_k()
            attn_only()
            with dve.Fori(0, DEPTH - 1) as l:
                for p in range(ITEMS):
                    step(l, p, False)
            for p in range(ITEMS):
                step(DEPTH - 1, p, True)

            def norm(q, p):
                for t in range(TILES):
                    last = dve.bn_stats(tstats[:, t, :], x[:, TILES * p + t, :])
                last.then_inc(t_stats, 1)
                dve.wait_ge(t_stats, q + 1)
                for t in range(TILES):
                    last = dve.bn_aggr(tmv[:, t, :], tstats[:, t, :])
                last.then_inc(t_mv, 1)
                dve.wait_ge(t_mv, q + 1)
                dve.tensor_scalar(tvar[:, :], tmv[:, :, 1], EPS, None, ALU.add).then_inc(t_var, 1)
                dve.wait_ge(t_rstd, q + 1)
                for t in range(TILES):
                    xs = x[:, TILES * p + t, :]
                    last = dve.tensor_scalar(xs, xs, tmv[:, t, 0:1], trstd[:, t:t + 1], ALU.subtract, ALU.mult)
                last.then_inc(t_norm, 1)

            dve.wait_ge(x0_loaded, 16)
            dve.wait_ge(res2, RES2_0 + 16 * DEPTH)
            for p in range(ITEMS):
                dve.tensor_tensor(x[:, slot(p), :], x[:, slot(p), :], x0[:, slot(p), :], ALU.add).then_inc(t_sum, 1)
                dve.wait_ge(t_sum, p + 1)
                norm(p, p)
            for c in range(DC):
                for s in range(2):
                    dve.wait_ge(ctxt_psum, 2 * c + s + 1)
                    if c == 0 and s == 0:
                        dve.wait_ge(wvt_psum, 4)
                    dve.tensor_copy(ctxt[:, c, 4 * s:4 * s + 4, 0:NKV],
                                    A[:, 2 * c + s, :].rearrange("p (b t) -> p b t", b=4)[:, :, 0:NKV]).then_inc(ctxt_out, 1)
            dve.wait_ge(ctxt_out, 4)
            dve.tensor_reduce(ctx_mean[:, :, :], ctxt[:, :, :, 0:NKV], AX_X, ALU.add).then_inc(ctx_sum, 1)
            dve.wait_ge(ctx_sum, 1)
            for c in range(DC):
                last = dve.tensor_scalar(ctxt[:, c, :, NKV:CB],
                                         ctx_mean[:, c, :].rearrange("p (b o) -> p b o", o=1).broadcast_to([P, B, CB - NKV]),
                                         1.0 / NKV, None, ALU.mult)
            last.then_inc(ctxt_ready, 1)

            def pair_lo(f, g, kk, r, use):
                w = wcol[:, f, bass.ds(kk, 1)]
                dve.wait_ge(big_hi, g + 1)
                dve.wait_ge(small_hi, g + 1)
                dve.wait_ge(big_loaded[r], 32 * use)
                dve.wait_ge(small_loaded[r], 32 * use)
                if f == 0:
                    dve.scalar_tensor_tensor(out=big[r][1], in0=big_raw[:, r, :], scalar=w, in1=big[r][0].bitcast(F32),
                                             op0=ALU.mult, op1=ALU.subtract).then_inc(big_lo, 1)
                    lo(dve, small[r][1], A[:, 4 + r, 0:D], small[r][0]).then_inc(small_lo, 1)
                else:
                    bank = (F[:, :, :], A[:, 4:6, :])[r].rearrange("p s n -> p (s n)")
                    for s in range(2):
                        half = slice(512 * s, 512 * s + 512)
                        last = lo(dve, big[r][1][:, half], bank[:, half], big[r][0][:, half])
                    last.then_inc(big_lo, 1)
                    dve.scalar_tensor_tensor(out=small[r][1], in0=small_raw[:, r, :], scalar=w,
                                             in1=small[r][0].bitcast(F32), op0=ALU.mult, op1=ALU.subtract).then_inc(small_lo, 1)

            def composed(dst, src, k):
                dve.wait_ge(comp_hi, k + 1)
                lo(dve, dst(1), src, dst(0)).then_inc(comp_lo, 1)

            dve.wait_ge(top_wcol, 1)
            for f in range(2):
                with dve.Fori(0, PAIRS // 2) as i:
                    for r in range(2):
                        pair_lo(f, PAIRS * f + 2 * i + r, 2 * i + r, r, PAIRS // 2 * f + i + 1)
                if f == 0:
                    for k in range(4):
                        composed(*w1_part(k), k)
                    for p in range(ITEMS):
                        dve.wait_ge(t_bout, p + 1)
                        for t in range(TILES):
                            xs = x[:, TILES * p + t, :]
                            dve.wait_ge(cross_psum, TILES * p + t + 1)
                            dve.tensor_tensor(xs, A[:, t, 0:D], xs, ALU.add).then_inc(cross_added, 1)
                        dve.wait_ge(cross_added, TILES * p + TILES)
                        norm(ITEMS + p, p)
                else:
                    for k in range(4):
                        composed(*w2_part(k), 4 + k)
            for p in range(ITEMS):
                for c in range(DC):
                    dve.wait_ge(f_xt_hi, 2 * p + c + 1)
                    lo(dve, xt[1][:, 1, c, :], A[:, c, :], xt[1][:, 0, c, :]).then_inc(f_xt_lo, 1)
                for m in range(FC):
                    dve.wait_ge(f_gelu, FC * p + m + 1)
                    dve.tensor_copy(ht[:, 0, m, :], hf[:, m % 2, :]).then_inc(f_h_hi, 1)
                if p + 1 < ITEMS:
                    pass
                for t in range(TILES):
                    xs = x[:, TILES * p + t, :]
                    dve.wait_ge(f_y_psum, TILES * p + t + 1)
                    dve.tensor_tensor(xs, A[:, 2 + t, 0:D], xs, ALU.add).then_inc(f_res, 1)
                dve.wait_ge(f_res, TILES * p + TILES)
                norm(2 * ITEMS + p, p)

        def act_xt_hi(act, i, n):
            for c in range(DC):
                act.wait_ge(xt_psum[i], 2 * n + c + 1)
                act.activation(xt[i][:, 0, c, :], A[:, (0, 2)[i] + c, :], ACT.Copy).then_inc(xt_hi[i], 1)

        def act_qk_hi(act, n):
            act.wait_ge(qk_psum, 2 * n + 1)
            for h in range(NH):
                r = slice(E * h, E * h + E)
                last = act.activation(qm[r, 0, h, :], A[r, 2, :], ACT.Copy)
            last.then_inc(q_hi, 1)
            act.wait_ge(qk_psum, 2 * n + 2)
            act.activation(kt[:, 0, :], A[:, 3, :], ACT.Copy).then_inc(k_hi, 1)

        def act_tok(act, n, t):
            act.wait_ge(tok_psum, 4 * n + t + 1)
            ps = A[:, (4, 5, 0, 1)[t], :]
            act.activation(v8[:, t, :, 0:E], ps[:, 0:2 * P].rearrange("p (h e) -> p h e", e=E), ACT.Copy)
            act.activation(qk[:, t, :], ps[:, 2 * P:4 * P], ACT.Copy).then_inc(tok_out, 1)

        def act_features(act, n):
            act.wait_ge(tok_out, 4 * n + 4)
            act.activation(kexp[:, :, :], qk[:, :, P:2 * P], ACT.Exp).then_inc(kexp_done, 1)
            act.wait_ge(qsub_done, n + 1)
            act.activation(qexp[:, :, :], qexp[:, :, :], ACT.Exp).then_inc(qexp_done, 1)

        def act_qnt(act, n):
            act.wait_ge(qnt_psum, n + 1)
            act.activation(qnt[:, :], A[:, 0, :], ACT.Copy).then_inc(qnt_out, 1)

        def act_lin_hi(act, n):
            act.wait_ge(lin_psum, n + 1)
            act.activation(later_buckets(at[:, 0, 1, :]), later_buckets(A[:, 1, :]), ACT.Copy).then_inc(lin_hi, 1)

        def act_exp(act, n, b):
            act.wait_ge(nmax_done, 2 * n + b + 1)
            for h in range(NH):
                for w, (a, z) in enumerate(((0, P), (P, 3 * P))):
                    last = act.activation(prob[:, h, a:z], A[:, 2 + h, a:z], ACT.Exp, bias=smax[:, b, w, h:h + 1],
                                          scale=SCALE)
            last.then_inc(exp_done, 1)

        def act_pt(act, n, b):
            act.wait_ge(pt_psum, 6 * n + 3 * b + 1)
            act.activation(pt[:, 0, :], A[:, 0, :], ACT.Copy).then_inc(pt_out_act, 1)

        def act_al_hi(act, n):
            act.wait_ge(al_psum, n + 1)
            act.activation(at[:, 0, 0, :], A[:, 0, :], ACT.Copy).then_inc(al_hi, 1)

        def act_b1(act, l):
            act.activation(b1_now[:, :], b1c[:, bass.ds(l * FC, FC)], ACT.Copy).then_inc(b1_turn, 1)
            act.wait_ge(b1_turn, l + 1)

        def act_gelu(act, n, m, l):
            act.wait_ge(h_psum, FC * n + m + 1)
            act.wait_ge(h_lo, FC * n + m + 1)
            act.activation(hf[:, m % 2, :], F[:, m % 2, :], ACT.Gelu,
                           bias=b1_now[:, m:m + 1]).then_inc(gelu_done, 1)

        @block.scalar
        def _(act):
            act.wait_ge(const_ready, 1)
            act.wait_ge(zero_ready, 1)
            act.wait_ge(top_step, 2)
            for f in range(2):
                last = act.activation(lexp[:, f:f + 1], lcol[:, f:f + 1], ACT.Exp, bias=lmax[:, f:f + 1])
            last.then_inc(top_exp, 1)
            act_xt_hi(act, 0, 0)
            act_qk_hi(act, 0)
            for t in range(TILES):
                act_tok(act, 0, t)
            act_features(act, 0)
            act_exp(act, 0, 0)
            act_qnt(act, 0)
            act_lin_hi(act, 0)
            act_pt(act, 0, 0)
            act_exp(act, 0, 1)
            act_pt(act, 0, 1)
            act_al_hi(act, 0)
            act.wait_ge(b1_psum, 1)
            act.activation(b1c[:, :], F[:, 0, 0:DEPTH * FC], ACT.Copy).then_inc(b1_ready, 1)
            act.wait_ge(b1_ready, 1)
            act.wait_ge(top_wcol, 1)

            def step(l, p, last):
                n = 4 * l + p + 1
                attn = not (last and p == ITEMS - 1)
                if attn:
                    act_xt_hi(act, 0, n)
                    act_qk_hi(act, n)
                    for t in range(TILES):
                        act_tok(act, n, t)
                    act_features(act, n)
                act_xt_hi(act, 1, n - 1)
                act_gelu(act, n - 1, 0, l)
                if attn:
                    act_exp(act, n, 0)
                act_gelu(act, n - 1, 1, l)
                act_gelu(act, n - 1, 2, l)
                if attn:
                    act_qnt(act, n)
                act_gelu(act, n - 1, 3, l)
                if attn:
                    act_lin_hi(act, n)
                act_gelu(act, n - 1, 4, l)
                if attn:
                    act_pt(act, n, 0)
                    act_exp(act, n, 1)
                act_gelu(act, n - 1, 5, l)
                act_gelu(act, n - 1, 6, l)
                act_gelu(act, n - 1, 7, l)
                if attn:
                    act_pt(act, n, 1)
                    act_al_hi(act, n)

            with act.Fori(0, DEPTH - 1) as l:
                act_b1(act, l)
                for p in range(ITEMS):
                    step(l, p, False)
            act_b1(act, DEPTH - 1)
            for p in range(ITEMS):
                step(DEPTH - 1, p, True)

            for k in range(4):
                act.wait_ge(wvt_psum, k + 1)
                act.wait_ge(t_sum, ITEMS)
                act.activation(wvt[:, 2 * k:2 * k + 2, :].rearrange("p j i -> p (j i)"), A[:, k, :], ACT.Copy).then_inc(wvt_out, 1)
            for c in range(DC):
                act.wait_ge(wvo_psum, c + 1)
                act.activation(wvo[:, c, :], A[:, 4 + c, 0:D], ACT.Copy).then_inc(wvo_out, 1)

            def pair_hi(f, g, kk, r, use, peel):
                w = wcol[:, f, bass.ds(kk, 1)]
                act.wait_ge(big_loaded[r], 32 * use)
                act.wait_ge(small_loaded[r], 32 * use)
                if not peel:
                    act.wait_ge(pair_done, g - 1)
                if not peel:
                    act.activation(carrier[:, 1 + r:2 + r], ones[:, :], ACT.Copy)
                if f == 0:
                    act.activation(big[r][0], big_raw[:, r, :], ACT.Copy, scale=w).then_inc(big_hi, 1)
                    act.wait_ge(at_psum, g + 1)
                    act.activation(small[r][0], A[:, 4 + r, 0:D], ACT.Copy).then_inc(small_hi, 1)
                else:
                    act.activation(small[r][0], small_raw[:, r, :], ACT.Copy, scale=w).then_inc(small_hi, 1)
                    act.wait_ge(at_psum, g + 1)
                    for s in range(2):
                        last = act.activation(big[r][0][:, 512 * s:512 * s + 512], (F, A)[r][:, 4 * r + s, :], ACT.Copy)
                    last.then_inc(big_hi, 1)

            act.wait_ge(top_wcol, 1)
            act.wait_ge(y_psum, 16 * DEPTH)
            for r in range(2):
                pair_hi(0, r, r, r, 1, True)
            with act.Fori(1, PAIRS // 2) as i:
                for r in range(2):
                    pair_hi(0, 2 * i + r, 2 * i + r, r, i + 1, False)
            act.wait_ge(pair_done, PAIRS)
            for k in range(4):
                dst, src = w1_part(k)
                act.activation(dst(0), src, ACT.Copy).then_inc(comp_hi, 1)
            with act.Fori(0, PAIRS // 2) as i:
                for r in range(2):
                    pair_hi(1, PAIRS + 2 * i + r, 2 * i + r, r, PAIRS // 2 + i + 1, False)
            act.wait_ge(pair_done, 2 * PAIRS)
            for k in range(4):
                dst, src = w2_part(k)
                act.activation(dst(0), src, ACT.Copy).then_inc(comp_hi, 1)
            for p in range(ITEMS):
                for c in range(DC):
                    act.wait_ge(f_xt_psum, 2 * p + c + 1)
                    act.activation(xt[1][:, 0, c, :], A[:, c, :], ACT.Copy).then_inc(f_xt_hi, 1)
                for m in range(FC):
                    act.wait_ge(f_h_psum, FC * p + m + 1)
                    if FC * p + m >= 2:
                        act.wait_ge(f_h_lo, FC * p + m - 1)
                    act.activation(hf[:, m % 2, :], F[:, m % 2, :], ACT.Gelu_apprx_tanh).then_inc(f_gelu, 1)

        def pe_xt(pe, i, n):
            pe.wait_ge(ln_ready[i], n + 1)
            for c in range(DC):
                for t in range(TILES):
                    last = pe.transpose(A[:, (0, 2)[i] + c, P * t:P * t + P], xh[i][:, t, P * c:P * c + P], ident[:, :])
                last.then_inc(xt_psum[i], 1)

        def product(pe, out, lhs, rhs):
            total = [(c, a, b) for c in range(DC) for a, b in PASSES]
            for k, (c, a, b) in enumerate(total):
                last = pe.matmul(out, lhs(a, c), rhs(b, c), start=k == 0, stop=k == len(total) - 1)
            return last

        def pe_qk(pe, n, l):
            pe.wait_ge(xt_lo[0], 2 * n + 2)
            pe.wait_ge(wa_ready, l + 1)
            for i in range(2):
                product(pe, A[:, 2 + i, :], lambda a, c: wa[:, a, c, P * i:P * i + P],
                        lambda b, c: xt[0][:, b, c, :]).then_inc(qk_psum, 1)

        def pe_tok(pe, n, t):
            product(pe, A[:, (4, 5, 0, 1)[t], :], lambda a, c: xt[0][:, a, c, P * t:P * t + P],
                    lambda b, c: wa[:, b, c, 2 * P:6 * P]).then_inc(tok_psum, 1)

        def pe_s(pe, n, b):
            pe.wait_ge(k_lo, n + 1)
            if b == 0:
                pe.wait_ge(tok_out, 4 * n + 2)
            else:
                pe.wait_ge(exp_done, 2 * n + 1)
            for h in range(NH):
                pe.matmul(A[:, 2 + h, 0:3 * P], ident_bf[:, :], mask_bf[:, :], start=True, stop=False)
                for w, (c0, c1, t, k1) in enumerate(((0, P, 2 * b, 1), (P, 3 * P, 2 * b + 1, 2))):
                    for k, (i, j) in enumerate(PASSES):
                        last = pe.matmul(A[:, 2 + h, c0:c1], qm[:, i, h, P * t:P * t + P],
                                         kt[:, j, 2 * b * P:(2 * b + k1) * P], start=False, stop=w == 1 and k == 2)
            last.then_inc(s_psum, 1)

        def pe_qnt(pe, n):
            pe.wait_ge(qn_done, n + 1)
            for t in range(TILES):
                last = pe.transpose(A[:, 0, P * t:P * t + P], qexp[:, t, :], ident[:, :])
            last.then_inc(qnt_psum, 1)

        def pe_ctx(pe, n, b):
            pe.wait_ge(kf_done, n + 1)
            if b == 1:
                pe.wait_ge(qnt_out, n + 1)
            w = NH * HB

            def part(j, t, rows, start, stop):
                return pe.matmul(A[:, 1 - b, j * w:(j + 1) * w], kexp[0:rows, t, :],
                                 v8[0:rows, t, NH:2 * NH, :].rearrange("p h e -> p (h e)"), start=start, stop=stop)
            part(0, 2 * b, BUCKET, True, True)
            part(1, 2 * b, P, True, True)
            part(2, 2 * b, P, True, False)
            part(2, 2 * b + 1, BUCKET, False, True).then_inc(ctx_psum, 1)

        def pe_lin(pe, n):
            pe.wait_ge(ctxn_done, 2 * n + 2)
            pe.wait_ge(qnt_out, n + 1)
            for b in range(2):
                for u in range(1, 4):
                    cols = slice(b * T + u * BUCKET, b * T + (u + 1) * BUCKET)
                    last = pe.matmul(A[:, 1, cols], ctxn[:, b, u - 1, :], qnt[:, cols], start=True, stop=True)
            last.then_inc(lin_psum, 1)

        def pe_pt(pe, n, b):
            pe.wait_ge(exp_done, 2 * n + b + 1)
            for r in range(3):
                if r == 0:
                    if b == 0:
                        pe.wait_ge(ctxn_done, 2 * n + 2)
                    else:
                        pe.wait_ge(pt_out_dve, 4 * n + 2)
                if r == 1:
                    if b == 0:
                        pe.wait_ge(lin_lo, n + 1)
                    else:
                        pe.wait_ge(aloc_done, 2 * n + 1)
                if r == 2:
                    pe.wait_ge(pt_out_act, 2 * n + b + 1)
                for h in range(NH):
                    last = pe.transpose(A[:, r % 2, P * h:P * h + P], prob[:, h, P * r:P * r + P], ident[:, :])
                last.then_inc(pt_psum, 1)

        def pe_pv(pe, n, b):
            pe.wait_ge(pt_out_act, 2 * n + b + 1)
            pe.wait_ge(pt_out_dve, 4 * n + 2 * b + 2)
            for w in range(2):
                for h in range(NH):
                    parts = ((0, 0),) if w == 0 else ((1, 0), (2, 1))
                    for k, (r, t) in enumerate(parts):
                        last = pe.matmul(A[:, 1, (NH * w + h) * HB:(NH * w + h + 1) * HB],
                                         pt[:, r, P * h:P * h + P], v8[:, 2 * b + t, h, :],
                                         start=k == 0, stop=k == len(parts) - 1)
            last.then_inc(pv_psum, 1)

        def pe_al(pe, n):
            pe.wait_ge(aloc_done, 2 * n + 2)
            pe.wait_ge(pt_out_dve, 4 * n + 4)
            for t in range(TILES):
                last = pe.transpose(A[:, 0, P * t:P * t + P], aloc[:, t, :], ident[:, :])
            last.then_inc(al_psum, 1)

        def pe_wo(pe, n, l):
            pe.wait_ge(al_lo, n + 1)
            pe.wait_ge(lin_lo, n + 1)
            pe.wait_ge(wo_ready, l + 1)
            pe.wait_ge(exp_done, 2 * n + 2)
            for t in range(TILES):
                product(pe, A[:, 2 + t, 0:D], lambda a, c: at[:, a, c, P * t:P * t + P],
                        lambda b, c: wo[:, b, c, :]).then_inc(wo_psum, 1)

        def pe_h(pe, n, m, l, first=False):
            if m == 0:
                pe.wait_ge(xt_lo[1], 2 * n + 2)
                pe.wait_ge(w1_ready, l + 1)
            if m < 2:
                pe.wait_ge(res2, RES2_0 + 4 * n - 1 + m)
            else:
                pe.wait_ge(gelu_done, FC * n + m - 1)
            product(pe, F[:, m % 2, :], lambda a, c: w1[:, a, c, P * m:P * m + P],
                    lambda b, c: xt[1][:, b, c, :]).then_inc(h_psum, 1)

        def pe_y(pe, n, t, l):
            if t == 0:
                pe.wait_ge(h_lo, H_LO_0 + FC * n + FC)
                pe.wait_ge(w2_ready, l + 1)
            if t < 2:
                pe.wait_ge(gelu_done, FC * n + FC - 1 + t)
            else:
                pe.wait_ge(res2, RES2_0 + 4 * n + t - 1)
            passes = [(c, a, b) for c in range(FC) for a, b in PASSES]
            for k, (c, a, b) in enumerate(passes):
                last = pe.matmul(F[:, t % 2, 0:D], ht[:, a, c, P * t:P * t + P], w2[:, b, c, :],
                                 start=k == 0, stop=k == len(passes) - 1)
            last.then_inc(y_psum, 1)

        @block.tensor
        def _(pe):
            pe.wait_ge(const_ready, 1)
            pe.wait_ge(zero_ready, 1)

            def top_k():
                bank = F[:, 1, :]
                pe.wait_ge(top_step, 5)
                pe.matmul(bank[0:PRIMS, 0:2], ones64[:, 0:PRIMS], lexp[:, :], start=True, stop=True).then_inc(top_sum, 1)
                pe.wait_ge(top_step, 7)
                both = chosen[:, :, :].rearrange("i f k -> i (f k)")
                pe.matmul(bank[0:1, 64:64 + 2 * TOPK], own[:, :], both, start=True, stop=True).then_inc(top_idx, 1)
                pe.wait_ge(top_w, 1)
                pe.wait_ge(index_ready, 1)
                for j in range(2):
                    for f in range(2):
                        last = pe.matmul(bank[:, 128 + 32 * j + 16 * f:144 + 32 * j + 16 * f], lw_wide[:, f, :],
                                         chosen[:, f, :].rearrange("i (k j) -> i j k", j=2)[:, j, :], start=True, stop=True)
                last.then_inc(top_wcol_psum, 1)

            top_k()
            pe_xt(pe, 0, 0)
            pe_qk(pe, 0, 0)
            for t in range(TILES):
                pe_tok(pe, 0, t)
            pe_s(pe, 0, 0)
            pe_qnt(pe, 0)
            pe_ctx(pe, 0, 0)
            pe_ctx(pe, 0, 1)
            pe_lin(pe, 0)
            pe_pt(pe, 0, 0)
            pe_s(pe, 0, 1)
            pe_pv(pe, 0, 0)
            pe_pt(pe, 0, 1)
            pe_pv(pe, 0, 1)
            pe_al(pe, 0)
            pe_wo(pe, 0, 0)
            pe.wait_ge(b1_loaded, 16)
            pe.transpose(F[:, 0, 0:DEPTH * FC], b1_rows[:, :], ident[0:DEPTH * FC, 0:DEPTH * FC]).then_inc(b1_psum, 1)
            pe.wait_ge(b1_ready, 1)

            def step(l, p, last):
                n = 4 * l + p + 1
                attn = not (last and p == ITEMS - 1)
                la = l + 1 if p == ITEMS - 1 else l
                if attn:
                    pe_xt(pe, 0, n)
                    pe.wait_ge(res1, 4 * n)
                    pe_qk(pe, n, la)
                    for t in range(TILES):
                        pe_tok(pe, n, t)
                    pe.wait_ge(k_lo, n + 1)
                pe_xt(pe, 1, n - 1)
                pe_h(pe, n - 1, 0, l)
                if attn:
                    pe.wait_ge(xt_lo[1], 2 * n)
                    pe_s(pe, n, 0)
                pe_h(pe, n - 1, 1, l)
                pe_h(pe, n - 1, 2, l)
                if attn:
                    pe_qnt(pe, n)
                    pe_ctx(pe, n, 0)
                pe_h(pe, n - 1, 3, l)
                if attn:
                    pe_ctx(pe, n, 1)
                    pe_lin(pe, n)
                pe_h(pe, n - 1, 4, l)
                if attn:
                    pe_pt(pe, n, 0)
                    pe_s(pe, n, 1)
                pe_h(pe, n - 1, 5, l)
                if attn:
                    pe_pv(pe, n, 0)
                pe_h(pe, n - 1, 6, l)
                pe_h(pe, n - 1, 7, l)
                if attn:
                    pe_pt(pe, n, 1)
                pe_y(pe, n - 1, 0, l)
                if attn:
                    pe_pv(pe, n, 1)
                pe_y(pe, n - 1, 1, l)
                if attn:
                    pe_al(pe, n)
                pe_y(pe, n - 1, 2, l)
                if attn:
                    pe_wo(pe, n, la)
                pe_y(pe, n - 1, 3, l)

            with pe.Fori(0, DEPTH - 1) as l:
                for p in range(ITEMS):
                    step(l, p, False)
            for p in range(ITEMS):
                step(DEPTH - 1, p, True)

            pe.wait_ge(wv_loaded, 16)
            for k in range(4):
                for j in (2 * k, 2 * k + 1):
                    for c in range(DC):
                        last = pe.transpose(A[:, k, (j % 2) * D + P * c:(j % 2) * D + P * c + P],
                                            wv_raw[:, c, P * j:P * j + P], ident[:, :])
                last.then_inc(wvt_psum, 1)
            pe.wait_ge(wvt_out, 4)
            pe.wait_ge(wout_loaded, 16)
            for c in range(DC):
                for j in range(FC):
                    last = pe.matmul(A[:, 4 + c, 0:D], wvt[:, j, P * c:P * c + P], wout_raw[:, j, :],
                                     start=j == 0, stop=j == FC - 1)
                last.then_inc(wvo_psum, 1)
            pe.wait_ge(ctx_loaded, 16)
            for c in range(DC):
                for s in range(2):
                    for b in range(4):
                        last = pe.transpose(A[:, 2 * c + s, P * b:P * b + NKV], ctx_raw[:, 4 * s + b, P * c:P * c + P],
                                            ident[0:NKV, 0:NKV])
                    last.then_inc(ctxt_psum, 1)
            pe.wait_ge(wvo_out, 2)
            pe.wait_ge(ctxt_out, 4)

            def turn(f, g, r, use, peel):
                pe.wait_ge((small_loaded, big_loaded)[f][r], 32 * use)
                if not peel:
                    pe.wait_ge((small_lo, big_lo)[f], g - 1)
                if f == 0:
                    for c in range(DC):
                        last = pe.transpose(A[:, 4 + r, P * c:P * c + P], small_raw[:, r, P * c:P * c + P], ident[:, :])
                else:
                    for m in range(FC):
                        last = pe.transpose((F, A)[r][:, 4 * r + m // 4, P * (m % 4):P * (m % 4) + P],
                                            big_raw[:, r, P * m:P * m + P], ident[:, :])
                last.then_inc(at_psum, 1)

            def multiply(f, g, r, first, final):
                pe.wait_ge(small_lo, g + 1)
                pe.wait_ge(big_lo, g + 1)
                if f == 0:
                    for c in range(DC):
                        for k, (a, b) in enumerate(PASSES):
                            for s in range(2):
                                last = pe.matmul(A[:, 2 * c + s, :], small[r][a][:, P * c:P * c + P],
                                                 big[r][b][:, 512 * s:512 * s + 512], start=first and k == 0,
                                                 stop=final and k == 2, skip_group_check=True)
                else:
                    for m in range(FC):
                        for k, (a, b) in enumerate(PASSES):
                            last = pe.matmul(A[:, m // 2, D * (m % 2):D * (m % 2) + D], big[r][a][:, P * m:P * m + P],
                                             small[r][b], start=first and k == 0 and m % 2 == 0,
                                             stop=final and k == 2, skip_group_check=True)
                last.then_inc(pair_done, 1)

            def compose(f):
                h = PAIRS // 2
                base = PAIRS * f
                turn(f, base, 0, h * f + 1, f == 0)
                turn(f, base + 1, 1, h * f + 1, f == 0)
                multiply(f, base, 0, True, False)
                turn(f, base + 2, 0, h * f + 2, False)
                multiply(f, base + 1, 1, False, False)
                with pe.Fori(1, h - 1) as i:
                    turn(f, base + 2 * i + 1, 1, h * f + i + 1, False)
                    multiply(f, base + 2 * i, 0, False, False)
                    turn(f, base + 2 * i + 2, 0, h * f + i + 2, False)
                    multiply(f, base + 2 * i + 1, 1, False, False)
                turn(f, base + 2 * h - 1, 1, h * f + h, False)
                multiply(f, base + 2 * h - 2, 0, False, False)
                multiply(f, base + 2 * h - 1, 1, False, True)

            compose(0)
            pe.wait_ge(comp_lo, 4)
            pe.wait_ge(ctxt_ready, 1)
            for p in range(ITEMS):
                for t in range(TILES):
                    if p:
                        pe.wait_ge(cross_added, TILES * (p - 1) + t + 1)
                    for c in range(DC):
                        b = 2 * p + t // 2
                        rows = ctxt[:, c, b, :] if t % 2 == 0 else ctxt[:, c, b, NKV:NKV + 1].broadcast_to([P, P])
                        last = pe.matmul(A[:, t, 0:D], rows, wvo[:, c, :], start=c == 0, stop=c == DC - 1)
                    last.then_inc(cross_psum, 1)
            pe.wait_ge(cross_added, TILES * ITEMS)
            compose(1)
            pe.wait_ge(comp_lo, 8)

            def f_xt(p):
                pe.wait_ge(t_norm, ITEMS + p + 1)
                if p:
                    pe.wait_ge(f_xt_lo, 2 * p)
                for c in range(DC):
                    for t in range(TILES):
                        last = pe.transpose(A[:, c, P * t:P * t + P], x[:, TILES * p + t, P * c:P * c + P], ident[:, :])
                    last.then_inc(f_xt_psum, 1)

            f_xt(0)
            for p in range(ITEMS):
                pe.wait_ge(f_xt_lo, 2 * p + 2)
                for m in range(FC):
                    if FC * p + m >= 2:
                        pe.wait_ge(f_gelu, FC * p + m - 1)
                    product(pe, F[:, m % 2, :], lambda a, c: w1[:, a, c, P * m:P * m + P],
                            lambda b, c: xt[1][:, b, c, :]).then_inc(f_h_psum, 1)
                if p + 1 < ITEMS:
                    f_xt(p + 1)
                pe.wait_ge(f_h_lo, FC * p + FC)
                for t in range(TILES):
                    if p:
                        pe.wait_ge(f_res, TILES * (p - 1) + t + 1)
                    passes = [(c, a, b) for c in range(FC) for a, b in PASSES]
                    for k, (c, a, b) in enumerate(passes):
                        last = pe.matmul(A[:, 2 + t, 0:D], ht[:, a, c, P * t:P * t + P], w2[:, b, c, :],
                                         start=k == 0, stop=k == len(passes) - 1)
                    last.then_inc(f_y_psum, 1)


_INS = ['x', 'L0_attn_Wq', 'L0_attn_Wk', 'L0_attn_Wv', 'L0_attn_Wo', 'L0_attn_bo', 'L0_attn_ln1_g', 'L0_attn_ln1_b',
        'L0_attn_W1', 'L0_attn_b1', 'L0_attn_W2', 'L0_attn_b2', 'L0_attn_ln2_g', 'L0_attn_ln2_b',
        'ctx_1024', 'L0_xattn_Wkv', 'L0_xattn_Wout', 'L0_xattn_bout', 'L0_ffn_fc1_A', 'L0_ffn_fc1_B', 'L0_ffn_fc2_A',
        'L0_ffn_fc2_B', 'L0_ffn_fc1_logits', 'L0_ffn_fc2_logits']
_OUTS = [((8, 256, 256), 'float32')]


def kernel(**inputs):
    import numpy as _np
    import concourse.bacc as _bacc
    from concourse import mybir as _mybir
    from concourse.bass_utils import run_bass_kernel_spmd as _run

    nc = _bacc.Bacc("TRN2", target_bir_lowering=False, num_devices=1)
    arrays, args = {}, []
    for name in _INS:
        a = _np.ascontiguousarray(inputs[name])
        arrays[f"in_{name}_dram"] = a
        args.append(nc.dram_tensor(f"in_{name}_dram", a.shape, _mybir.dt.from_np(a.dtype), kind="ExternalInput").ap())
    for i, (shape, dtype) in enumerate(_OUTS):
        dt = _mybir.dt.from_np(_np.dtype(dtype))
        args.append(nc.dram_tensor(f"out_{i}_dram", shape, dt, kind="ExternalOutput").ap())
    build(nc, *args)
    r = _run(nc, [arrays], core_ids=[0])
    got = tuple(r.results[0][f"out_{i}_dram"] for i in range(len(_OUTS)))
    return got[0]
```

```python
from contextlib import ExitStack

import concourse.bass as bass
from concourse import mybir

F32 = mybir.dt.float32
F32R = mybir.dt.float32r
BF16 = mybir.dt.bfloat16
I32 = mybir.dt.int32
ALU = mybir.AluOpType
ACT = mybir.ActivationFunctionType
AX_X = mybir.AxisListType.X

P = 128
B, T, D = 8, 256, 256
DC = D // P
DEPTH = 4
FF = 4 * D
FC = FF // P
E = 32
NH = 4
BUCKET = 64
TILES = 4
TOK = TILES * P
ITEMS = B * T // TOK
HB = E + 1
SCALE = float(E) ** -0.5
MASKED = -1.0e30
EPS = 1.0e-5
NKV = 120
CB = 128
PRIMS, TOPK, RANK = 64, 32, 64
PAIRS = TOPK // 2
PASSES = ((0, 0), (1, 0), (0, 1))


def build(nc, x_in, Wq, Wk, Wv, Wo, bo, ln1_g, ln1_b, W1, b1, W2, b2, ln2_g, ln2_b,
          ctx_in, Wkv, Wout, bout, fc1_A, fc1_B, fc2_A, fc2_B, fc1_logits, fc2_logits, out):
    with ExitStack() as ctx:
        def sb(name, shape, dt=F32):
            return ctx.enter_context(nc.sbuf_tensor(name, shape, dt))

        def sem(name):
            return ctx.enter_context(nc.semaphore(name))

        x = sb("x", [P, ITEMS * TILES, D])
        wa = sb("wa", [P, 2, DC, 768], F32R)
        wo = sb("wo", [P, 2, DC, D], F32R)
        w1 = sb("w1", [P, 2, DC, FF], F32R)
        w2 = sb("w2", [P, 2, FC, D], F32R)
        raw_a = sb("raw_a", [P, DC, 1024])
        raw_f = sb("raw_f", [P, 2048])
        vec_a = sb("vec_a", [P, 3, D])
        vec_f = sb("vec_f", [P, 3, D])
        b1c = sb("b1c", [P, DEPTH * FC])
        b1_now = sb("b1_now", [P, FC])
        carrier = sb("carrier", [P, 3])
        b1_rows = sb("b1_rows", [DEPTH * FC, P])
        slot_mark = sb("slot_mark", [P, 2])
        loaded_mark = sb("loaded_mark", [P, ITEMS * TILES])
        ident = sb("ident", [P, P])
        ident_bf = sb("ident_bf", [P, P], BF16)
        mask_bf = sb("mask_bf", [P, 3 * P], BF16)
        headmask = sb("headmask", [P, NH, E])
        ones = sb("ones", [P, 1])
        minus_half = sb("minus_half", [P, 4])
        xt = [sb("xt1", [P, 2, DC, TOK], F32R), sb("xt2", [P, 2, DC, TOK], F32R)]
        ht = sb("ht", [P, 2, FC, TOK], F32R)
        scratch = sb("scratch", [P, 9760])
        v8 = scratch[:, 0:1056].rearrange("p (t h e) -> p t h e", t=TILES, h=2 * NH)
        qk = scratch[:, 1056:2080].rearrange("p (t d) -> p t d", t=TILES)
        qexp = scratch[:, 2080:2592].rearrange("p (t d) -> p t d", t=TILES)
        qf = scratch[:, 2080:2592]
        kexp = scratch[:, 2592:3104].rearrange("p (t d) -> p t d", t=TILES)
        qnt = scratch[:, 3104:3616]
        prob = scratch[:, 3616:5152].rearrange("p (h k) -> p h k", h=NH)
        pt = scratch[:, 5152:6688].rearrange("p (r k) -> p r k", r=3)
        xh = [scratch[:, a:a + 1024].rearrange("p (t d) -> p t d", t=TILES) for a in (6688, 7712)]
        hf = scratch[:, 8736:9760].rearrange("p (s t) -> p s t", s=2)
        x0 = scratch[:, 0:4096].rearrange("p (t d) -> p t d", d=D)
        wvt = scratch[:, 0:2048].rearrange("p (j i) -> p j i", j=FC)
        wvo = scratch[:, 2048:2560].rearrange("p (c n) -> p c n", c=DC)
        wv_raw = scratch[:, 4096:6144].rearrange("p (c n) -> p c n", c=DC)
        ctxt = scratch[:, 4096:6144].rearrange("p (c b t) -> p c b t", c=DC, b=B)
        small_raw = scratch[:, 6144:6656].rearrange("p (r n) -> p r n", r=2)
        wout_raw = scratch[:, 6656:8704].rearrange("p (j n) -> p j n", j=FC)
        ctx_raw = raw_a[0:NKV, :, :].rearrange("p c n -> p (c n)").rearrange("p (b n) -> p b n", b=B)
        big_raw = raw_f[:, :].rearrange("p (r n) -> p r n", r=2)
        big = [[ht[:, i, 2 * r:2 * r + 2, :].rearrange("p c n -> p (c n)") for i in range(2)] for r in range(2)]
        small = [[xt[0][:, i, r, 0:D] for i in range(2)] for r in range(2)]
        ctx_mean = sb("ctx_mean", [P, DC, B])
        tstats, tmv = sb("tstats", [P, TILES, 6]), sb("tmv", [P, TILES, 2])
        tvar, trstd = sb("tvar", [P, TILES]), sb("trstd", [P, TILES])
        top = scratch[0:PRIMS, 8736:9760]
        lrow, tie, beats = (top[:, P * i:P * i + P].rearrange("p (f n) -> p f n", f=2) for i in range(3))
        lw_wide = top[:, 384:640].rearrange("p (f n) -> p f n", f=2)
        ones64, earlier = top[:, 640:768], top[:, 768:832]
        chosen = top[:, 832:896].rearrange("p (f n) -> p f n", f=2)
        lcol, lmax, lexp, rank, lsum, lw = (sb(n, [PRIMS, 2]) for n in ("lcol", "lmax", "lexp", "rank", "lsum", "lw"))
        places_i, places = sb("places_i", [PRIMS, TOPK], I32), sb("places", [PRIMS, TOPK])
        own_i, own = sb("own_i", [PRIMS, 1], I32), sb("own", [PRIMS, 1])
        index = sb("index", [1, 2 * TOPK], I32)
        wcol = sb("wcol", [P, 2, PAIRS])
        stats = [sb("stats1", [P, TILES, 6]), sb("stats2", [P, TILES, 6])]
        mv = [sb("mv1", [P, TILES, 2]), sb("mv2", [P, TILES, 2])]
        var = [sb("var1", [P, TILES]), sb("var2", [P, TILES])]
        rstd = [sb("rstd1", [P, TILES]), sb("rstd2", [P, TILES])]
        qm = sb("qm", [P, 2, NH, TOK], F32R)
        kt = sb("kt", [P, 2, TOK], F32R)
        qmax = sb("qmax", [P, TILES, NH])
        qsum = sb("qsum", [P, TILES, NH])
        kcum = sb("kcum", [P, 2, 3])
        ctxn = sb("ctxn", [P, 2, 3, P])
        smax = sb("smax", [P, 2, 2, NH])
        psum_r = sb("psum_r", [P, 8])
        aloc = qnt.rearrange("p (t d) -> p t d", t=TILES)
        at = sb("at", [P, 2, DC, TOK], F32R)
        A = ctx.enter_context(nc.psum_tensor("A", [P, 6, 512], F32))
        F = ctx.enter_context(nc.psum_tensor("F", [P, 2, 512], F32))

        x_loaded = [sem(f"x_loaded{p}") for p in range(ITEMS)]
        raw_a_loaded, raw_w1_loaded, raw_w2_loaded = sem("raw_a_loaded"), sem("raw_w1_loaded"), sem("raw_w2_loaded")
        vec_a_loaded, vec_f_loaded, b1_loaded = sem("vec_a_loaded"), sem("vec_f_loaded"), sem("b1_loaded")
        const_step, const_ready, zero_ready = sem("const_step"), sem("const_ready"), sem("zero_ready")
        wa_hi, wa_ready, wo_hi, wo_ready = sem("wa_hi"), sem("wa_ready"), sem("wo_hi"), sem("wo_ready")
        w1_hi, w1_ready, w2_hi, w2_ready = sem("w1_hi"), sem("w1_ready"), sem("w2_hi"), sem("w2_ready")
        ln_stats = [sem("ln1_stats"), sem("ln2_stats")]
        ln_mv = [sem("ln1_mv"), sem("ln2_mv")]
        ln_var = [sem("ln1_var"), sem("ln2_var")]
        ln_rstd = [sem("ln1_rstd"), sem("ln2_rstd")]
        ln_xhat = [sem("ln1_xhat"), sem("ln2_xhat")]
        ln_ready = [sem("ln1_ready"), sem("ln2_ready")]
        biased = [sem("bo_added"), sem("b2_added")]
        xt_psum = [sem("xt1_psum"), sem("xt2_psum")]
        xt_hi = [sem("xt1_hi"), sem("xt2_hi")]
        xt_lo = [sem("xt1_lo"), sem("xt2_lo")]
        qk_psum, q_hi, k_hi, q_lo, k_lo = sem("qk_psum"), sem("q_hi"), sem("k_hi"), sem("q_lo"), sem("k_lo")
        tok_psum, tok_out = sem("tok_psum"), sem("tok_out")
        qmax_done, qsub_done, qexp_done, kexp_done = sem("qmax_done"), sem("qsub_done"), sem("qexp_done"), sem("kexp_done")
        qsum_done, qrec_done, qn_done, krelu_done, kf_done = (
            sem("qsum_done"), sem("qrec_done"), sem("qn_done"), sem("krelu_done"), sem("kf_done"))
        qnt_psum, qnt_out, ctx_psum, kcum_done, krec_done, ctxn_done, lin_psum, lin_hi, lin_lo = (
            sem("qnt_psum"), sem("qnt_out"), sem("ctx_psum"), sem("kcum_done"), sem("krec_done"),
            sem("ctxn_done"), sem("lin_psum"), sem("lin_hi"), sem("lin_lo"))
        s_psum, smax_done, nmax_done, exp_done = sem("s_psum"), sem("smax_done"), sem("nmax_done"), sem("exp_done")
        pt_psum, pt_out_act, pt_out_dve, pv_psum, prec_done, aloc_done = (
            sem("pt_psum"), sem("pt_out_act"), sem("pt_out_dve"), sem("pv_psum"), sem("prec_done"), sem("aloc_done"))
        al_psum, al_hi, al_lo, wo_psum, res1 = sem("al_psum"), sem("al_hi"), sem("al_lo"), sem("wo_psum"), sem("res1")
        h_psum, gelu_done, h_hi, h_lo, y_psum, res2 = (
            sem("h_psum"), sem("gelu_done"), sem("h_hi"), sem("h_lo"), sem("y_psum"), sem("res2"))
        top_wcol_psum = sem("top_wcol_psum")
        b1_turn = sem("b1_turn")
        stored, b1_psum, b1_ready = sem("stored"), sem("b1_psum"), sem("b1_ready")
        logits_loaded, top_const, top_step, top_exp, top_sum, top_w, top_idx, top_wcol, index_ready = (
            sem(n) for n in ("logits_loaded", "top_const", "top_step", "top_exp", "top_sum", "top_w", "top_idx",
                             "top_wcol", "index_ready"))
        x0_loaded, wv_loaded, wout_loaded, ctx_loaded, bout_loaded = (
            sem(n) for n in ("x0_loaded", "wv_loaded", "wout_loaded", "ctx_loaded", "bout_loaded"))
        big_loaded = [sem("big_loaded0"), sem("big_loaded1")]
        small_loaded = [sem("small_loaded0"), sem("small_loaded1")]
        t_sum, t_stats, t_mv, t_var, t_rstd, t_norm, t_bout = (
            sem(n) for n in ("t_sum", "t_stats", "t_mv", "t_var", "t_rstd", "t_norm", "t_bout"))
        wvt_psum, wvt_out, wvo_psum, wvo_out, ctxt_psum, ctxt_out, ctx_sum, ctxt_ready, cross_psum, cross_added = (
            sem(n) for n in ("wvt_psum", "wvt_out", "wvo_psum", "wvo_out", "ctxt_psum", "ctxt_out", "ctx_sum",
                             "ctxt_ready", "cross_psum", "cross_added"))
        at_psum, big_hi, big_lo, small_hi, small_lo, pair_done, comp_hi, comp_lo = (
            sem(n) for n in ("at_psum", "big_hi", "big_lo", "small_hi", "small_lo", "pair_done", "comp_hi", "comp_lo"))
        f_xt_psum, f_xt_hi, f_xt_lo, f_h_psum, f_gelu, f_h_hi, f_h_lo, f_y_psum, f_res = (
            sem(n) for n in ("f_xt_psum", "f_xt_hi", "f_xt_lo", "f_h_psum", "f_gelu", "f_h_hi", "f_h_lo", "f_y_psum",
                             "f_res"))
        H_LO_0 = 2
        RES2_0 = 4 * ITEMS

        def slot(p):
            return slice(TILES * p, TILES * p + TILES)

        def w1_part(k):
            c, s = k // 2, k % 2

            def dst(i):
                return w1[:, i, c, :].rearrange("q (m p) -> q p m", p=P)[:, 64 * s:64 * s + 64, :]
            return dst, A[:, k, :].rearrange("q (p m) -> q p m", m=FC)

        def w2_part(k):
            def dst(i):
                return w2[:, i, 2 * k:2 * k + 2, :].rearrange("p m n -> p (m n)")
            return dst, A[:, k, :]


        def load_a(sp, l, first=False):
            if not first:
                sp.wait_ge(wo_ready, l)
            for i, (w, lo, hi, at_col) in enumerate((
                    (Wq, 0, P, 0), (Wk, 0, P, P), (Wv, 0, D, 2 * P), (Wq, P, D, 4 * P), (Wk, P, D, 5 * P),
                    (Wo, 0, D, 6 * P))):
                src = w[bass.ds(l, 1)].rearrange("a (c p) n -> p (a c) n", p=P)[:, :, lo:hi]
                sp.dma_start(raw_a[:, :, at_col:at_col + hi - lo], src).then_inc(raw_a_loaded, 16)

        def load_w1(sp, l, first=False):
            if not first:
                sp.wait_ge(w2_ready, l)
            sp.dma_start(raw_f[:, :].rearrange("p (c n) -> p c n", c=DC),
                         W1[bass.ds(l, 1)].rearrange("a (c p) n -> p (a c) n", p=P)).then_inc(raw_w1_loaded, 16)

        def load_w2(sp, l):
            sp.wait_ge(w1_ready, l + 1)
            sp.dma_start(raw_f[:, :].rearrange("p (c n) -> p c n", c=FC),
                         W2[bass.ds(l, 1)].rearrange("a (c p) n -> p (a c) n", p=P)).then_inc(raw_w2_loaded, 16)

        def load_vec(sp, l, which, n=None):
            dst, src, loaded = ((vec_a, (ln1_g, ln1_b, bo), vec_a_loaded), (vec_f, (ln2_g, ln2_b, b2), vec_f_loaded))[which]
            if n is not None:
                sp.wait_ge(biased[which], n + 1)
                sp.wait_ge(ln_ready[which], n + 1)
            for i, s in enumerate(src):
                row = s[bass.ds(l, 1)]
                sp.dma_start(dst[:, i, :], row.broadcast_to([P, D])).then_inc(loaded, 16)

        block = ctx.enter_context(nc.Block())

        @block.sync
        def _(sp):
            sp.dma_start(x[:, slot(0), :], x_in[0:2].rearrange("b (s p) d -> p (b s) d", p=P)).then_inc(x_loaded[0], 16)
            load_vec(sp, 0, 0)
            load_a(sp, 0, first=True)
            for p in range(1, ITEMS):
                sp.dma_start(x[:, slot(p), :],
                             x_in[2 * p:2 * p + 2].rearrange("b (s p) d -> p (b s) d", p=P)).then_inc(x_loaded[p], 16)
            sp.dma_start(b1_rows[:, :], b1.rearrange("l (m p) -> (l m) p", p=P)).then_inc(b1_loaded, 16)
            for f, lg in enumerate((fc1_logits, fc2_logits)):
                sp.dma_start(lrow[:, f, :], lg.rearrange("(a n) -> a n", a=1).broadcast_to([PRIMS, PRIMS])).then_inc(logits_loaded, 16)
                sp.dma_start(lcol[:, f:f + 1], lg.rearrange("(p o) -> p o", o=1)).then_inc(logits_loaded, 16)
            load_w1(sp, 0, first=True)
            load_vec(sp, 0, 1)
            load_w2(sp, 0)
            with sp.Fori(0, DEPTH - 1) as l:
                load_a(sp, l + 1)
                load_w1(sp, l + 1)
                load_vec(sp, l + 1, 0, 4 * l + 3)
                load_vec(sp, l + 1, 1, 4 * l + 3)
                load_w2(sp, l + 1)
            sp.wait_ge(wo_ready, DEPTH)
            sp.dma_start(ctx_raw, ctx_in.rearrange("b t d -> t b d")).then_inc(ctx_loaded, 16)
            sp.wait_ge(biased[0], 4 * DEPTH)
            sp.wait_ge(ln_ready[0], 4 * DEPTH)
            sp.dma_start(vec_a[:, 0, :], bout.rearrange("(a n) -> a n", a=1).broadcast_to([P, D])).then_inc(bout_loaded, 16)
            sp.wait_ge(wo_psum, 16 * DEPTH)
            sp.wait_ge(xt_psum[1], 8 * DEPTH)
            sp.dma_start(x0, x_in.rearrange("b (s p) d -> p (b s) d", p=P)).then_inc(x0_loaded, 16)
            sp.dma_start(wv_raw, Wkv.rearrange("(c p) n -> p c n", p=P)[:, :, 1024:2048]).then_inc(wv_loaded, 16)
            sp.dma_start(wout_raw, Wout.rearrange("(j p) n -> p j n", p=P)).then_inc(wout_loaded, 16)
            sp.wait_ge(w2_ready, DEPTH)
            sp.wait_ge(index_ready, 1)

            def load_pair(f, g, kk, r, peel):
                if not peel:
                    sp.wait_ge(big_lo, g - 1)
                    sp.wait_ge(small_lo, g - 1)
                for j in range(2):
                    k = sp.value_load(index[0:1, bass.ds(f * TOPK + 2 * kk + j, 1)], min_val=0, max_val=PRIMS - 1)
                    rows = slice(RANK * j, RANK * j + RANK)
                    if f == 0:
                        sp.dma_start(small_raw[:, r, :].rearrange("p (c n) -> p c n", c=DC)[:, :, rows],
                                     fc1_A[bass.ds(k, 1)].rearrange("a (c p) r -> p (a c) r", p=P)).then_inc(small_loaded[r], 16)
                        sp.dma_start(big_raw[rows, r, :],
                                     fc1_B[bass.ds(k, 1)].rearrange("a r n -> (a r) n")).then_inc(big_loaded[r], 16)
                    else:
                        sp.dma_start(big_raw[:, r, :].rearrange("p (m n) -> p m n", m=FC)[:, :, rows],
                                     fc2_A[bass.ds(k, 1)].rearrange("a (p m) r -> p (a m) r", p=P)).then_inc(big_loaded[r], 16)
                        sp.dma_start(small_raw[rows, r, :],
                                     fc2_B[bass.ds(k, 1)].rearrange("a r n -> (a r) n")).then_inc(small_loaded[r], 16)

            for r in range(2):
                load_pair(0, r, r, r, True)
            with sp.Fori(1, PAIRS // 2) as i:
                for r in range(2):
                    load_pair(0, 2 * i + r, 2 * i + r, r, False)
            with sp.Fori(0, PAIRS // 2) as i:
                for r in range(2):
                    load_pair(1, PAIRS + 2 * i + r, 2 * i + r, r, False)
            for p in range(ITEMS):
                sp.wait_ge(t_norm, 2 * ITEMS + p + 1)
                sp.dma_start(out[2 * p:2 * p + 2].rearrange("b (s p) d -> p (b s) d", p=P), x[:, slot(p), :]).then_inc(stored, 16)
            sp.wait_ge(stored, 16 * ITEMS)

        def split(pool, dst, src, hi_sem, ready, l):
            one = ones[:, :].broadcast_to([P, 2048]) if len(src.shape) == 2 else ones[:, :].rearrange(
                "p (a o) -> p a o", a=1).broadcast_to(list(src.shape))
            pool.tensor_tensor(dst[0], src, one, ALU.mult).then_inc(hi_sem, 1)
            pool.wait_ge(hi_sem, l + 1)
            pool.tensor_tensor(dst[1], src, dst[0].bitcast(F32), ALU.subtract).then_inc(ready, 1)

        def split_wa(pool, l, n=None):
            pool.wait_ge(raw_a_loaded, 96 * (l + 1))
            if n is not None:
                pool.wait_ge(tok_psum, 4 * n + 4)
            split(pool, [wa[:, i] for i in range(2)], raw_a[:, :, 0:768], wa_hi, wa_ready, l)

        def split_wo(pool, l, n=None):
            pool.wait_ge(raw_a_loaded, 96 * (l + 1))
            if n is not None:
                pool.wait_ge(wo_psum, 4 * n + 4)
            split(pool, [wo[:, i] for i in range(2)], raw_a[:, :, 768:1024], wo_hi, wo_ready, l)

        def split_w1(pool, l, n=None):
            pool.wait_ge(raw_w1_loaded, 16 * (l + 1))
            if n is not None:
                pool.wait_ge(h_psum, FC * n + FC)
            split(pool, [w1[:, i].rearrange("p c n -> p (c n)") for i in range(2)], raw_f[:, :], w1_hi, w1_ready, l)

        def split_w2(pool, l, n=None):
            pool.wait_ge(raw_w2_loaded, 16 * (l + 1))
            if n is not None:
                pool.wait_ge(y_psum, 4 * n + 4)
            split(pool, [w2[:, i].rearrange("p c n -> p (c n)") for i in range(2)], raw_f[:, :], w2_hi, w2_ready, l)

        def pool_rstd(pool, i, n):
            pool.wait_ge(ln_var[i], n + 1)
            pool.tensor_tensor(rstd[i][:, :], var[i][:, :], minus_half[:, :], ALU.pow).then_inc(ln_rstd[i], 1)

        def pool_bias(pool, i, n, p):
            vec = (vec_a, vec_f)[i]
            pool.wait_ge(ln_ready[i], n + 1)
            pool.tensor_tensor(x[:, slot(p), :], x[:, slot(p), :], vec[:, 2:3, :].broadcast_to([P, TILES, D]),
                               ALU.add).then_inc(biased[i], 1)

        def pool_q_lo(pool, n):
            pool.wait_ge(q_hi, n + 1)
            for h in range(NH):
                r = slice(E * h, E * h + E)
                last = pool.tensor_tensor(qm[r, 1, h, :], qf[r, :], qm[r, 0, h, :].bitcast(F32), ALU.subtract)
            last.then_inc(q_lo, 1)
            pool.wait_ge(q_lo, n + 1)

        def pool_h_lo(pool, n, m):
            pool.wait_ge(h_hi, FC * n + m + 1)
            pool.tensor_tensor(ht[:, 1, m, :], hf[:, m % 2, :], ht[:, 0, m, :].bitcast(F32),
                               ALU.subtract).then_inc(h_lo, 1)

        @block.gpsimd
        def _(pool):
            pool.memset(ones[:, :], 1.0).then_inc(const_step, 1)
            pool.memset(minus_half[:, :], -0.5).then_inc(const_step, 1)
            pool.memset(ident[:, :], 0.0).then_inc(const_step, 1)
            pool.memset(ident_bf[:, :], 0.0).then_inc(const_step, 1)
            pool.memset(mask_bf[:, :], 0.0).then_inc(const_step, 1)
            pool.memset(headmask[:, :, :], 1.0).then_inc(const_step, 1)
            pool.memset(v8[:, :, :, :], 1.0).then_inc(const_step, 1)
            for i in range(H_LO_0):
                pool.memset(slot_mark[:, i:i + 1], 0.0).then_inc(h_lo, 1)
            pool.wait_ge(const_step, 7)
            for m in (ident, ident_bf):
                pool.affine_select(out=m[:, :], in_=m[:, :], compare_op=ALU.not_equal, fill=1.0, base=0,
                                   pattern=[[-1, P]], channel_multiplier=1).then_inc(const_step, 1)
            for col in (0, 2 * P):
                m = mask_bf[:, col:col + P]
                pool.affine_select(out=m, in_=m, compare_op=ALU.is_ge, fill=MASKED, base=0,
                                   pattern=[[-1, P]], channel_multiplier=1).then_inc(const_step, 1)
            pool.affine_select(out=headmask[:, :, :], in_=headmask[:, :, :], compare_op=ALU.is_ge, fill=0.0, base=0,
                               pattern=[[-E, NH], [0, E]], channel_multiplier=1).then_inc(const_step, 1)
            pool.wait_ge(const_step, 12)
            pool.affine_select(out=headmask[:, :, :], in_=headmask[:, :, :], compare_op=ALU.is_ge, fill=0.0, base=E - 1,
                               pattern=[[E, NH], [0, E]], channel_multiplier=-1).then_inc(const_ready, 1)
            pool.wait_ge(const_ready, 1)
            pool_rstd(pool, 0, 0)
            pool.iota(places_i[:, :], pattern=[[1, TOPK]], base=0, channel_multiplier=0).then_inc(top_const, 1)
            pool.iota(own_i[:, :], pattern=[[0, 1]], base=0, channel_multiplier=1).then_inc(top_const, 1)
            pool.memset(ones64[:, :], 1.0).then_inc(top_const, 1)
            pool.memset(earlier[:, :], 1.0).then_inc(top_const, 1)
            pool.wait_ge(top_const, 4)
            pool.affine_select(out=earlier[:, :], in_=earlier[:, :], compare_op=ALU.is_gt, fill=0.0, base=0,
                               pattern=[[-1, PRIMS]], channel_multiplier=1).then_inc(top_const, 1)
            split_wa(pool, 0)
            pool.wait_ge(zero_ready, 1)
            pool.wait_ge(top_const, 5)
            pool.wait_ge(wa_ready, 1)
            pool_q_lo(pool, 0)
            pool_bias(pool, 0, 0, 0)
            split_wo(pool, 0)
            split_w1(pool, 0)

            def step(l, p, last, mlp=True):
                n = 4 * l + p + 1
                attn = not (last and p == ITEMS - 1)
                nxt = not (last and p >= ITEMS - 2)
                if mlp:
                    pool_bias(pool, 1, n - 1, p)
                    for m in range(FC):
                        pool_h_lo(pool, n - 1, m)
                if p == ITEMS - 2 and not last:
                    split_wa(pool, l + 1, n)
                if nxt:
                    pool_rstd(pool, 0, n + 1)
                    pool_bias(pool, 0, n + 1, (p + 2) % ITEMS)
                if p == ITEMS - 1 and not last:
                    split_wo(pool, l + 1, n - 1)
                    split_w1(pool, l + 1, n - 1)
                if not mlp:
                    split_w2(pool, 0)
                if nxt:
                    pool.wait_ge(biased[0], n + 2)
                    if p == ITEMS - 1 and not last:
                        pool.wait_ge(w1_ready, l + 2)
                    if not mlp:
                        pool.wait_ge(w2_ready, 1)
                    pool_q_lo(pool, n + 1)
                if attn:
                    pool_rstd(pool, 1, n)
                if p == ITEMS - 1 and not last:
                    split_w2(pool, l + 1, n - 1)

            step(0, -1, False, mlp=False)
            with pool.Fori(0, DEPTH - 1) as l:
                for p in range(ITEMS):
                    step(l, p, False)
            for p in range(ITEMS):
                step(DEPTH - 1, p, True)

            def inverse_std(q):
                pool.wait_ge(t_var, q + 1)
                pool.tensor_tensor(trstd[:, :], tvar[:, :], minus_half[:, :], ALU.pow).then_inc(t_rstd, 1)

            pool.wait_ge(bout_loaded, 16)
            for p in range(ITEMS):
                inverse_std(p)
                pool.wait_ge(t_norm, p + 1)
                pool.tensor_tensor(x[:, slot(p), :], x[:, slot(p), :],
                                   vec_a[:, 0:1, :].broadcast_to([P, TILES, D]), ALU.add).then_inc(t_bout, 1)
            for p in range(ITEMS):
                inverse_std(ITEMS + p)
            for p in range(ITEMS):
                for m in range(FC):
                    pool.wait_ge(f_h_hi, FC * p + m + 1)
                    pool.tensor_tensor(ht[:, 1, m, :], hf[:, m % 2, :], ht[:, 0, m, :].bitcast(F32),
                                       ALU.subtract).then_inc(f_h_lo, 1)
                inverse_std(2 * ITEMS + p)

        def ln(dve, i, n, p, l):
            for t in range(TILES):
                last = dve.bn_stats(stats[i][:, t, :], x[:, TILES * p + t, :])
            last.then_inc(ln_stats[i], 1)
            dve.wait_ge(ln_stats[i], n + 1)
            dve.memset(carrier[:, 0:1], 0.0)
            for t in range(TILES):
                last = dve.bn_aggr(mv[i][:, t, :], stats[i][:, t, :])
            last.then_inc(ln_mv[i], 1)
            dve.wait_ge(ln_mv[i], n + 1)
            dve.tensor_scalar(var[i][:, :], mv[i][:, :, 1], EPS, None, ALU.add).then_inc(ln_var[i], 1)
            vec, loaded = ((vec_a, vec_a_loaded), (vec_f, vec_f_loaded))[i]
            dve.wait_ge(loaded, 48 * (l + 1))
            for t in range(TILES):
                last = dve.scalar_tensor_tensor(out=xh[i][:, t, :], in0=x[:, TILES * p + t, :], scalar=mv[i][:, t, 0:1],
                                                in1=vec[:, 0, :], op0=ALU.subtract, op1=ALU.mult)
            last.then_inc(ln_xhat[i], 1)
            dve.wait_ge(ln_rstd[i], n + 1)
            dve.wait_ge(ln_xhat[i], n + 1)
            for t in range(TILES):
                last = dve.scalar_tensor_tensor(out=xh[i][:, t, :], in0=xh[i][:, t, :], scalar=rstd[i][:, t:t + 1],
                                                in1=vec[:, 1, :], op0=ALU.mult, op1=ALU.add)
            last.then_inc(ln_ready[i], 1)

        def lo(dve, dst, src, hi):
            return dve.tensor_tensor(dst, src, hi.bitcast(F32), ALU.subtract)

        def xt_bank(i, c):
            return (A[:, 2 + c, :], F[:, c, :])[i]

        def dve_xt_lo(dve, i, n):
            for c in range(DC):
                dve.wait_ge(xt_hi[i], 2 * n + c + 1)
                lo(dve, xt[i][:, 1, c, :], xt_bank(i, c), xt[i][:, 0, c, :]).then_inc(xt_lo[i], 1)

        def dve_k_lo(dve, n):
            dve.wait_ge(k_hi, n + 1)
            lo(dve, kt[:, 1, :], A[:, 5, :], kt[:, 0, :]).then_inc(k_lo, 1)

        def heads(ap):
            return ap.rearrange("p t (h e) -> p t h e", h=NH)

        def over_e(ap):
            return ap.rearrange("p t (h o) -> p t h o", o=1).broadcast_to([P, TILES, NH, E])

        def dve_features(dve, n):
            dve.wait_ge(tok_out, 4 * n + 4)
            q = qk[:, :, 0:P]
            dve.tensor_reduce(qmax[:, :, :], heads(q), AX_X, ALU.max).then_inc(qmax_done, 1)
            dve.wait_ge(qmax_done, n + 1)
            dve.wait_ge(q_lo, n + 1)
            dve.tensor_tensor(heads(qexp[:, :, :]), heads(q), over_e(qmax[:, :, :]), ALU.subtract).then_inc(qsub_done, 1)

        def dve_features2(dve, n):
            k = qk[:, :, P:2 * P]
            dve.wait_ge(kexp_done, n + 1)
            dve.tensor_scalar(k, k, 0.0, None, ALU.max).then_inc(krelu_done, 1)
            dve.wait_ge(krelu_done, n + 1)
            dve.scalar_tensor_tensor(out=kexp[:, :, :], in0=kexp[:, :, :], scalar=1.0, in1=k,
                                     op0=ALU.min, op1=ALU.add).then_inc(kf_done, 1)
            dve.wait_ge(qexp_done, n + 1)
            dve.tensor_reduce(qsum[:, :, :], heads(qexp[:, :, :]), AX_X, ALU.add).then_inc(qsum_done, 1)
            dve.wait_ge(qsum_done, n + 1)
            dve.reciprocal(qsum[:, :, :], qsum[:, :, :]).then_inc(qrec_done, 1)
            dve.wait_ge(qrec_done, n + 1)
            dve.tensor_tensor(heads(qexp[:, :, :]), heads(qexp[:, :, :]), over_e(qsum[:, :, :]),
                              ALU.mult).then_inc(qn_done, 1)

        def dve_ctx(dve, n, b):
            dve.wait_ge(ctx_psum, 2 * n + b + 1)
            ps = A[:, 1 - b, 0:3 * NH * HB].rearrange("p (j h e) -> p j h e", j=3, h=NH)
            dve.tensor_scalar(kcum[:, b, :], ps[:, :, 0, E], 1e-6, None, ALU.add).then_inc(kcum_done, 1)
            dve.wait_ge(kcum_done, 2 * n + b + 1)
            dve.reciprocal(kcum[:, b, :], kcum[:, b, :]).then_inc(krec_done, 1)
            dve.wait_ge(krec_done, 2 * n + b + 1)
            for j in range(3):
                last = dve.scalar_tensor_tensor(
                    out=ctxn[:, b, j, :].rearrange("p (h e) -> p h e", h=NH), in0=ps[:, j, :, 0:E],
                    scalar=kcum[:, b, j:j + 1], in1=headmask[:, :, :], op0=ALU.mult, op1=ALU.mult)
            last.then_inc(ctxn_done, 1)

        def later_buckets(ap):
            return ap.rearrange("p (b t) -> p b t", b=2)[:, :, BUCKET:T]

        def dve_lin_lo(dve, n):
            dve.wait_ge(lin_hi, n + 1)
            lo(dve, later_buckets(at[:, 1, 1, :]), later_buckets(A[:, 1, :]),
               later_buckets(at[:, 0, 1, :])).then_inc(lin_lo, 1)

        def dve_max(dve, n, b):
            dve.wait_ge(s_psum, 2 * n + b + 1)
            dve.tensor_reduce(smax[:, b, 0, :], A[:, 2:6, 0:P], AX_X, ALU.max)
            dve.tensor_reduce(smax[:, b, 1, :], A[:, 2:6, P:3 * P], AX_X, ALU.max).then_inc(smax_done, 1)
            dve.wait_ge(smax_done, 2 * n + b + 1)
            dve.tensor_scalar(smax[:, b, :, :], smax[:, b, :, :], -SCALE, None, ALU.mult).then_inc(nmax_done, 1)

        def dve_pt(dve, n, b):
            for r in (1, 2):
                dve.wait_ge(pt_psum, 6 * n + 3 * b + r + 1)
                dve.tensor_copy(pt[:, r, :], A[:, r % 2, :]).then_inc(pt_out_dve, 1)

        def dve_aloc(dve, n, b):
            dve.wait_ge(pv_psum, 2 * n + b + 1)
            ps = A[:, 1, 0:8 * HB].rearrange("p (w e) -> p w e", w=8)
            dve.reciprocal(psum_r[:, :], ps[:, :, E]).then_inc(prec_done, 1)
            dve.wait_ge(prec_done, 2 * n + b + 1)
            dve.tensor_tensor(aloc[:, 2 * b:2 * b + 2, :].rearrange("p t (h e) -> p (t h) e", h=NH), ps[:, :, 0:E],
                              psum_r[:, :].rearrange("p (w o) -> p w o", o=1).broadcast_to([P, 8, E]),
                              ALU.mult).then_inc(aloc_done, 1)

        def dve_al_lo(dve, n):
            dve.wait_ge(al_hi, n + 1)
            lo(dve, at[:, 1, 0, :], A[:, 0, :], at[:, 0, 0, :]).then_inc(al_lo, 1)

        def dve_res1(dve, n, p):
            dve.wait_ge(biased[0], n + 1)
            for t in range(TILES):
                dve.wait_ge(wo_psum, 4 * n + t + 1)
                xs = x[:, TILES * p + t, :]
                dve.tensor_tensor(xs, A[:, (2, 3, 0, 1)[t], 0:D], xs, ALU.add).then_inc(res1, 1)
            dve.wait_ge(res1, 4 * n + 4)

        def dve_h_hi(dve, n, m):
            dve.wait_ge(gelu_done, FC * n + m + 1)
            dve.tensor_copy(ht[:, 0, m, :], hf[:, m % 2, :]).then_inc(h_hi, 1)

        def dve_res2(dve, n, p, t):
            if t == 0:
                dve.wait_ge(biased[1], n + 1)
            dve.wait_ge(y_psum, 4 * n + t + 1)
            xs = x[:, TILES * p + t, :]
            dve.tensor_tensor(xs, F[:, t % 2, 0:D], xs, ALU.add).then_inc(res2, 1)

        @block.vector
        def _(dve):
            dve.memset(qm[:, :, :, :].bitcast(F32), 0.0)
            for i in range(2):
                last = dve.memset(at[:, i, 1, :].bitcast(F32), 0.0)
            last.then_inc(zero_ready, 1)
            dve.wait_ge(x_loaded[0], 16)
            ln(dve, 0, 0, 0, 0)
            for p in range(ITEMS):
                dve.wait_ge(x_loaded[p], 16)
                for t in range(TILES):
                    dve.memset(loaded_mark[:, TILES * p + t:TILES * p + t + 1], 0.0).then_inc(res2, 1)

            def top_k():
                dve.wait_ge(logits_loaded, 64)
                dve.wait_ge(top_const, 5)
                dve.tensor_copy(places[:, :], places_i[:, :])
                dve.tensor_copy(own[:, :], own_i[:, :])
                for f in range(2):
                    dve.scalar_tensor_tensor(out=tie[:, f, :], in0=lrow[:, f, :], scalar=lcol[:, f:f + 1],
                                             in1=earlier[:, :], op0=ALU.is_equal, op1=ALU.mult)
                dve.tensor_reduce(lmax[:, :], lrow[:, :, :], AX_X, ALU.max).then_inc(top_step, 1)
                dve.wait_ge(top_step, 1)
                dve.tensor_scalar(lmax[:, :], lmax[:, :], -1.0, None, ALU.mult).then_inc(top_step, 1)
                for f in range(2):
                    last = dve.scalar_tensor_tensor(out=beats[:, f, :], in0=lrow[:, f, :], scalar=lcol[:, f:f + 1],
                                                    in1=tie[:, f, :], op0=ALU.is_gt, op1=ALU.add)
                last.then_inc(top_step, 1)
                dve.wait_ge(top_step, 3)
                dve.tensor_reduce(rank[:, :], beats[:, :, :], AX_X, ALU.add).then_inc(top_step, 1)
                dve.wait_ge(top_step, 4)
                dve.wait_ge(top_exp, 1)
                dve.scalar_tensor_tensor(out=lexp[:, :], in0=rank[:, :], scalar=TOPK - 0.5, in1=lexp[:, :],
                                         op0=ALU.is_lt, op1=ALU.mult).then_inc(top_step, 1)
                for f in range(2):
                    last = dve.tensor_scalar(chosen[:, f, :], places[:, :], rank[:, f:f + 1], None, ALU.is_equal)
                last.then_inc(top_step, 1)
                dve.wait_ge(top_sum, 1)
                dve.reciprocal(lsum[:, :], F[0:PRIMS, 1, 0:2]).then_inc(top_step, 1)
                dve.wait_ge(top_step, 7)
                dve.tensor_tensor(lw[:, :], lexp[:, :], lsum[:, :], ALU.mult).then_inc(top_step, 1)
                dve.wait_ge(top_step, 8)
                for f in range(2):
                    last = dve.tensor_scalar(lw_wide[:, f, :], ones64[:, :], lw[:, f:f + 1], None, ALU.mult)
                last.then_inc(top_w, 1)
                dve.wait_ge(top_idx, 1)
                dve.tensor_copy(index[:, :], F[0:1, 1, 64:64 + 2 * TOPK]).then_inc(index_ready, 1)
                dve.wait_ge(top_wcol_psum, 1)
                for j in range(2):
                    rows = slice(RANK * j, RANK * j + RANK)
                    last = dve.tensor_copy(wcol[rows, :, :], F[rows, 1, 128 + 32 * j:160 + 32 * j].rearrange(
                        "p (f k) -> p f k", f=2))
                last.then_inc(top_wcol, 1)

            dve_xt_lo(dve, 0, 0)
            def step(l, p, last, mlp=True):
                n = 4 * l + p + 1
                pa = (p + 1) % ITEMS
                attn = not (last and p == ITEMS - 1)
                nxt = not (last and p >= ITEMS - 2)
                la = l + 1 if p == ITEMS - 1 else l

                def h_hi(*chunks):
                    for m in chunks if mlp else ():
                        dve_h_hi(dve, n - 1, m)

                def y_add(t):
                    if mlp:
                        dve_res2(dve, n - 1, p, t)

                if attn:
                    dve_k_lo(dve, n)
                    dve_features(dve, n)
                if mlp:
                    dve_xt_lo(dve, 1, n - 1)
                if attn:
                    dve_features2(dve, n)
                    dve_max(dve, n, 0)
                h_hi(0, 1, 2, 3)
                if attn:
                    dve_ctx(dve, n, 0)
                h_hi(4, 5)
                if attn:
                    dve_ctx(dve, n, 1)
                h_hi(6, 7)
                if attn:
                    dve_lin_lo(dve, n)
                if nxt:
                    if not mlp:
                        dve.wait_ge(x_loaded[1], 16)
                    dve.wait_ge(res2, 4 * (n + 1) + 4)
                    ln(dve, 0, n + 1, (pa + 1) % ITEMS, l + 1 if p >= ITEMS - 2 else l)
                y_add(0)
                y_add(1)
                if attn:
                    dve_pt(dve, n, 0)
                    dve_max(dve, n, 1)
                    dve_aloc(dve, n, 0)
                y_add(2)
                if attn:
                    dve_pt(dve, n, 1)
                if nxt:
                    dve_xt_lo(dve, 0, n + 1)
                y_add(3)
                if attn:
                    dve_aloc(dve, n, 1)
                    dve_al_lo(dve, n)
                    dve_res1(dve, n, pa)
                    ln(dve, 1, n, pa, la)

            step(0, -1, False, mlp=False)
            top_k()
            with dve.Fori(0, DEPTH - 1) as l:
                for p in range(ITEMS):
                    step(l, p, False)
            for p in range(ITEMS):
                step(DEPTH - 1, p, True)

            def norm(q, p):
                for t in range(TILES):
                    last = dve.bn_stats(tstats[:, t, :], x[:, TILES * p + t, :])
                last.then_inc(t_stats, 1)
                dve.wait_ge(t_stats, q + 1)
                for t in range(TILES):
                    last = dve.bn_aggr(tmv[:, t, :], tstats[:, t, :])
                last.then_inc(t_mv, 1)
                dve.wait_ge(t_mv, q + 1)
                dve.tensor_scalar(tvar[:, :], tmv[:, :, 1], EPS, None, ALU.add).then_inc(t_var, 1)
                dve.wait_ge(t_rstd, q + 1)
                for t in range(TILES):
                    xs = x[:, TILES * p + t, :]
                    last = dve.tensor_scalar(xs, xs, tmv[:, t, 0:1], trstd[:, t:t + 1], ALU.subtract, ALU.mult)
                last.then_inc(t_norm, 1)

            dve.wait_ge(x0_loaded, 16)
            dve.wait_ge(res2, RES2_0 + 16 * DEPTH)
            for p in range(ITEMS):
                dve.tensor_tensor(x[:, slot(p), :], x[:, slot(p), :], x0[:, slot(p), :], ALU.add).then_inc(t_sum, 1)
                dve.wait_ge(t_sum, p + 1)
                norm(p, p)
            for c in range(DC):
                for s in range(2):
                    dve.wait_ge(ctxt_psum, 2 * c + s + 1)
                    if c == 0 and s == 0:
                        dve.wait_ge(wvt_psum, 4)
                    dve.tensor_copy(ctxt[:, c, 4 * s:4 * s + 4, 0:NKV],
                                    A[:, 2 * c + s, :].rearrange("p (b t) -> p b t", b=4)[:, :, 0:NKV]).then_inc(ctxt_out, 1)
            dve.wait_ge(ctxt_out, 4)
            dve.tensor_reduce(ctx_mean[:, :, :], ctxt[:, :, :, 0:NKV], AX_X, ALU.add).then_inc(ctx_sum, 1)
            dve.wait_ge(ctx_sum, 1)
            for c in range(DC):
                last = dve.tensor_scalar(ctxt[:, c, :, NKV:CB],
                                         ctx_mean[:, c, :].rearrange("p (b o) -> p b o", o=1).broadcast_to([P, B, CB - NKV]),
                                         1.0 / NKV, None, ALU.mult)
            last.then_inc(ctxt_ready, 1)

            def pair_lo(f, g, kk, r, use):
                w = wcol[:, f, bass.ds(kk, 1)]
                dve.wait_ge(big_hi, g + 1)
                dve.wait_ge(small_hi, g + 1)
                dve.wait_ge(big_loaded[r], 32 * use)
                dve.wait_ge(small_loaded[r], 32 * use)
                if f == 0:
                    dve.scalar_tensor_tensor(out=big[r][1], in0=big_raw[:, r, :], scalar=w, in1=big[r][0].bitcast(F32),
                                             op0=ALU.mult, op1=ALU.subtract).then_inc(big_lo, 1)
                    lo(dve, small[r][1], A[:, 4 + r, 0:D], small[r][0]).then_inc(small_lo, 1)
                else:
                    bank = (F[:, :, :], A[:, 4:6, :])[r].rearrange("p s n -> p (s n)")
                    for s in range(2):
                        half = slice(512 * s, 512 * s + 512)
                        last = lo(dve, big[r][1][:, half], bank[:, half], big[r][0][:, half])
                    last.then_inc(big_lo, 1)
                    dve.scalar_tensor_tensor(out=small[r][1], in0=small_raw[:, r, :], scalar=w,
                                             in1=small[r][0].bitcast(F32), op0=ALU.mult, op1=ALU.subtract).then_inc(small_lo, 1)

            def composed(dst, src, k):
                dve.wait_ge(comp_hi, k + 1)
                lo(dve, dst(1), src, dst(0)).then_inc(comp_lo, 1)

            dve.wait_ge(top_wcol, 1)
            for f in range(2):
                with dve.Fori(0, PAIRS // 2) as i:
                    for r in range(2):
                        pair_lo(f, PAIRS * f + 2 * i + r, 2 * i + r, r, PAIRS // 2 * f + i + 1)
                if f == 0:
                    for k in range(4):
                        composed(*w1_part(k), k)
                    for p in range(ITEMS):
                        dve.wait_ge(t_bout, p + 1)
                        for t in range(TILES):
                            xs = x[:, TILES * p + t, :]
                            dve.wait_ge(cross_psum, TILES * p + t + 1)
                            dve.tensor_tensor(xs, A[:, t, 0:D], xs, ALU.add).then_inc(cross_added, 1)
                        dve.wait_ge(cross_added, TILES * p + TILES)
                        norm(ITEMS + p, p)
                else:
                    for k in range(4):
                        composed(*w2_part(k), 4 + k)
            for p in range(ITEMS):
                for c in range(DC):
                    dve.wait_ge(f_xt_hi, 2 * p + c + 1)
                    lo(dve, xt[1][:, 1, c, :], A[:, c, :], xt[1][:, 0, c, :]).then_inc(f_xt_lo, 1)
                for m in range(FC):
                    dve.wait_ge(f_gelu, FC * p + m + 1)
                    dve.tensor_copy(ht[:, 0, m, :], hf[:, m % 2, :]).then_inc(f_h_hi, 1)
                if p + 1 < ITEMS:
                    pass
                for t in range(TILES):
                    xs = x[:, TILES * p + t, :]
                    dve.wait_ge(f_y_psum, TILES * p + t + 1)
                    dve.tensor_tensor(xs, A[:, 2 + t, 0:D], xs, ALU.add).then_inc(f_res, 1)
                dve.wait_ge(f_res, TILES * p + TILES)
                norm(2 * ITEMS + p, p)

        def act_xt_hi(act, i, n):
            for c in range(DC):
                act.wait_ge(xt_psum[i], 2 * n + c + 1)
                act.activation(xt[i][:, 0, c, :], xt_bank(i, c), ACT.Copy).then_inc(xt_hi[i], 1)

        def act_q_copy(act, n):
            act.wait_ge(qk_psum, 2 * n + 1)
            act.activation(qf, A[:, 4, :], ACT.Copy)

        def act_qk_hi(act, n):
            for h in range(NH):
                r = slice(E * h, E * h + E)
                last = act.activation(qm[r, 0, h, :], A[r, 4, :], ACT.Copy)
            last.then_inc(q_hi, 1)
            act.wait_ge(qk_psum, 2 * n + 2)
            act.activation(kt[:, 0, :], A[:, 5, :], ACT.Copy).then_inc(k_hi, 1)

        def act_tok(act, n, t):
            act.wait_ge(tok_psum, 4 * n + t + 1)
            ps = A[:, (2, 3, 0, 1)[t], :]
            act.activation(v8[:, t, :, 0:E], ps[:, 0:2 * P].rearrange("p (h e) -> p h e", e=E), ACT.Copy)
            act.activation(qk[:, t, :], ps[:, 2 * P:4 * P], ACT.Copy).then_inc(tok_out, 1)

        def act_features(act, n):
            act.wait_ge(tok_out, 4 * n + 4)
            act.activation(kexp[:, :, :], qk[:, :, P:2 * P], ACT.Exp).then_inc(kexp_done, 1)
            act.wait_ge(qsub_done, n + 1)
            act.activation(qexp[:, :, :], qexp[:, :, :], ACT.Exp).then_inc(qexp_done, 1)

        def act_qnt(act, n):
            act.wait_ge(qnt_psum, n + 1)
            act.activation(qnt[:, :], A[:, 0, :], ACT.Copy).then_inc(qnt_out, 1)

        def act_lin_hi(act, n):
            act.wait_ge(lin_psum, n + 1)
            act.activation(later_buckets(at[:, 0, 1, :]), later_buckets(A[:, 1, :]), ACT.Copy).then_inc(lin_hi, 1)

        def act_exp(act, n, b):
            act.wait_ge(nmax_done, 2 * n + b + 1)
            for h in range(NH):
                for w, (a, z) in enumerate(((0, P), (P, 3 * P))):
                    last = act.activation(prob[:, h, a:z], A[:, 2 + h, a:z], ACT.Exp, bias=smax[:, b, w, h:h + 1],
                                          scale=SCALE)
            last.then_inc(exp_done, 1)

        def act_pt(act, n, b):
            act.wait_ge(pt_psum, 6 * n + 3 * b + 1)
            act.activation(pt[:, 0, :], A[:, 0, :], ACT.Copy).then_inc(pt_out_act, 1)

        def act_al_hi(act, n):
            act.wait_ge(al_psum, n + 1)
            act.activation(at[:, 0, 0, :], A[:, 0, :], ACT.Copy).then_inc(al_hi, 1)

        def act_b1(act, l):
            act.activation(b1_now[:, :], b1c[:, bass.ds(l * FC, FC)], ACT.Copy).then_inc(b1_turn, 1)
            act.wait_ge(b1_turn, l + 1)

        def act_gelu(act, n, m, l):
            act.wait_ge(h_psum, FC * n + m + 1)
            act.wait_ge(h_lo, FC * n + m + 1)
            act.activation(hf[:, m % 2, :], F[:, m % 2, :], ACT.Gelu,
                           bias=b1_now[:, m:m + 1]).then_inc(gelu_done, 1)

        @block.scalar
        def _(act):
            act.wait_ge(const_ready, 1)
            act.wait_ge(zero_ready, 1)
            act_xt_hi(act, 0, 0)
            act_q_copy(act, 0)
            act_qk_hi(act, 0)

            def step(l, p, last, mlp=True):
                n = 4 * l + p + 1
                attn = not (last and p == ITEMS - 1)
                nxt = not (last and p >= ITEMS - 2)

                def gelu(*chunks):
                    for m in chunks if mlp else ():
                        act_gelu(act, n - 1, m, l)

                if attn:
                    for t in range(TILES):
                        act_tok(act, n, t)
                if mlp:
                    act_xt_hi(act, 1, n - 1)
                if attn:
                    act_features(act, n)
                gelu(0, 1, 2)
                if attn:
                    act_qnt(act, n)
                gelu(3, 4, 5, 6, 7)
                if attn:
                    act_lin_hi(act, n)
                    act_exp(act, n, 0)
                    act_pt(act, n, 0)
                    act_exp(act, n, 1)
                if attn:
                    act_pt(act, n, 1)
                if nxt:
                    act_xt_hi(act, 0, n + 1)
                    act_q_copy(act, n + 1)
                if attn:
                    act_al_hi(act, n)
                if nxt:
                    act_qk_hi(act, n + 1)

            step(0, -1, False, mlp=False)
            act.wait_ge(top_step, 2)
            for f in range(2):
                last = act.activation(lexp[:, f:f + 1], lcol[:, f:f + 1], ACT.Exp, bias=lmax[:, f:f + 1])
            last.then_inc(top_exp, 1)
            act.wait_ge(b1_psum, 1)
            act.activation(b1c[:, :], F[:, 0, 0:DEPTH * FC], ACT.Copy).then_inc(b1_ready, 1)
            act.wait_ge(b1_ready, 1)
            act.wait_ge(top_wcol, 1)

            with act.Fori(0, DEPTH - 1) as l:
                act_b1(act, l)
                for p in range(ITEMS):
                    step(l, p, False)
            act_b1(act, DEPTH - 1)
            for p in range(ITEMS):
                step(DEPTH - 1, p, True)

            for k in range(4):
                act.wait_ge(wvt_psum, k + 1)
                act.wait_ge(t_sum, ITEMS)
                act.activation(wvt[:, 2 * k:2 * k + 2, :].rearrange("p j i -> p (j i)"), A[:, k, :], ACT.Copy).then_inc(wvt_out, 1)
            for c in range(DC):
                act.wait_ge(wvo_psum, c + 1)
                act.activation(wvo[:, c, :], A[:, 4 + c, 0:D], ACT.Copy).then_inc(wvo_out, 1)

            def pair_hi(f, g, kk, r, use, peel):
                w = wcol[:, f, bass.ds(kk, 1)]
                act.wait_ge(big_loaded[r], 32 * use)
                act.wait_ge(small_loaded[r], 32 * use)
                if not peel:
                    act.wait_ge(pair_done, g - 1)
                if not peel:
                    act.activation(carrier[:, 1 + r:2 + r], ones[:, :], ACT.Copy)
                if f == 0:
                    act.activation(big[r][0], big_raw[:, r, :], ACT.Copy, scale=w).then_inc(big_hi, 1)
                    act.wait_ge(at_psum, g + 1)
                    act.activation(small[r][0], A[:, 4 + r, 0:D], ACT.Copy).then_inc(small_hi, 1)
                else:
                    act.activation(small[r][0], small_raw[:, r, :], ACT.Copy, scale=w).then_inc(small_hi, 1)
                    act.wait_ge(at_psum, g + 1)
                    for s in range(2):
                        last = act.activation(big[r][0][:, 512 * s:512 * s + 512], (F, A)[r][:, 4 * r + s, :], ACT.Copy)
                    last.then_inc(big_hi, 1)

            act.wait_ge(top_wcol, 1)
            act.wait_ge(y_psum, 16 * DEPTH)
            for r in range(2):
                pair_hi(0, r, r, r, 1, True)
            with act.Fori(1, PAIRS // 2) as i:
                for r in range(2):
                    pair_hi(0, 2 * i + r, 2 * i + r, r, i + 1, False)
            act.wait_ge(pair_done, PAIRS)
            for k in range(4):
                dst, src = w1_part(k)
                act.activation(dst(0), src, ACT.Copy).then_inc(comp_hi, 1)
            with act.Fori(0, PAIRS // 2) as i:
                for r in range(2):
                    pair_hi(1, PAIRS + 2 * i + r, 2 * i + r, r, PAIRS // 2 + i + 1, False)
            act.wait_ge(pair_done, 2 * PAIRS)
            for k in range(4):
                dst, src = w2_part(k)
                act.activation(dst(0), src, ACT.Copy).then_inc(comp_hi, 1)
            for p in range(ITEMS):
                for c in range(DC):
                    act.wait_ge(f_xt_psum, 2 * p + c + 1)
                    act.activation(xt[1][:, 0, c, :], A[:, c, :], ACT.Copy).then_inc(f_xt_hi, 1)
                for m in range(FC):
                    act.wait_ge(f_h_psum, FC * p + m + 1)
                    if FC * p + m >= 2:
                        act.wait_ge(f_h_lo, FC * p + m - 1)
                    act.activation(hf[:, m % 2, :], F[:, m % 2, :], ACT.Gelu_apprx_tanh).then_inc(f_gelu, 1)

        def pe_xt(pe, i, n):
            pe.wait_ge(ln_ready[i], n + 1)
            for c in range(DC):
                for t in range(TILES):
                    last = pe.transpose(xt_bank(i, c)[:, P * t:P * t + P], xh[i][:, t, P * c:P * c + P], ident[:, :])
                last.then_inc(xt_psum[i], 1)

        def product(pe, out, lhs, rhs):
            total = [(c, a, b) for c in range(DC) for a, b in PASSES]
            for k, (c, a, b) in enumerate(total):
                last = pe.matmul(out, lhs(a, c), rhs(b, c), start=k == 0, stop=k == len(total) - 1)
            return last

        def pe_qk(pe, n, l, i):
            if i == 0:
                pe.wait_ge(xt_lo[0], 2 * n + 2)
                pe.wait_ge(wa_ready, l + 1)
            product(pe, A[:, 4 + i, :], lambda a, c: wa[:, a, c, P * i:P * i + P],
                    lambda b, c: xt[0][:, b, c, :]).then_inc(qk_psum, 1)

        def pe_tok(pe, n, t):
            product(pe, A[:, (2, 3, 0, 1)[t], :], lambda a, c: xt[0][:, a, c, P * t:P * t + P],
                    lambda b, c: wa[:, b, c, 2 * P:6 * P]).then_inc(tok_psum, 1)

        def pe_s(pe, n, b):
            pe.wait_ge(k_lo, n + 1)
            pe.wait_ge(q_lo, n + 1)
            if b == 0:
                pe.wait_ge(tok_out, 4 * n + 4)
            else:
                pe.wait_ge(exp_done, 2 * n + 1)
            for h in range(NH):
                pe.matmul(A[:, 2 + h, 0:3 * P], ident_bf[:, :], mask_bf[:, :], start=True, stop=False)
                for w, (c0, c1, t, k1) in enumerate(((0, P, 2 * b, 1), (P, 3 * P, 2 * b + 1, 2))):
                    for k, (i, j) in enumerate(PASSES):
                        last = pe.matmul(A[:, 2 + h, c0:c1], qm[:, i, h, P * t:P * t + P],
                                         kt[:, j, 2 * b * P:(2 * b + k1) * P], start=False, stop=w == 1 and k == 2)
            last.then_inc(s_psum, 1)

        def pe_qnt(pe, n):
            pe.wait_ge(qn_done, n + 1)
            for t in range(TILES):
                last = pe.transpose(A[:, 0, P * t:P * t + P], qexp[:, t, :], ident[:, :])
            last.then_inc(qnt_psum, 1)

        def pe_ctx(pe, n, b):
            pe.wait_ge(kf_done, n + 1)
            if b == 1:
                pe.wait_ge(qnt_out, n + 1)
            w = NH * HB

            def part(j, t, rows, start, stop):
                return pe.matmul(A[:, 1 - b, j * w:(j + 1) * w], kexp[0:rows, t, :],
                                 v8[0:rows, t, NH:2 * NH, :].rearrange("p h e -> p (h e)"), start=start, stop=stop)
            part(0, 2 * b, BUCKET, True, True)
            part(1, 2 * b, P, True, True)
            part(2, 2 * b, P, True, False)
            part(2, 2 * b + 1, BUCKET, False, True).then_inc(ctx_psum, 1)

        def pe_lin(pe, n):
            pe.wait_ge(ctxn_done, 2 * n + 2)
            pe.wait_ge(qnt_out, n + 1)
            for b in range(2):
                for u in range(1, 4):
                    cols = slice(b * T + u * BUCKET, b * T + (u + 1) * BUCKET)
                    last = pe.matmul(A[:, 1, cols], ctxn[:, b, u - 1, :], qnt[:, cols], start=True, stop=True)
            last.then_inc(lin_psum, 1)

        def pe_pt(pe, n, b):
            pe.wait_ge(exp_done, 2 * n + b + 1)
            for r in range(3):
                if r == 0:
                    if b == 0:
                        pe.wait_ge(ctxn_done, 2 * n + 2)
                    else:
                        pe.wait_ge(pt_out_dve, 4 * n + 2)
                if r == 1:
                    if b == 0:
                        pe.wait_ge(lin_lo, n + 1)
                    else:
                        pe.wait_ge(aloc_done, 2 * n + 1)
                if r == 2:
                    pe.wait_ge(pt_out_act, 2 * n + b + 1)
                for h in range(NH):
                    last = pe.transpose(A[:, r % 2, P * h:P * h + P], prob[:, h, P * r:P * r + P], ident[:, :])
                last.then_inc(pt_psum, 1)

        def pe_pv(pe, n, b):
            pe.wait_ge(pt_out_act, 2 * n + b + 1)
            pe.wait_ge(pt_out_dve, 4 * n + 2 * b + 2)
            for w in range(2):
                for h in range(NH):
                    parts = ((0, 0),) if w == 0 else ((1, 0), (2, 1))
                    for k, (r, t) in enumerate(parts):
                        last = pe.matmul(A[:, 1, (NH * w + h) * HB:(NH * w + h + 1) * HB],
                                         pt[:, r, P * h:P * h + P], v8[:, 2 * b + t, h, :],
                                         start=k == 0, stop=k == len(parts) - 1)
            last.then_inc(pv_psum, 1)

        def pe_al(pe, n):
            pe.wait_ge(aloc_done, 2 * n + 2)
            pe.wait_ge(pt_out_dve, 4 * n + 4)
            for t in range(TILES):
                last = pe.transpose(A[:, 0, P * t:P * t + P], aloc[:, t, :], ident[:, :])
            last.then_inc(al_psum, 1)

        def pe_wo(pe, n, l):
            pe.wait_ge(al_lo, n + 1)
            pe.wait_ge(lin_lo, n + 1)
            pe.wait_ge(wo_ready, l + 1)
            pe.wait_ge(exp_done, 2 * n + 2)
            for t in range(TILES):
                product(pe, A[:, (2, 3, 0, 1)[t], 0:D], lambda a, c: at[:, a, c, P * t:P * t + P],
                        lambda b, c: wo[:, b, c, :]).then_inc(wo_psum, 1)

        def pe_h(pe, n, m, l, first=False):
            if m == 0:
                pe.wait_ge(xt_lo[1], 2 * n + 2)
                pe.wait_ge(w1_ready, l + 1)
            if m >= 2:
                pe.wait_ge(gelu_done, FC * n + m - 1)
            product(pe, F[:, m % 2, :], lambda a, c: w1[:, a, c, P * m:P * m + P],
                    lambda b, c: xt[1][:, b, c, :]).then_inc(h_psum, 1)

        def pe_y(pe, n, t, l):
            if t == 0:
                pe.wait_ge(h_lo, H_LO_0 + FC * n + FC)
                pe.wait_ge(w2_ready, l + 1)
            if t < 2:
                pe.wait_ge(gelu_done, FC * n + FC - 1 + t)
            else:
                pe.wait_ge(res2, RES2_0 + 4 * n + t - 1)
            passes = [(c, a, b) for c in range(FC) for a, b in PASSES]
            for k, (c, a, b) in enumerate(passes):
                last = pe.matmul(F[:, t % 2, 0:D], ht[:, a, c, P * t:P * t + P], w2[:, b, c, :],
                                 start=k == 0, stop=k == len(passes) - 1)
            last.then_inc(y_psum, 1)

        @block.tensor
        def _(pe):
            pe.wait_ge(const_ready, 1)
            pe.wait_ge(zero_ready, 1)

            def top_k():
                bank = F[:, 1, :]
                pe.wait_ge(top_step, 5)
                pe.matmul(bank[0:PRIMS, 0:2], ones64[:, 0:PRIMS], lexp[:, :], start=True, stop=True).then_inc(top_sum, 1)
                pe.wait_ge(top_step, 7)
                both = chosen[:, :, :].rearrange("i f k -> i (f k)")
                pe.matmul(bank[0:1, 64:64 + 2 * TOPK], own[:, :], both, start=True, stop=True).then_inc(top_idx, 1)
                pe.wait_ge(top_w, 1)
                pe.wait_ge(index_ready, 1)
                for j in range(2):
                    for f in range(2):
                        last = pe.matmul(bank[:, 128 + 32 * j + 16 * f:144 + 32 * j + 16 * f], lw_wide[:, f, :],
                                         chosen[:, f, :].rearrange("i (k j) -> i j k", j=2)[:, j, :], start=True, stop=True)
                last.then_inc(top_wcol_psum, 1)

            pe_xt(pe, 0, 0)
            for i in range(2):
                pe_qk(pe, 0, 0, i)

            def step(l, p, last, mlp=True):
                n = 4 * l + p + 1
                attn = not (last and p == ITEMS - 1)
                nxt = not (last and p >= ITEMS - 2)
                la = l + 1 if p == ITEMS - 1 else l

                def h(*chunks):
                    for m in chunks if mlp else ():
                        pe_h(pe, n - 1, m, l)

                def y(t):
                    if mlp:
                        pe_y(pe, n - 1, t, l)

                if attn:
                    for t in range(TILES):
                        if mlp:
                            pe.wait_ge(res1, 4 * n + t - 3)
                        pe_tok(pe, n, t)
                if mlp:
                    pe.wait_ge(res2, RES2_0 + 4 * (n - 1))
                    pe_xt(pe, 1, n - 1)
                if attn:
                    pe_s(pe, n, 0)
                h(0, 1, 2)
                if attn:
                    pe_qnt(pe, n)
                h(3)
                if attn:
                    pe_ctx(pe, n, 0)
                h(4, 5)
                if attn:
                    pe_ctx(pe, n, 1)
                h(6, 7)
                if attn:
                    pe_lin(pe, n)
                y(0)
                y(1)
                if attn:
                    pe_pt(pe, n, 0)
                    pe_s(pe, n, 1)
                    pe_pv(pe, n, 0)
                y(2)
                y(3)
                if attn:
                    pe_pt(pe, n, 1)
                if nxt:
                    pe.wait_ge(exp_done, 2 * n + 2)
                    pe_xt(pe, 0, n + 1)
                if attn:
                    pe_pv(pe, n, 1)
                if nxt:
                    pe_qk(pe, n + 1, l + 1 if p >= ITEMS - 2 else l, 0)
                if attn:
                    pe_al(pe, n)
                if nxt:
                    pe_qk(pe, n + 1, l + 1 if p >= ITEMS - 2 else l, 1)
                if attn:
                    pe_wo(pe, n, la)

            step(0, -1, False, mlp=False)
            top_k()
            pe.wait_ge(b1_loaded, 16)
            pe.transpose(F[:, 0, 0:DEPTH * FC], b1_rows[:, :], ident[0:DEPTH * FC, 0:DEPTH * FC]).then_inc(b1_psum, 1)
            pe.wait_ge(b1_ready, 1)
            pe.wait_ge(top_wcol, 1)

            with pe.Fori(0, DEPTH - 1) as l:
                for p in range(ITEMS):
                    step(l, p, False)
            for p in range(ITEMS):
                step(DEPTH - 1, p, True)

            pe.wait_ge(wv_loaded, 16)
            for k in range(4):
                for j in (2 * k, 2 * k + 1):
                    for c in range(DC):
                        last = pe.transpose(A[:, k, (j % 2) * D + P * c:(j % 2) * D + P * c + P],
                                            wv_raw[:, c, P * j:P * j + P], ident[:, :])
                last.then_inc(wvt_psum, 1)
            pe.wait_ge(wvt_out, 4)
            pe.wait_ge(wout_loaded, 16)
            for c in range(DC):
                for j in range(FC):
                    last = pe.matmul(A[:, 4 + c, 0:D], wvt[:, j, P * c:P * c + P], wout_raw[:, j, :],
                                     start=j == 0, stop=j == FC - 1)
                last.then_inc(wvo_psum, 1)
            pe.wait_ge(ctx_loaded, 16)
            for c in range(DC):
                for s in range(2):
                    for b in range(4):
                        last = pe.transpose(A[:, 2 * c + s, P * b:P * b + NKV], ctx_raw[:, 4 * s + b, P * c:P * c + P],
                                            ident[0:NKV, 0:NKV])
                    last.then_inc(ctxt_psum, 1)
            pe.wait_ge(wvo_out, 2)
            pe.wait_ge(ctxt_out, 4)

            def turn(f, g, r, use, peel):
                pe.wait_ge((small_loaded, big_loaded)[f][r], 32 * use)
                if not peel:
                    pe.wait_ge((small_lo, big_lo)[f], g - 1)
                if f == 0:
                    for c in range(DC):
                        last = pe.transpose(A[:, 4 + r, P * c:P * c + P], small_raw[:, r, P * c:P * c + P], ident[:, :])
                else:
                    for m in range(FC):
                        last = pe.transpose((F, A)[r][:, 4 * r + m // 4, P * (m % 4):P * (m % 4) + P],
                                            big_raw[:, r, P * m:P * m + P], ident[:, :])
                last.then_inc(at_psum, 1)

            def multiply(f, g, r, first, final):
                pe.wait_ge(small_lo, g + 1)
                pe.wait_ge(big_lo, g + 1)
                if f == 0:
                    for c in range(DC):
                        for k, (a, b) in enumerate(PASSES):
                            for s in range(2):
                                last = pe.matmul(A[:, 2 * c + s, :], small[r][a][:, P * c:P * c + P],
                                                 big[r][b][:, 512 * s:512 * s + 512], start=first and k == 0,
                                                 stop=final and k == 2, skip_group_check=True)
                else:
                    for m in range(FC):
                        for k, (a, b) in enumerate(PASSES):
                            last = pe.matmul(A[:, m // 2, D * (m % 2):D * (m % 2) + D], big[r][a][:, P * m:P * m + P],
                                             small[r][b], start=first and k == 0 and m % 2 == 0,
                                             stop=final and k == 2, skip_group_check=True)
                last.then_inc(pair_done, 1)

            def compose(f):
                h = PAIRS // 2
                base = PAIRS * f
                turn(f, base, 0, h * f + 1, f == 0)
                turn(f, base + 1, 1, h * f + 1, f == 0)
                multiply(f, base, 0, True, False)
                turn(f, base + 2, 0, h * f + 2, False)
                multiply(f, base + 1, 1, False, False)
                with pe.Fori(1, h - 1) as i:
                    turn(f, base + 2 * i + 1, 1, h * f + i + 1, False)
                    multiply(f, base + 2 * i, 0, False, False)
                    turn(f, base + 2 * i + 2, 0, h * f + i + 2, False)
                    multiply(f, base + 2 * i + 1, 1, False, False)
                turn(f, base + 2 * h - 1, 1, h * f + h, False)
                multiply(f, base + 2 * h - 2, 0, False, False)
                multiply(f, base + 2 * h - 1, 1, False, True)

            compose(0)
            pe.wait_ge(comp_lo, 4)
            pe.wait_ge(ctxt_ready, 1)
            for p in range(ITEMS):
                for t in range(TILES):
                    if p:
                        pe.wait_ge(cross_added, TILES * (p - 1) + t + 1)
                    for c in range(DC):
                        b = 2 * p + t // 2
                        rows = ctxt[:, c, b, :] if t % 2 == 0 else ctxt[:, c, b, NKV:NKV + 1].broadcast_to([P, P])
                        last = pe.matmul(A[:, t, 0:D], rows, wvo[:, c, :], start=c == 0, stop=c == DC - 1)
                    last.then_inc(cross_psum, 1)
            pe.wait_ge(cross_added, TILES * ITEMS)
            compose(1)
            pe.wait_ge(comp_lo, 8)

            def f_xt(p):
                pe.wait_ge(t_norm, ITEMS + p + 1)
                if p:
                    pe.wait_ge(f_xt_lo, 2 * p)
                for c in range(DC):
                    for t in range(TILES):
                        last = pe.transpose(A[:, c, P * t:P * t + P], x[:, TILES * p + t, P * c:P * c + P], ident[:, :])
                    last.then_inc(f_xt_psum, 1)

            f_xt(0)
            for p in range(ITEMS):
                pe.wait_ge(f_xt_lo, 2 * p + 2)
                for m in range(FC):
                    if FC * p + m >= 2:
                        pe.wait_ge(f_gelu, FC * p + m - 1)
                    product(pe, F[:, m % 2, :], lambda a, c: w1[:, a, c, P * m:P * m + P],
                            lambda b, c: xt[1][:, b, c, :]).then_inc(f_h_psum, 1)
                if p + 1 < ITEMS:
                    f_xt(p + 1)
                pe.wait_ge(f_h_lo, FC * p + FC)
                for t in range(TILES):
                    if p:
                        pe.wait_ge(f_res, TILES * (p - 1) + t + 1)
                    passes = [(c, a, b) for c in range(FC) for a, b in PASSES]
                    for k, (c, a, b) in enumerate(passes):
                        last = pe.matmul(A[:, 2 + t, 0:D], ht[:, a, c, P * t:P * t + P], w2[:, b, c, :],
                                         start=k == 0, stop=k == len(passes) - 1)
                    last.then_inc(f_y_psum, 1)


_INS = ['x', 'L0_attn_Wq', 'L0_attn_Wk', 'L0_attn_Wv', 'L0_attn_Wo', 'L0_attn_bo', 'L0_attn_ln1_g', 'L0_attn_ln1_b',
        'L0_attn_W1', 'L0_attn_b1', 'L0_attn_W2', 'L0_attn_b2', 'L0_attn_ln2_g', 'L0_attn_ln2_b',
        'ctx_1024', 'L0_xattn_Wkv', 'L0_xattn_Wout', 'L0_xattn_bout', 'L0_ffn_fc1_A', 'L0_ffn_fc1_B', 'L0_ffn_fc2_A',
        'L0_ffn_fc2_B', 'L0_ffn_fc1_logits', 'L0_ffn_fc2_logits']
_OUTS = [((8, 256, 256), 'float32')]


def kernel(**inputs):
    import numpy as _np
    import concourse.bacc as _bacc
    from concourse import mybir as _mybir
    from concourse.bass_utils import run_bass_kernel_spmd as _run

    nc = _bacc.Bacc("TRN2", target_bir_lowering=False, num_devices=1)
    arrays, args = {}, []
    for name in _INS:
        a = _np.ascontiguousarray(inputs[name])
        arrays[f"in_{name}_dram"] = a
        args.append(nc.dram_tensor(f"in_{name}_dram", a.shape, _mybir.dt.from_np(a.dtype), kind="ExternalInput").ap())
    for i, (shape, dtype) in enumerate(_OUTS):
        dt = _mybir.dt.from_np(_np.dtype(dtype))
        args.append(nc.dram_tensor(f"out_{i}_dram", shape, dt, kind="ExternalOutput").ap())
    build(nc, *args)
    r = _run(nc, [arrays], core_ids=[0])
    got = tuple(r.results[0][f"out_{i}_dram"] for i in range(len(_OUTS)))
    return got[0]
```

```python
from contextlib import ExitStack

import concourse.bass as bass
from concourse import mybir

F32 = mybir.dt.float32
F32R = mybir.dt.float32r
BF16 = mybir.dt.bfloat16
I32 = mybir.dt.int32
ALU = mybir.AluOpType
ACT = mybir.ActivationFunctionType
AX_X = mybir.AxisListType.X

P = 128
B, T, D = 8, 256, 256
DC = D // P
DEPTH = 4
FF = 4 * D
FC = FF // P
E = 32
NH = 4
BUCKET = 64
TILES = 4
TOK = TILES * P
ITEMS = B * T // TOK
HB = E + 1
SCALE = float(E) ** -0.5
MASKED = -1.0e30
EPS = 1.0e-5
NKV = 120
CB = 128
PRIMS, TOPK, RANK = 64, 32, 64
PAIRS = TOPK // 2
PASSES = ((0, 0), (1, 0), (0, 1))


def build(nc, x_in, Wq, Wk, Wv, Wo, bo, ln1_g, ln1_b, W1, b1, W2, b2, ln2_g, ln2_b,
          ctx_in, Wkv, Wout, bout, fc1_A, fc1_B, fc2_A, fc2_B, fc1_logits, fc2_logits, out):
    with ExitStack() as ctx:
        def sb(name, shape, dt=F32):
            return ctx.enter_context(nc.sbuf_tensor(name, shape, dt))

        def sem(name):
            return ctx.enter_context(nc.semaphore(name))

        x = sb("x", [P, ITEMS * TILES, D])
        wa = sb("wa", [P, 2, DC, 768], F32R)
        wo = sb("wo", [P, 2, DC, D], F32R)
        w1 = sb("w1", [P, 2, DC, FF], F32R)
        w2 = sb("w2", [P, 2, FC, D], F32R)
        raw_a = sb("raw_a", [P, DC, 1024])
        raw_f = sb("raw_f", [P, 2048])
        vec_a = sb("vec_a", [P, 3, D])
        vec_f = sb("vec_f", [P, 3, D])
        b1c = sb("b1c", [P, DEPTH * FC])
        b1_now = sb("b1_now", [P, FC])
        carrier = sb("carrier", [P, 3])
        b1_rows = sb("b1_rows", [DEPTH * FC, P])
        slot_mark = sb("slot_mark", [P, 2])
        loaded_mark = sb("loaded_mark", [P, ITEMS * TILES])
        ident = sb("ident", [P, P])
        ident_bf = sb("ident_bf", [P, P], BF16)
        mask_bf = sb("mask_bf", [P, 3 * P], BF16)
        headmask = sb("headmask", [P, NH, E])
        ones = sb("ones", [P, 1])
        minus_half = sb("minus_half", [P, 4])
        xt = [sb("xt1", [P, 2, DC, TOK], F32R), sb("xt2", [P, 2, DC, TOK], F32R)]
        ht = sb("ht", [P, 2, FC, TOK], F32R)
        scratch = sb("scratch", [P, 9760])
        v8 = scratch[:, 0:1056].rearrange("p (t h e) -> p t h e", t=TILES, h=2 * NH)
        qk = scratch[:, 1056:2080].rearrange("p (t d) -> p t d", t=TILES)
        qexp = scratch[:, 2080:2592].rearrange("p (t d) -> p t d", t=TILES)
        qf = scratch[:, 2080:2592]
        kexp = scratch[:, 2592:3104].rearrange("p (t d) -> p t d", t=TILES)
        qnt = scratch[:, 3104:3616]
        prob = scratch[:, 3616:5152].rearrange("p (h k) -> p h k", h=NH)
        pt = scratch[:, 5152:6688].rearrange("p (r k) -> p r k", r=3)
        xh = [scratch[:, a:a + 1024].rearrange("p (t d) -> p t d", t=TILES) for a in (6688, 7712)]
        hf = scratch[:, 8736:9760].rearrange("p (s t) -> p s t", s=2)
        x0 = scratch[:, 0:4096].rearrange("p (t d) -> p t d", d=D)
        ctx_raw = scratch[0:NKV, 0:2048].rearrange("p (b n) -> p b n", b=B)
        wvt = scratch[:, 2048:4096].rearrange("p (j i) -> p j i", j=FC)
        wout_raw = raw_a[:, :, :].rearrange("p c n -> p (c n)").rearrange("p (j n) -> p j n", j=FC)
        ctxt = raw_a[:, :, :].rearrange("p c (b t) -> p c b t", b=B)
        wv_raw = raw_f[:, :].rearrange("p (c n) -> p c n", c=DC)
        big_raw = scratch[:, 4096:8192].rearrange("p (r n) -> p r n", r=4)
        small_raw = raw_f[:, 1024:2048].rearrange("p (r n) -> p r n", r=4)
        ctx_mean = sb("ctx_mean", [P, DC, B])
        tstats, tmv = sb("tstats", [P, TILES, 6]), sb("tmv", [P, TILES, 2])
        tvar, trstd = sb("tvar", [P, TILES]), sb("trstd", [P, TILES])
        top = scratch[0:PRIMS, 8736:9760]
        lrow, tie, beats = (top[:, P * i:P * i + P].rearrange("p (f n) -> p f n", f=2) for i in range(3))
        lw_wide = top[:, 384:640].rearrange("p (f n) -> p f n", f=2)
        ones64, earlier = top[:, 640:768], top[:, 768:832]
        chosen = top[:, 832:896].rearrange("p (f n) -> p f n", f=2)
        lcol, lmax, lexp, rank, lsum, lw = (sb(n, [PRIMS, 2]) for n in ("lcol", "lmax", "lexp", "rank", "lsum", "lw"))
        places_i, places = sb("places_i", [PRIMS, TOPK], I32), sb("places", [PRIMS, TOPK])
        own_i, own = sb("own_i", [PRIMS, 1], I32), sb("own", [PRIMS, 1])
        index = sb("index", [1, 2 * TOPK], I32)
        wcol = sb("wcol", [P, 2, PAIRS])
        stats = [sb("stats1", [P, TILES, 6]), sb("stats2", [P, TILES, 6])]
        mv = [sb("mv1", [P, TILES, 2]), sb("mv2", [P, TILES, 2])]
        var = [sb("var1", [P, TILES]), sb("var2", [P, TILES])]
        rstd = [sb("rstd1", [P, TILES]), sb("rstd2", [P, TILES])]
        qm = sb("qm", [P, 2, NH, TOK], F32R)
        kt = sb("kt", [P, 2, TOK], F32R)
        qmax = sb("qmax", [P, TILES, NH])
        qsum = sb("qsum", [P, TILES, NH])
        kcum = sb("kcum", [P, 2, 3])
        ctxn = sb("ctxn", [P, 2, 3, P])
        wvo = ctxn[:, :, :, :].rearrange("p b t n -> p (b t n)")[:, 0:512].rearrange("p (c n) -> p c n", c=DC)
        smax = sb("smax", [P, 2, 2, NH])
        psum_r = sb("psum_r", [P, 8])
        aloc = qnt.rearrange("p (t d) -> p t d", t=TILES)
        at = sb("at", [P, 2, DC, TOK], F32R)
        big = [[buf[:, i, :, :].rearrange("p c n -> p (c n)") for i in range(2)] for buf in (at, xt[0])]
        small = [[kt[:, i, D * r:D * r + D] for i in range(2)] for r in range(2)]
        wa_flat = wa[:, :, :, :].rearrange("p i c n -> p (i c n)")

        def f_ht(p, i, m):
            if p % 2 == 0:
                return ht[:, i, m, :]
            if i == 0:
                return qm[:, m // NH, m % NH, :]
            return at[:, m // 2, m % 2, :] if m < 4 else wa_flat[:, TOK * (m - 4):TOK * (m - 3)]
        A = ctx.enter_context(nc.psum_tensor("A", [P, 6, 512], F32))
        F = ctx.enter_context(nc.psum_tensor("F", [P, 2, 512], F32))

        x_loaded = [sem(f"x_loaded{p}") for p in range(ITEMS)]
        raw_a_loaded, raw_w1_loaded, raw_w2_loaded = sem("raw_a_loaded"), sem("raw_w1_loaded"), sem("raw_w2_loaded")
        vec_a_loaded, vec_f_loaded, b1_loaded = sem("vec_a_loaded"), sem("vec_f_loaded"), sem("b1_loaded")
        const_step, const_ready, zero_ready = sem("const_step"), sem("const_ready"), sem("zero_ready")
        wa_hi, wa_ready, wo_hi, wo_ready = sem("wa_hi"), sem("wa_ready"), sem("wo_hi"), sem("wo_ready")
        w1_hi, w1_ready, w2_hi, w2_ready = sem("w1_hi"), sem("w1_ready"), sem("w2_hi"), sem("w2_ready")
        ln_stats = [sem("ln1_stats"), sem("ln2_stats")]
        ln_mv = [sem("ln1_mv"), sem("ln2_mv")]
        ln_var = [sem("ln1_var"), sem("ln2_var")]
        ln_rstd = [sem("ln1_rstd"), sem("ln2_rstd")]
        ln_xhat = [sem("ln1_xhat"), sem("ln2_xhat")]
        ln_ready = [sem("ln1_ready"), sem("ln2_ready")]
        biased = [sem("bo_added"), sem("b2_added")]
        xt_psum = [sem("xt1_psum"), sem("xt2_psum")]
        xt_hi = [sem("xt1_hi"), sem("xt2_hi")]
        xt_lo = [sem("xt1_lo"), sem("xt2_lo")]
        qk_psum, q_hi, k_hi, q_lo, k_lo = sem("qk_psum"), sem("q_hi"), sem("k_hi"), sem("q_lo"), sem("k_lo")
        tok_psum, tok_out = sem("tok_psum"), sem("tok_out")
        qmax_done, qsub_done, qexp_done, kexp_done = sem("qmax_done"), sem("qsub_done"), sem("qexp_done"), sem("kexp_done")
        qsum_done, qrec_done, qn_done, krelu_done, kf_done = (
            sem("qsum_done"), sem("qrec_done"), sem("qn_done"), sem("krelu_done"), sem("kf_done"))
        qnt_psum, qnt_out, ctx_psum, kcum_done, krec_done, ctxn_done, lin_psum, lin_hi, lin_lo = (
            sem("qnt_psum"), sem("qnt_out"), sem("ctx_psum"), sem("kcum_done"), sem("krec_done"),
            sem("ctxn_done"), sem("lin_psum"), sem("lin_hi"), sem("lin_lo"))
        s_psum, smax_done, nmax_done, exp_done = sem("s_psum"), sem("smax_done"), sem("nmax_done"), sem("exp_done")
        pt_psum, pt_out_act, pt_out_dve, pv_psum, prec_done, aloc_done = (
            sem("pt_psum"), sem("pt_out_act"), sem("pt_out_dve"), sem("pv_psum"), sem("prec_done"), sem("aloc_done"))
        al_psum, al_hi, al_lo, wo_psum, res1 = sem("al_psum"), sem("al_hi"), sem("al_lo"), sem("wo_psum"), sem("res1")
        h_psum, gelu_done, h_hi, h_lo, y_psum, res2 = (
            sem("h_psum"), sem("gelu_done"), sem("h_hi"), sem("h_lo"), sem("y_psum"), sem("res2"))
        top_wcol_psum = sem("top_wcol_psum")
        b1_turn = sem("b1_turn")
        stored, b1_psum, b1_ready = sem("stored"), sem("b1_psum"), sem("b1_ready")
        logits_loaded, top_const, top_step, top_exp, top_sum, top_w, top_idx, top_wcol, index_ready = (
            sem(n) for n in ("logits_loaded", "top_const", "top_step", "top_exp", "top_sum", "top_w", "top_idx",
                             "top_wcol", "index_ready"))
        x0_loaded, wv_loaded, wout_loaded, ctx_loaded, bout_loaded = (
            sem(n) for n in ("x0_loaded", "wv_loaded", "wout_loaded", "ctx_loaded", "bout_loaded"))
        big_loaded = [sem(f"big_loaded{r}") for r in range(4)]
        small_loaded = [sem(f"small_loaded{r}") for r in range(4)]
        t_sum, t_stats, t_mv, t_var, t_rstd, t_norm, t_bout = (
            sem(n) for n in ("t_sum", "t_stats", "t_mv", "t_var", "t_rstd", "t_norm", "t_bout"))
        wvt_psum, wvt_out, wvo_psum, wvo_out, ctxt_psum, ctxt_out, ctx_sum, ctxt_ready, cross_psum, cross_added = (
            sem(n) for n in ("wvt_psum", "wvt_out", "wvo_psum", "wvo_out", "ctxt_psum", "ctxt_out", "ctx_sum",
                             "ctxt_ready", "cross_psum", "cross_added"))
        at_psum, big_hi, big_lo, small_hi, small_lo, pair_done, comp_hi, comp_lo = (
            sem(n) for n in ("at_psum", "big_hi", "big_lo", "small_hi", "small_lo", "pair_done", "comp_hi", "comp_lo"))
        f_xt_psum, f_xt_hi, f_xt_lo, f_h_psum, f_gelu, f_h_hi, f_h_lo, f_y_psum, f_res = (
            sem(n) for n in ("f_xt_psum", "f_xt_hi", "f_xt_lo", "f_h_psum", "f_gelu", "f_h_hi", "f_h_lo", "f_y_psum",
                             "f_res"))
        H_LO_0 = 2
        RES2_0 = 4 * ITEMS

        def slot(p):
            return slice(TILES * p, TILES * p + TILES)

        def w1_part(k):
            c, s = k // 2, k % 2

            def dst(i):
                return w1[:, i, c, :].rearrange("q (m p) -> q p m", p=P)[:, 64 * s:64 * s + 64, :]
            return dst, A[:, k, :].rearrange("q (p m) -> q p m", m=FC)

        WVT_BANKS = (4, 5, 2, 3)
        CROSS_BANKS = (4, 5, 0, 1, 2, 3, 4, 5)

        def f_xt_bank(p, c):
            return (A[:, 4 + c, :] if p else F[:, c, :])

        def w2_part(k):
            def dst(i):
                return w2[:, i, 2 * k:2 * k + 2, :].rearrange("p m n -> p (m n)")
            return dst, A[:, k, :]


        def load_a(sp, l, first=False):
            if not first:
                sp.wait_ge(wo_ready, l)
            for i, (w, lo, hi, at_col) in enumerate((
                    (Wq, 0, P, 0), (Wk, 0, P, P), (Wv, 0, D, 2 * P), (Wq, P, D, 4 * P), (Wk, P, D, 5 * P),
                    (Wo, 0, D, 6 * P))):
                src = w[bass.ds(l, 1)].rearrange("a (c p) n -> p (a c) n", p=P)[:, :, lo:hi]
                sp.dma_start(raw_a[:, :, at_col:at_col + hi - lo], src).then_inc(raw_a_loaded, 16)

        def load_w1(sp, l, first=False):
            if not first:
                sp.wait_ge(w2_ready, l)
            sp.dma_start(raw_f[:, :].rearrange("p (c n) -> p c n", c=DC),
                         W1[bass.ds(l, 1)].rearrange("a (c p) n -> p (a c) n", p=P)).then_inc(raw_w1_loaded, 16)

        def load_w2(sp, l):
            sp.wait_ge(w1_ready, l + 1)
            sp.dma_start(raw_f[:, :].rearrange("p (c n) -> p c n", c=FC),
                         W2[bass.ds(l, 1)].rearrange("a (c p) n -> p (a c) n", p=P)).then_inc(raw_w2_loaded, 16)

        def load_vec(sp, l, which, n=None):
            dst, src, loaded = ((vec_a, (ln1_g, ln1_b, bo), vec_a_loaded), (vec_f, (ln2_g, ln2_b, b2), vec_f_loaded))[which]
            if n is not None:
                sp.wait_ge(biased[which], n + 1)
                sp.wait_ge(ln_ready[which], n + 1)
            for i, s in enumerate(src):
                row = s[bass.ds(l, 1)]
                sp.dma_start(dst[:, i, :], row.broadcast_to([P, D])).then_inc(loaded, 16)

        block = ctx.enter_context(nc.Block())

        @block.sync
        def _(sp):
            sp.dma_start(x[:, slot(0), :], x_in[0:2].rearrange("b (s p) d -> p (b s) d", p=P)).then_inc(x_loaded[0], 16)
            load_vec(sp, 0, 0)
            load_a(sp, 0, first=True)
            for p in range(1, ITEMS):
                sp.dma_start(x[:, slot(p), :],
                             x_in[2 * p:2 * p + 2].rearrange("b (s p) d -> p (b s) d", p=P)).then_inc(x_loaded[p], 16)
            sp.dma_start(b1_rows[:, :], b1.rearrange("l (m p) -> (l m) p", p=P)).then_inc(b1_loaded, 16)
            for f, lg in enumerate((fc1_logits, fc2_logits)):
                sp.dma_start(lrow[:, f, :], lg.rearrange("(a n) -> a n", a=1).broadcast_to([PRIMS, PRIMS])).then_inc(logits_loaded, 16)
                sp.dma_start(lcol[:, f:f + 1], lg.rearrange("(p o) -> p o", o=1)).then_inc(logits_loaded, 16)
            load_w1(sp, 0, first=True)
            load_vec(sp, 0, 1)
            load_w2(sp, 0)
            with sp.Fori(0, DEPTH - 1) as l:
                load_a(sp, l + 1)
                load_w1(sp, l + 1)
                load_vec(sp, l + 1, 0, 4 * l + 3)
                load_vec(sp, l + 1, 1, 4 * l + 3)
                load_w2(sp, l + 1)
            sp.wait_ge(wo_ready, DEPTH)
            sp.dma_start(wout_raw, Wout.rearrange("(j p) n -> p j n", p=P)).then_inc(wout_loaded, 16)
            sp.wait_ge(biased[0], 4 * DEPTH)
            sp.wait_ge(ln_ready[0], 4 * DEPTH)
            sp.dma_start(vec_a[:, 0, :], bout.rearrange("(a n) -> a n", a=1).broadcast_to([P, D])).then_inc(bout_loaded, 16)
            sp.wait_ge(w2_ready, DEPTH)
            sp.dma_start(wv_raw, Wkv.rearrange("(c p) n -> p c n", p=P)[:, :, 1024:2048]).then_inc(wv_loaded, 16)
            sp.wait_ge(wo_psum, 16 * DEPTH)
            sp.dma_start(ctx_raw, ctx_in.rearrange("b t d -> t b d")).then_inc(ctx_loaded, 16)
            sp.wait_ge(wvt_psum, 4)
            sp.wait_ge(index_ready, 1)

            def load_pair(f, g, kk, r, peel):
                if not peel:
                    sp.wait_ge(big_lo, g - 3)
                    sp.wait_ge(small_lo, g - 3)
                for j in range(2):
                    k = sp.value_load(index[0:1, bass.ds(f * TOPK + 2 * kk + j, 1)], min_val=0, max_val=PRIMS - 1)
                    rows = slice(RANK * j, RANK * j + RANK)
                    if f == 0:
                        sp.dma_start(small_raw[:, r, :].rearrange("p (c n) -> p c n", c=DC)[:, :, rows],
                                     fc1_A[bass.ds(k, 1)].rearrange("a (c p) r -> p (a c) r", p=P)).then_inc(small_loaded[r], 16)
                        sp.dma_start(big_raw[rows, r, :],
                                     fc1_B[bass.ds(k, 1)].rearrange("a r n -> (a r) n")).then_inc(big_loaded[r], 16)
                    else:
                        sp.dma_start(big_raw[:, r, :].rearrange("p (m n) -> p m n", m=FC)[:, :, rows],
                                     fc2_A[bass.ds(k, 1)].rearrange("a (p m) r -> p (a m) r", p=P)).then_inc(big_loaded[r], 16)
                        sp.dma_start(small_raw[rows, r, :],
                                     fc2_B[bass.ds(k, 1)].rearrange("a r n -> (a r) n")).then_inc(small_loaded[r], 16)

            for r in range(4):
                if r == 2:
                    sp.wait_ge(xt_psum[1], 8 * DEPTH)
                load_pair(0, r, r, r, True)
            sp.wait_ge(wvo_psum, 2)
            sp.wait_ge(ctxt_psum, 4)
            sp.dma_start(x0, x_in.rearrange("b (s p) d -> p (b s) d", p=P)).then_inc(x0_loaded, 16)
            with sp.Fori(1, PAIRS // 4) as i:
                for r in range(4):
                    load_pair(0, 4 * i + r, 4 * i + r, r, False)
            with sp.Fori(0, PAIRS // 4) as i:
                for r in range(4):
                    load_pair(1, PAIRS + 4 * i + r, 4 * i + r, r, False)
            for p in range(ITEMS - 1):
                sp.wait_ge(t_norm, 2 * ITEMS + p + 1)
                sp.dma_start(out[2 * p:2 * p + 2].rearrange("b (s p) d -> p (b s) d", p=P), x[:, slot(p), :]).then_inc(stored, 16)
            for b in range(2):
                sp.wait_ge(t_norm, 3 * ITEMS + b)
                t = TILES * (ITEMS - 1) + 2 * b
                sp.dma_start(out[B - 2 + b].rearrange("(s p) d -> p s d", p=P), x[:, t:t + 2, :]).then_inc(stored, 16)
            sp.wait_ge(stored, 16 * (ITEMS + 1))

        def split(pool, dst, src, hi_sem, ready, l):
            one = ones[:, :].broadcast_to([P, 2048]) if len(src.shape) == 2 else ones[:, :].rearrange(
                "p (a o) -> p a o", a=1).broadcast_to(list(src.shape))
            pool.tensor_tensor(dst[0], src, one, ALU.mult).then_inc(hi_sem, 1)
            pool.wait_ge(hi_sem, l + 1)
            pool.tensor_tensor(dst[1], src, dst[0].bitcast(F32), ALU.subtract).then_inc(ready, 1)

        def split_wa(pool, l, n=None):
            pool.wait_ge(raw_a_loaded, 96 * (l + 1))
            if n is not None:
                pool.wait_ge(tok_psum, 4 * n + 4)
            split(pool, [wa[:, i] for i in range(2)], raw_a[:, :, 0:768], wa_hi, wa_ready, l)

        def split_wo(pool, l, n=None):
            pool.wait_ge(raw_a_loaded, 96 * (l + 1))
            if n is not None:
                pool.wait_ge(wo_psum, 4 * n + 4)
            split(pool, [wo[:, i] for i in range(2)], raw_a[:, :, 768:1024], wo_hi, wo_ready, l)

        def split_w1(pool, l, n=None):
            pool.wait_ge(raw_w1_loaded, 16 * (l + 1))
            if n is not None:
                pool.wait_ge(h_psum, FC * n + FC)
            split(pool, [w1[:, i].rearrange("p c n -> p (c n)") for i in range(2)], raw_f[:, :], w1_hi, w1_ready, l)

        def split_w2(pool, l, n=None):
            pool.wait_ge(raw_w2_loaded, 16 * (l + 1))
            if n is not None:
                pool.wait_ge(y_psum, 4 * n + 4)
            split(pool, [w2[:, i].rearrange("p c n -> p (c n)") for i in range(2)], raw_f[:, :], w2_hi, w2_ready, l)

        def pool_rstd(pool, i, n):
            pool.wait_ge(ln_var[i], n + 1)
            pool.tensor_tensor(rstd[i][:, :], var[i][:, :], minus_half[:, :], ALU.pow).then_inc(ln_rstd[i], 1)

        def pool_bias(pool, i, n, p):
            vec = (vec_a, vec_f)[i]
            pool.wait_ge(ln_ready[i], n + 1)
            pool.tensor_tensor(x[:, slot(p), :], x[:, slot(p), :], vec[:, 2:3, :].broadcast_to([P, TILES, D]),
                               ALU.add).then_inc(biased[i], 1)

        def pool_q_lo(pool, n):
            pool.wait_ge(q_hi, n + 1)
            for h in range(NH):
                r = slice(E * h, E * h + E)
                last = pool.tensor_tensor(qm[r, 1, h, :], qf[r, :], qm[r, 0, h, :].bitcast(F32), ALU.subtract)
            last.then_inc(q_lo, 1)
            pool.wait_ge(q_lo, n + 1)

        def pool_h_lo(pool, n, m):
            pool.wait_ge(h_hi, FC * n + m + 1)
            pool.tensor_tensor(ht[:, 1, m, :], hf[:, m % 2, :], ht[:, 0, m, :].bitcast(F32),
                               ALU.subtract).then_inc(h_lo, 1)

        @block.gpsimd
        def _(pool):
            pool.memset(ones[:, :], 1.0).then_inc(const_step, 1)
            pool.memset(minus_half[:, :], -0.5).then_inc(const_step, 1)
            pool.memset(ident[:, :], 0.0).then_inc(const_step, 1)
            pool.memset(ident_bf[:, :], 0.0).then_inc(const_step, 1)
            pool.memset(mask_bf[:, :], 0.0).then_inc(const_step, 1)
            pool.memset(headmask[:, :, :], 1.0).then_inc(const_step, 1)
            pool.memset(v8[:, :, :, :], 1.0).then_inc(const_step, 1)
            for i in range(H_LO_0):
                pool.memset(slot_mark[:, i:i + 1], 0.0).then_inc(h_lo, 1)
            pool.wait_ge(const_step, 7)
            for m in (ident, ident_bf):
                pool.affine_select(out=m[:, :], in_=m[:, :], compare_op=ALU.not_equal, fill=1.0, base=0,
                                   pattern=[[-1, P]], channel_multiplier=1).then_inc(const_step, 1)
            for col in (0, 2 * P):
                m = mask_bf[:, col:col + P]
                pool.affine_select(out=m, in_=m, compare_op=ALU.is_ge, fill=MASKED, base=0,
                                   pattern=[[-1, P]], channel_multiplier=1).then_inc(const_step, 1)
            pool.affine_select(out=headmask[:, :, :], in_=headmask[:, :, :], compare_op=ALU.is_ge, fill=0.0, base=0,
                               pattern=[[-E, NH], [0, E]], channel_multiplier=1).then_inc(const_step, 1)
            pool.wait_ge(const_step, 12)
            pool.affine_select(out=headmask[:, :, :], in_=headmask[:, :, :], compare_op=ALU.is_ge, fill=0.0, base=E - 1,
                               pattern=[[E, NH], [0, E]], channel_multiplier=-1).then_inc(const_ready, 1)
            pool.wait_ge(const_ready, 1)
            pool_rstd(pool, 0, 0)
            pool.iota(places_i[:, :], pattern=[[1, TOPK]], base=0, channel_multiplier=0).then_inc(top_const, 1)
            pool.iota(own_i[:, :], pattern=[[0, 1]], base=0, channel_multiplier=1).then_inc(top_const, 1)
            pool.memset(ones64[:, :], 1.0).then_inc(top_const, 1)
            pool.memset(earlier[:, :], 1.0).then_inc(top_const, 1)
            pool.wait_ge(top_const, 4)
            pool.affine_select(out=earlier[:, :], in_=earlier[:, :], compare_op=ALU.is_gt, fill=0.0, base=0,
                               pattern=[[-1, PRIMS]], channel_multiplier=1).then_inc(top_const, 1)
            split_wa(pool, 0)
            pool.wait_ge(zero_ready, 1)
            pool.wait_ge(top_const, 5)
            pool.wait_ge(wa_ready, 1)
            pool_q_lo(pool, 0)
            pool_bias(pool, 0, 0, 0)
            split_wo(pool, 0)
            split_w1(pool, 0)

            def step(l, p, last, mlp=True):
                n = 4 * l + p + 1
                attn = not (last and p == ITEMS - 1)
                nxt = not (last and p >= ITEMS - 2)
                if mlp:
                    pool_bias(pool, 1, n - 1, p)
                    for m in range(FC):
                        pool_h_lo(pool, n - 1, m)
                if p == ITEMS - 2 and not last:
                    split_wa(pool, l + 1, n)
                if nxt:
                    pool_rstd(pool, 0, n + 1)
                    pool_bias(pool, 0, n + 1, (p + 2) % ITEMS)
                if p == ITEMS - 1 and not last:
                    split_wo(pool, l + 1, n - 1)
                    split_w1(pool, l + 1, n - 1)
                if not mlp:
                    split_w2(pool, 0)
                if nxt:
                    pool.wait_ge(biased[0], n + 2)
                    if p == ITEMS - 1 and not last:
                        pool.wait_ge(w1_ready, l + 2)
                    if not mlp:
                        pool.wait_ge(w2_ready, 1)
                    pool_q_lo(pool, n + 1)
                if attn:
                    pool_rstd(pool, 1, n)
                if p == ITEMS - 1 and not last:
                    split_w2(pool, l + 1, n - 1)

            step(0, -1, False, mlp=False)
            with pool.Fori(0, DEPTH - 1) as l:
                for p in range(ITEMS):
                    step(l, p, False)
            for p in range(ITEMS):
                step(DEPTH - 1, p, True)

            def inverse_std(q, tiles=slice(0, TILES)):
                n = tiles.stop - tiles.start
                pool.wait_ge(t_var, q + 1)
                pool.tensor_tensor(trstd[:, tiles], tvar[:, tiles], minus_half[:, 0:n], ALU.pow).then_inc(t_rstd, 1)

            pool.wait_ge(x0_loaded, 16)
            for p in range(ITEMS):
                pool.wait_ge(res2, RES2_0 + 16 * (DEPTH - 1) + 4 * (p + 1))
                pool.tensor_tensor(x[:, slot(p), :], x[:, slot(p), :], x0[:, slot(p), :], ALU.add).then_inc(t_sum, 1)
            pool.wait_ge(bout_loaded, 16)
            for p in range(ITEMS):
                inverse_std(p)
                pool.wait_ge(t_norm, p + 1)
                pool.tensor_tensor(x[:, slot(p), :], x[:, slot(p), :],
                                   vec_a[:, 0:1, :].broadcast_to([P, TILES, D]), ALU.add).then_inc(t_bout, 1)
            for p in range(ITEMS):
                inverse_std(ITEMS + p)
            for p in range(ITEMS):
                for m in range(FC):
                    pool.wait_ge(f_h_hi, FC * p + m + 1)
                    pool.tensor_tensor(f_ht(p, 1, m), hf[:, m % 2, :], f_ht(p, 0, m).bitcast(F32),
                                       ALU.subtract).then_inc(f_h_lo, 1)
                if p:
                    inverse_std(2 * ITEMS + p - 1)
            for b in range(2):
                inverse_std(3 * ITEMS - 1 + b, slice(2 * b, 2 * b + 2))

        def ln(dve, i, n, p, l):
            for t in range(TILES):
                last = dve.bn_stats(stats[i][:, t, :], x[:, TILES * p + t, :])
            last.then_inc(ln_stats[i], 1)
            dve.wait_ge(ln_stats[i], n + 1)
            dve.memset(carrier[:, 0:1], 0.0)
            for t in range(TILES):
                last = dve.bn_aggr(mv[i][:, t, :], stats[i][:, t, :])
            last.then_inc(ln_mv[i], 1)
            dve.wait_ge(ln_mv[i], n + 1)
            dve.tensor_scalar(var[i][:, :], mv[i][:, :, 1], EPS, None, ALU.add).then_inc(ln_var[i], 1)
            vec, loaded = ((vec_a, vec_a_loaded), (vec_f, vec_f_loaded))[i]
            dve.wait_ge(loaded, 48 * (l + 1))
            for t in range(TILES):
                last = dve.scalar_tensor_tensor(out=xh[i][:, t, :], in0=x[:, TILES * p + t, :], scalar=mv[i][:, t, 0:1],
                                                in1=vec[:, 0, :], op0=ALU.subtract, op1=ALU.mult)
            last.then_inc(ln_xhat[i], 1)
            dve.wait_ge(ln_rstd[i], n + 1)
            dve.wait_ge(ln_xhat[i], n + 1)
            for t in range(TILES):
                last = dve.scalar_tensor_tensor(out=xh[i][:, t, :], in0=xh[i][:, t, :], scalar=rstd[i][:, t:t + 1],
                                                in1=vec[:, 1, :], op0=ALU.mult, op1=ALU.add)
            last.then_inc(ln_ready[i], 1)

        def lo(dve, dst, src, hi):
            return dve.tensor_tensor(dst, src, hi.bitcast(F32), ALU.subtract)

        def xt_bank(i, c):
            return (A[:, 2 + c, :], F[:, c, :])[i]

        def dve_xt_lo(dve, i, n):
            for c in range(DC):
                dve.wait_ge(xt_hi[i], 2 * n + c + 1)
                lo(dve, xt[i][:, 1, c, :], xt_bank(i, c), xt[i][:, 0, c, :]).then_inc(xt_lo[i], 1)

        def dve_k_lo(dve, n):
            dve.wait_ge(k_hi, n + 1)
            lo(dve, kt[:, 1, :], A[:, 5, :], kt[:, 0, :]).then_inc(k_lo, 1)

        def heads(ap):
            return ap.rearrange("p t (h e) -> p t h e", h=NH)

        def over_e(ap):
            return ap.rearrange("p t (h o) -> p t h o", o=1).broadcast_to([P, TILES, NH, E])

        def dve_features(dve, n):
            dve.wait_ge(tok_out, 4 * n + 4)
            q = qk[:, :, 0:P]
            dve.tensor_reduce(qmax[:, :, :], heads(q), AX_X, ALU.max).then_inc(qmax_done, 1)
            dve.wait_ge(qmax_done, n + 1)
            dve.wait_ge(q_lo, n + 1)
            dve.tensor_tensor(heads(qexp[:, :, :]), heads(q), over_e(qmax[:, :, :]), ALU.subtract).then_inc(qsub_done, 1)

        def dve_features2(dve, n):
            k = qk[:, :, P:2 * P]
            dve.wait_ge(kexp_done, n + 1)
            dve.tensor_scalar(k, k, 0.0, None, ALU.max).then_inc(krelu_done, 1)
            dve.wait_ge(krelu_done, n + 1)
            dve.scalar_tensor_tensor(out=kexp[:, :, :], in0=kexp[:, :, :], scalar=1.0, in1=k,
                                     op0=ALU.min, op1=ALU.add).then_inc(kf_done, 1)
            dve.wait_ge(qexp_done, n + 1)
            dve.tensor_reduce(qsum[:, :, :], heads(qexp[:, :, :]), AX_X, ALU.add).then_inc(qsum_done, 1)
            dve.wait_ge(qsum_done, n + 1)
            dve.reciprocal(qsum[:, :, :], qsum[:, :, :]).then_inc(qrec_done, 1)
            dve.wait_ge(qrec_done, n + 1)
            dve.tensor_tensor(heads(qexp[:, :, :]), heads(qexp[:, :, :]), over_e(qsum[:, :, :]),
                              ALU.mult).then_inc(qn_done, 1)

        def dve_ctx(dve, n, b):
            dve.wait_ge(ctx_psum, 2 * n + b + 1)
            ps = A[:, 1 - b, 0:3 * NH * HB].rearrange("p (j h e) -> p j h e", j=3, h=NH)
            dve.tensor_scalar(kcum[:, b, :], ps[:, :, 0, E], 1e-6, None, ALU.add).then_inc(kcum_done, 1)
            dve.wait_ge(kcum_done, 2 * n + b + 1)
            dve.reciprocal(kcum[:, b, :], kcum[:, b, :]).then_inc(krec_done, 1)
            dve.wait_ge(krec_done, 2 * n + b + 1)
            for j in range(3):
                last = dve.scalar_tensor_tensor(
                    out=ctxn[:, b, j, :].rearrange("p (h e) -> p h e", h=NH), in0=ps[:, j, :, 0:E],
                    scalar=kcum[:, b, j:j + 1], in1=headmask[:, :, :], op0=ALU.mult, op1=ALU.mult)
            last.then_inc(ctxn_done, 1)

        def later_buckets(ap):
            return ap.rearrange("p (b t) -> p b t", b=2)[:, :, BUCKET:T]

        def dve_lin_lo(dve, n):
            dve.wait_ge(lin_hi, n + 1)
            lo(dve, later_buckets(at[:, 1, 1, :]), later_buckets(A[:, 1, :]),
               later_buckets(at[:, 0, 1, :])).then_inc(lin_lo, 1)

        def dve_max(dve, n, b):
            dve.wait_ge(s_psum, 2 * n + b + 1)
            dve.tensor_reduce(smax[:, b, 0, :], A[:, 2:6, 0:P], AX_X, ALU.max)
            dve.tensor_reduce(smax[:, b, 1, :], A[:, 2:6, P:3 * P], AX_X, ALU.max).then_inc(smax_done, 1)
            dve.wait_ge(smax_done, 2 * n + b + 1)
            dve.tensor_scalar(smax[:, b, :, :], smax[:, b, :, :], -SCALE, None, ALU.mult).then_inc(nmax_done, 1)

        def dve_pt(dve, n, b):
            for r in (1, 2):
                dve.wait_ge(pt_psum, 6 * n + 3 * b + r + 1)
                dve.tensor_copy(pt[:, r, :], A[:, r % 2, :]).then_inc(pt_out_dve, 1)

        def dve_aloc(dve, n, b):
            dve.wait_ge(pv_psum, 2 * n + b + 1)
            ps = A[:, 1, 0:8 * HB].rearrange("p (w e) -> p w e", w=8)
            dve.reciprocal(psum_r[:, :], ps[:, :, E]).then_inc(prec_done, 1)
            dve.wait_ge(prec_done, 2 * n + b + 1)
            dve.tensor_tensor(aloc[:, 2 * b:2 * b + 2, :].rearrange("p t (h e) -> p (t h) e", h=NH), ps[:, :, 0:E],
                              psum_r[:, :].rearrange("p (w o) -> p w o", o=1).broadcast_to([P, 8, E]),
                              ALU.mult).then_inc(aloc_done, 1)

        def dve_al_lo(dve, n):
            dve.wait_ge(al_hi, n + 1)
            lo(dve, at[:, 1, 0, :], A[:, 0, :], at[:, 0, 0, :]).then_inc(al_lo, 1)

        def dve_res1(dve, n, p):
            dve.wait_ge(biased[0], n + 1)
            for t in range(TILES):
                dve.wait_ge(wo_psum, 4 * n + t + 1)
                xs = x[:, TILES * p + t, :]
                dve.tensor_tensor(xs, A[:, (2, 3, 0, 1)[t], 0:D], xs, ALU.add).then_inc(res1, 1)
            dve.wait_ge(res1, 4 * n + 4)

        def dve_h_hi(dve, n, m):
            dve.wait_ge(gelu_done, FC * n + m + 1)
            dve.tensor_copy(ht[:, 0, m, :], hf[:, m % 2, :]).then_inc(h_hi, 1)

        def dve_res2(dve, n, p, t):
            if t == 0:
                dve.wait_ge(biased[1], n + 1)
            dve.wait_ge(y_psum, 4 * n + t + 1)
            xs = x[:, TILES * p + t, :]
            dve.tensor_tensor(xs, F[:, t % 2, 0:D], xs, ALU.add).then_inc(res2, 1)

        @block.vector
        def _(dve):
            dve.memset(qm[:, :, :, :].bitcast(F32), 0.0)
            for i in range(2):
                last = dve.memset(at[:, i, 1, :].bitcast(F32), 0.0)
            last.then_inc(zero_ready, 1)
            dve.wait_ge(x_loaded[0], 16)
            ln(dve, 0, 0, 0, 0)
            for p in range(ITEMS):
                dve.wait_ge(x_loaded[p], 16)
                for t in range(TILES):
                    dve.memset(loaded_mark[:, TILES * p + t:TILES * p + t + 1], 0.0).then_inc(res2, 1)

            def top_k():
                dve.wait_ge(logits_loaded, 64)
                dve.wait_ge(top_const, 5)
                dve.tensor_copy(places[:, :], places_i[:, :])
                dve.tensor_copy(own[:, :], own_i[:, :])
                for f in range(2):
                    dve.scalar_tensor_tensor(out=tie[:, f, :], in0=lrow[:, f, :], scalar=lcol[:, f:f + 1],
                                             in1=earlier[:, :], op0=ALU.is_equal, op1=ALU.mult)
                dve.tensor_reduce(lmax[:, :], lrow[:, :, :], AX_X, ALU.max).then_inc(top_step, 1)
                dve.wait_ge(top_step, 1)
                dve.tensor_scalar(lmax[:, :], lmax[:, :], -1.0, None, ALU.mult).then_inc(top_step, 1)
                for f in range(2):
                    last = dve.scalar_tensor_tensor(out=beats[:, f, :], in0=lrow[:, f, :], scalar=lcol[:, f:f + 1],
                                                    in1=tie[:, f, :], op0=ALU.is_gt, op1=ALU.add)
                last.then_inc(top_step, 1)
                dve.wait_ge(top_step, 3)
                dve.tensor_reduce(rank[:, :], beats[:, :, :], AX_X, ALU.add).then_inc(top_step, 1)
                dve.wait_ge(top_step, 4)
                dve.wait_ge(top_exp, 1)
                dve.scalar_tensor_tensor(out=lexp[:, :], in0=rank[:, :], scalar=TOPK - 0.5, in1=lexp[:, :],
                                         op0=ALU.is_lt, op1=ALU.mult).then_inc(top_step, 1)
                for f in range(2):
                    last = dve.tensor_scalar(chosen[:, f, :], places[:, :], rank[:, f:f + 1], None, ALU.is_equal)
                last.then_inc(top_step, 1)
                dve.wait_ge(top_sum, 1)
                dve.reciprocal(lsum[:, :], F[0:PRIMS, 1, 0:2]).then_inc(top_step, 1)
                dve.wait_ge(top_step, 7)
                dve.tensor_tensor(lw[:, :], lexp[:, :], lsum[:, :], ALU.mult).then_inc(top_step, 1)
                dve.wait_ge(top_step, 8)
                for f in range(2):
                    last = dve.tensor_scalar(lw_wide[:, f, :], ones64[:, :], lw[:, f:f + 1], None, ALU.mult)
                last.then_inc(top_w, 1)
                dve.wait_ge(top_idx, 1)
                dve.tensor_copy(index[:, :], F[0:1, 1, 64:64 + 2 * TOPK]).then_inc(index_ready, 1)
                dve.wait_ge(top_wcol_psum, 1)
                for j in range(2):
                    rows = slice(RANK * j, RANK * j + RANK)
                    last = dve.tensor_copy(wcol[rows, :, :], F[rows, 1, 128 + 32 * j:160 + 32 * j].rearrange(
                        "p (f k) -> p f k", f=2))
                last.then_inc(top_wcol, 1)

            dve_xt_lo(dve, 0, 0)

            def norm_stats(q, p, tiles=range(TILES)):
                for t in tiles:
                    last = dve.bn_stats(tstats[:, t, :], x[:, bass.ds(TILES * p + t, 1), :].rearrange("p a d -> p (a d)"))
                last.then_inc(t_stats, 1)

            def norm_var(q, p, tiles=range(TILES)):
                dve.wait_ge(t_stats, q + 1)
                dve.memset(carrier[:, 0:1], 0.0)
                for t in tiles:
                    last = dve.bn_aggr(tmv[:, t, :], tstats[:, t, :])
                last.then_inc(t_mv, 1)
                dve.wait_ge(t_mv, q + 1)
                dve.tensor_scalar(tvar[:, tiles[0]:tiles[-1] + 1], tmv[:, tiles[0]:tiles[-1] + 1, 1], EPS, None,
                                  ALU.add).then_inc(t_var, 1)

            def norm_scale(q, p, tiles=range(TILES)):
                dve.wait_ge(t_rstd, q + 1)
                for t in tiles:
                    xs = x[:, bass.ds(TILES * p + t, 1), :].rearrange("p a d -> p (a d)")
                    last = dve.tensor_scalar(xs, xs, tmv[:, t, 0:1], trstd[:, t:t + 1], ALU.subtract, ALU.mult)
                last.then_inc(t_norm, 1)

            def norm(*args):
                norm_stats(*args)
                norm_var(*args)
                norm_scale(*args)

            def context():
                dve.wait_ge(wvo_psum, 2)
                for c in range(DC):
                    for s in range(2):
                        dve.wait_ge(ctxt_psum, 2 * c + s + 1)
                        dve.tensor_copy(ctxt[:, c, 4 * s:4 * s + 4, 0:NKV],
                                        A[:, 2 * c + s, :].rearrange("p (b t) -> p b t", b=4)[:, :, 0:NKV]).then_inc(ctxt_out, 1)
                dve.wait_ge(ctxt_out, 4)
                dve.tensor_reduce(ctx_mean[:, :, :], ctxt[:, :, :, 0:NKV], AX_X, ALU.add).then_inc(ctx_sum, 1)
                dve.wait_ge(ctx_sum, 1)
                for c in range(DC):
                    last = dve.tensor_scalar(ctxt[:, c, :, NKV:CB],
                                             ctx_mean[:, c, :].rearrange("p (b o) -> p b o", o=1).broadcast_to([P, B, CB - NKV]),
                                             1.0 / NKV, None, ALU.mult)
                last.then_inc(ctxt_ready, 1)

            def pair_lo(f, kk, j):
                g, r, raw = PAIRS * f + kk, j % 2, j % 4
                w = wcol[:, f, bass.ds(kk, 1)]
                bank = A[:, 4:6, :] if f == 0 or r else F[:, :, :]
                bank = bank.rearrange("p s n -> p (s n)")
                if f == 0:
                    dve.wait_ge(big_hi, g + 1)
                    dve.scalar_tensor_tensor(out=big[r][1], in0=big_raw[:, raw, :], scalar=w, in1=big[r][0].bitcast(F32),
                                             op0=ALU.mult, op1=ALU.subtract).then_inc(big_lo, 1)
                    dve.wait_ge(small_hi, g + 1)
                    lo(dve, small[r][1], A[:, 4 + r, 0:D], small[r][0]).then_inc(small_lo, 1)
                else:
                    dve.wait_ge(small_hi, g + 1)
                    dve.scalar_tensor_tensor(out=small[r][1], in0=small_raw[:, raw, :], scalar=w,
                                             in1=small[r][0].bitcast(F32), op0=ALU.mult, op1=ALU.subtract).then_inc(small_lo, 1)
                    dve.wait_ge(big_hi, g + 1)
                    for s in range(2):
                        half = slice(512 * s, 512 * s + 512)
                        last = lo(dve, big[r][1][:, half], bank[:, half], big[r][0][:, half])
                    last.then_inc(big_lo, 1)

            def pairs_lo(f, first, count, q, p):
                pair_lo(f, first, 2)
                norm_stats(q, p)
                pair_lo(f, first + 1, 3)
                norm_var(q, p)
                for j in range(2, count):
                    pair_lo(f, first + j, 2 + j)
                norm_scale(q, p)

            def composed(dst, src, k):
                dve.wait_ge(comp_hi, k + 1)
                lo(dve, dst(1), src, dst(0)).then_inc(comp_lo, 1)

            def step(l, p, last, mlp=True):
                n = 4 * l + p + 1
                pa = (p + 1) % ITEMS
                attn = not (last and p == ITEMS - 1)
                nxt = not (last and p >= ITEMS - 2)
                la = l + 1 if p == ITEMS - 1 else l

                def h_hi(*chunks):
                    for m in chunks if mlp else ():
                        dve_h_hi(dve, n - 1, m)

                def y_add(t):
                    if mlp:
                        dve_res2(dve, n - 1, p, t)

                if attn:
                    dve_k_lo(dve, n)
                    dve_features(dve, n)
                if mlp:
                    dve_xt_lo(dve, 1, n - 1)
                if not attn:
                    context()
                if attn:
                    dve_features2(dve, n)
                    dve_max(dve, n, 0)
                h_hi(0, 1, 2, 3)
                if attn:
                    dve_ctx(dve, n, 0)
                h_hi(4, 5)
                if attn:
                    dve_ctx(dve, n, 1)
                else:
                    pair_lo(0, 0, 0)
                h_hi(6, 7)
                if attn:
                    dve_lin_lo(dve, n)
                else:
                    pair_lo(0, 1, 1)
                if nxt:
                    if not mlp:
                        dve.wait_ge(x_loaded[1], 16)
                    dve.wait_ge(res2, 4 * (n + 1) + 4)
                    ln(dve, 0, n + 1, (pa + 1) % ITEMS, l + 1 if p >= ITEMS - 2 else l)
                y_add(0)
                y_add(1)
                if attn:
                    dve_pt(dve, n, 0)
                    dve_max(dve, n, 1)
                    dve_aloc(dve, n, 0)
                y_add(2)
                if attn:
                    dve_pt(dve, n, 1)
                if nxt:
                    dve_xt_lo(dve, 0, n + 1)
                y_add(3)
                if attn:
                    dve_aloc(dve, n, 1)
                    dve_al_lo(dve, n)
                    dve_res1(dve, n, pa)
                    ln(dve, 1, n, pa, la)

            step(0, -1, False, mlp=False)
            top_k()
            with dve.Fori(0, DEPTH - 1) as l:
                for p in range(ITEMS):
                    step(l, p, False)
            for p in range(ITEMS):
                step(DEPTH - 1, p, True)

            dve.wait_ge(t_sum, ITEMS)
            with dve.Fori(0, ITEMS - 1) as i:
                pairs_lo(0, 4 * i + 2, 4, i, i)
            pairs_lo(0, PAIRS - 2, 2, ITEMS - 1, ITEMS - 1)
            for u in range(2 * ITEMS):
                if u < 4:
                    composed(*w1_part(u), u)
                if u % 2 == 0:
                    dve.wait_ge(t_bout, u // 2 + 1)
                xs = x[:, 2 * u:2 * u + 2, :].rearrange("p t d -> p (t d)")
                dve.wait_ge(cross_psum, u + 1)
                dve.tensor_tensor(xs, A[:, CROSS_BANKS[u], :], xs, ALU.add).then_inc(cross_added, 1)
            dve.wait_ge(cross_added, 2 * ITEMS)
            pair_lo(1, 0, 0)
            pair_lo(1, 1, 1)
            with dve.Fori(0, ITEMS - 1) as i:
                pairs_lo(1, 4 * i + 2, 4, ITEMS + i, i)
            pairs_lo(1, PAIRS - 2, 2, 2 * ITEMS - 1, ITEMS - 1)

            def f_xt_lo_part(p):
                for c in range(DC):
                    dve.wait_ge(f_xt_hi, 2 * p + c + 1)
                    xb = xt[(p + 1) % 2]
                    lo(dve, xb[:, 1, c, :], f_xt_bank(p, c), xb[:, 0, c, :]).then_inc(f_xt_lo, 1)

            def f_add(p, t):
                xs = x[:, TILES * p + t, :]
                dve.wait_ge(f_y_psum, TILES * p + t + 1)
                dve.tensor_tensor(xs, A[:, t, 0:D], xs, ALU.add).then_inc(f_res, 1)

            def f_h_hi_parts(p, chunks):
                for m in chunks:
                    dve.wait_ge(f_gelu, FC * p + m + 1)
                    dve.tensor_copy(f_ht(p, 0, m), hf[:, m % 2, :]).then_inc(f_h_hi, 1)

            f_xt_lo_part(0)
            for k in range(4):
                composed(*w2_part(k), 4 + k)
            for p in range(ITEMS):
                f_h_hi_parts(p, range(4))
                if p + 1 < ITEMS:
                    f_xt_lo_part(p + 1)
                f_h_hi_parts(p, range(4, FC))
                if p:
                    for t in range(TILES):
                        f_add(p - 1, t)
                    dve.wait_ge(f_res, TILES * p)
                    norm(2 * ITEMS + p - 1, p - 1)
            for b in range(2):
                for t in (2 * b, 2 * b + 1):
                    f_add(ITEMS - 1, t)
                dve.wait_ge(f_res, TILES * (ITEMS - 1) + 2 * b + 2)
                norm(3 * ITEMS - 1 + b, ITEMS - 1, range(2 * b, 2 * b + 2))

        def act_xt_hi(act, i, n):
            for c in range(DC):
                act.wait_ge(xt_psum[i], 2 * n + c + 1)
                act.activation(xt[i][:, 0, c, :], xt_bank(i, c), ACT.Copy).then_inc(xt_hi[i], 1)

        def act_q_copy(act, n):
            act.wait_ge(qk_psum, 2 * n + 1)
            act.activation(qf, A[:, 4, :], ACT.Copy)

        def act_qk_hi(act, n):
            for h in range(NH):
                r = slice(E * h, E * h + E)
                last = act.activation(qm[r, 0, h, :], A[r, 4, :], ACT.Copy)
            last.then_inc(q_hi, 1)
            act.wait_ge(qk_psum, 2 * n + 2)
            act.activation(kt[:, 0, :], A[:, 5, :], ACT.Copy).then_inc(k_hi, 1)

        def act_tok(act, n, t):
            act.wait_ge(tok_psum, 4 * n + t + 1)
            ps = A[:, (2, 3, 0, 1)[t], :]
            act.activation(v8[:, t, :, 0:E], ps[:, 0:2 * P].rearrange("p (h e) -> p h e", e=E), ACT.Copy)
            act.activation(qk[:, t, :], ps[:, 2 * P:4 * P], ACT.Copy).then_inc(tok_out, 1)

        def act_features(act, n):
            act.wait_ge(tok_out, 4 * n + 4)
            act.activation(kexp[:, :, :], qk[:, :, P:2 * P], ACT.Exp).then_inc(kexp_done, 1)
            act.wait_ge(qsub_done, n + 1)
            act.activation(qexp[:, :, :], qexp[:, :, :], ACT.Exp).then_inc(qexp_done, 1)

        def act_qnt(act, n):
            act.wait_ge(qnt_psum, n + 1)
            act.activation(qnt[:, :], A[:, 0, :], ACT.Copy).then_inc(qnt_out, 1)

        def act_lin_hi(act, n):
            act.wait_ge(lin_psum, n + 1)
            act.activation(later_buckets(at[:, 0, 1, :]), later_buckets(A[:, 1, :]), ACT.Copy).then_inc(lin_hi, 1)

        def act_exp(act, n, b):
            act.wait_ge(nmax_done, 2 * n + b + 1)
            for h in range(NH):
                for w, (a, z) in enumerate(((0, P), (P, 3 * P))):
                    last = act.activation(prob[:, h, a:z], A[:, 2 + h, a:z], ACT.Exp, bias=smax[:, b, w, h:h + 1],
                                          scale=SCALE)
            last.then_inc(exp_done, 1)

        def act_pt(act, n, b):
            act.wait_ge(pt_psum, 6 * n + 3 * b + 1)
            act.activation(pt[:, 0, :], A[:, 0, :], ACT.Copy).then_inc(pt_out_act, 1)

        def act_al_hi(act, n):
            act.wait_ge(al_psum, n + 1)
            act.activation(at[:, 0, 0, :], A[:, 0, :], ACT.Copy).then_inc(al_hi, 1)

        def act_b1(act, l):
            act.activation(b1_now[:, :], b1c[:, bass.ds(l * FC, FC)], ACT.Copy).then_inc(b1_turn, 1)
            act.wait_ge(b1_turn, l + 1)

        def act_gelu(act, n, m, l):
            act.wait_ge(h_psum, FC * n + m + 1)
            act.wait_ge(h_lo, FC * n + m + 1)
            act.activation(hf[:, m % 2, :], F[:, m % 2, :], ACT.Gelu,
                           bias=b1_now[:, m:m + 1]).then_inc(gelu_done, 1)

        @block.scalar
        def _(act):
            act.wait_ge(const_ready, 1)
            act.wait_ge(zero_ready, 1)
            act_xt_hi(act, 0, 0)
            act_q_copy(act, 0)
            act_qk_hi(act, 0)

            def pair_hi(f, kk, j, peel):
                g, r, raw = PAIRS * f + kk, j % 2, j % 4
                w = wcol[:, f, bass.ds(kk, 1)]
                loads = 32 * (PAIRS // 4) * f + 8 * (kk + (4 - raw))
                act.wait_ge(big_loaded[raw], loads)
                act.wait_ge(small_loaded[raw], loads)
                if not peel:
                    act.wait_ge(pair_done, g - 1)
                    act.activation(carrier[:, 1 + r:2 + r], ones[:, :], ACT.Copy)
                if f == 0:
                    act.activation(big[r][0], big_raw[:, raw, :], ACT.Copy, scale=w).then_inc(big_hi, 1)
                    act.wait_ge(at_psum, g + 1)
                    act.activation(small[r][0], A[:, 4 + r, 0:D], ACT.Copy).then_inc(small_hi, 1)
                else:
                    act.activation(small[r][0], small_raw[:, raw, :], ACT.Copy, scale=w).then_inc(small_hi, 1)
                    act.wait_ge(at_psum, g + 1)
                    for s in range(2):
                        last = act.activation(big[r][0][:, 512 * s:512 * s + 512], (F, A)[r][:, 4 * r + s, :], ACT.Copy)
                    last.then_inc(big_hi, 1)

            def step(l, p, last, mlp=True):
                n = 4 * l + p + 1
                attn = not (last and p == ITEMS - 1)
                nxt = not (last and p >= ITEMS - 2)

                def gelu(*chunks):
                    for m in chunks if mlp else ():
                        act_gelu(act, n - 1, m, l)

                if attn:
                    for t in range(TILES):
                        act_tok(act, n, t)
                if not attn:
                    for k in range(4):
                        act.wait_ge(wvt_psum, k + 1)
                        act.activation(wvt[:, 2 * k:2 * k + 2, :].rearrange("p j i -> p (j i)"),
                                       A[:, WVT_BANKS[k], :], ACT.Copy).then_inc(wvt_out, 1)
                if mlp:
                    act_xt_hi(act, 1, n - 1)
                if attn:
                    act_features(act, n)
                else:
                    for c in range(DC):
                        act.wait_ge(wvo_psum, c + 1)
                        act.activation(wvo[:, c, :], A[:, 4 + c, 0:D], ACT.Copy).then_inc(wvo_out, 1)
                gelu(0, 1, 2)
                if attn:
                    act_qnt(act, n)
                gelu(3, 4)
                if not attn:
                    pair_hi(0, 0, 0, True)
                gelu(5, 6, 7)
                if not attn:
                    pair_hi(0, 1, 1, True)
                if attn:
                    act_lin_hi(act, n)
                    act_exp(act, n, 0)
                    act_pt(act, n, 0)
                    act_exp(act, n, 1)
                if attn:
                    act_pt(act, n, 1)
                if nxt:
                    act_xt_hi(act, 0, n + 1)
                    act_q_copy(act, n + 1)
                if attn:
                    act_al_hi(act, n)
                if nxt:
                    act_qk_hi(act, n + 1)

            step(0, -1, False, mlp=False)
            act.wait_ge(top_step, 2)
            for f in range(2):
                last = act.activation(lexp[:, f:f + 1], lcol[:, f:f + 1], ACT.Exp, bias=lmax[:, f:f + 1])
            last.then_inc(top_exp, 1)
            act.wait_ge(b1_psum, 1)
            act.activation(b1c[:, :], F[:, 0, 0:DEPTH * FC], ACT.Copy).then_inc(b1_ready, 1)
            act.wait_ge(b1_ready, 1)
            act.wait_ge(top_wcol, 1)

            with act.Fori(0, DEPTH - 1) as l:
                act_b1(act, l)
                for p in range(ITEMS):
                    step(l, p, False)
            act_b1(act, DEPTH - 1)
            for p in range(ITEMS):
                step(DEPTH - 1, p, True)

            with act.Fori(0, ITEMS - 1) as i:
                for j in range(4):
                    pair_hi(0, 4 * i + 2 + j, 2 + j, False)
            for kk in (PAIRS - 2, PAIRS - 1):
                pair_hi(0, kk, kk % 4, False)
            act.wait_ge(pair_done, PAIRS)
            for k in range(4):
                dst, src = w1_part(k)
                act.activation(dst(0), src, ACT.Copy).then_inc(comp_hi, 1)
            with act.Fori(0, PAIRS // 4) as i:
                for j in range(4):
                    pair_hi(1, 4 * i + j, j, False)

            def f_xt_hi_part(p):
                for c in range(DC):
                    act.wait_ge(f_xt_psum, 2 * p + c + 1)
                    act.activation(xt[(p + 1) % 2][:, 0, c, :], f_xt_bank(p, c), ACT.Copy).then_inc(f_xt_hi, 1)

            f_xt_hi_part(0)
            act.wait_ge(pair_done, 2 * PAIRS)
            for k in range(4):
                dst, src = w2_part(k)
                act.activation(dst(0), src, ACT.Copy).then_inc(comp_hi, 1)
            for p in range(ITEMS):
                for m in range(FC):
                    if m == 4 and p + 1 < ITEMS:
                        f_xt_hi_part(p + 1)
                    act.wait_ge(f_h_psum, FC * p + m + 1)
                    if FC * p + m >= 2:
                        act.wait_ge(f_h_lo, FC * p + m - 1)
                    act.activation(hf[:, m % 2, :], F[:, m % 2, :], ACT.Gelu_apprx_tanh).then_inc(f_gelu, 1)

        def pe_xt(pe, i, n):
            pe.wait_ge(ln_ready[i], n + 1)
            for c in range(DC):
                for t in range(TILES):
                    last = pe.transpose(xt_bank(i, c)[:, P * t:P * t + P], xh[i][:, t, P * c:P * c + P], ident[:, :])
                last.then_inc(xt_psum[i], 1)

        def product(pe, out, lhs, rhs):
            total = [(c, a, b) for c in range(DC) for a, b in PASSES]
            for k, (c, a, b) in enumerate(total):
                last = pe.matmul(out, lhs(a, c), rhs(b, c), start=k == 0, stop=k == len(total) - 1)
            return last

        def pe_qk(pe, n, l, i):
            if i == 0:
                pe.wait_ge(xt_lo[0], 2 * n + 2)
                pe.wait_ge(wa_ready, l + 1)
            product(pe, A[:, 4 + i, :], lambda a, c: wa[:, a, c, P * i:P * i + P],
                    lambda b, c: xt[0][:, b, c, :]).then_inc(qk_psum, 1)

        def pe_tok(pe, n, t):
            product(pe, A[:, (2, 3, 0, 1)[t], :], lambda a, c: xt[0][:, a, c, P * t:P * t + P],
                    lambda b, c: wa[:, b, c, 2 * P:6 * P]).then_inc(tok_psum, 1)

        def pe_s(pe, n, b):
            pe.wait_ge(k_lo, n + 1)
            pe.wait_ge(q_lo, n + 1)
            if b == 0:
                pe.wait_ge(tok_out, 4 * n + 4)
            else:
                pe.wait_ge(exp_done, 2 * n + 1)
            for h in range(NH):
                pe.matmul(A[:, 2 + h, 0:3 * P], ident_bf[:, :], mask_bf[:, :], start=True, stop=False)
                for w, (c0, c1, t, k1) in enumerate(((0, P, 2 * b, 1), (P, 3 * P, 2 * b + 1, 2))):
                    for k, (i, j) in enumerate(PASSES):
                        last = pe.matmul(A[:, 2 + h, c0:c1], qm[:, i, h, P * t:P * t + P],
                                         kt[:, j, 2 * b * P:(2 * b + k1) * P], start=False, stop=w == 1 and k == 2)
            last.then_inc(s_psum, 1)

        def pe_qnt(pe, n):
            pe.wait_ge(qn_done, n + 1)
            for t in range(TILES):
                last = pe.transpose(A[:, 0, P * t:P * t + P], qexp[:, t, :], ident[:, :])
            last.then_inc(qnt_psum, 1)

        def pe_ctx(pe, n, b):
            pe.wait_ge(kf_done, n + 1)
            if b == 1:
                pe.wait_ge(qnt_out, n + 1)
            w = NH * HB

            def part(j, t, rows, start, stop):
                return pe.matmul(A[:, 1 - b, j * w:(j + 1) * w], kexp[0:rows, t, :],
                                 v8[0:rows, t, NH:2 * NH, :].rearrange("p h e -> p (h e)"), start=start, stop=stop)
            part(0, 2 * b, BUCKET, True, True)
            part(1, 2 * b, P, True, True)
            part(2, 2 * b, P, True, False)
            part(2, 2 * b + 1, BUCKET, False, True).then_inc(ctx_psum, 1)

        def pe_lin(pe, n):
            pe.wait_ge(ctxn_done, 2 * n + 2)
            pe.wait_ge(qnt_out, n + 1)
            for b in range(2):
                for u in range(1, 4):
                    cols = slice(b * T + u * BUCKET, b * T + (u + 1) * BUCKET)
                    last = pe.matmul(A[:, 1, cols], ctxn[:, b, u - 1, :], qnt[:, cols], start=True, stop=True)
            last.then_inc(lin_psum, 1)

        def pe_pt(pe, n, b):
            pe.wait_ge(exp_done, 2 * n + b + 1)
            for r in range(3):
                if r == 0:
                    if b == 0:
                        pe.wait_ge(ctxn_done, 2 * n + 2)
                    else:
                        pe.wait_ge(pt_out_dve, 4 * n + 2)
                if r == 1:
                    if b == 0:
                        pe.wait_ge(lin_lo, n + 1)
                    else:
                        pe.wait_ge(aloc_done, 2 * n + 1)
                if r == 2:
                    pe.wait_ge(pt_out_act, 2 * n + b + 1)
                for h in range(NH):
                    last = pe.transpose(A[:, r % 2, P * h:P * h + P], prob[:, h, P * r:P * r + P], ident[:, :])
                last.then_inc(pt_psum, 1)

        def pe_pv(pe, n, b):
            pe.wait_ge(pt_out_act, 2 * n + b + 1)
            pe.wait_ge(pt_out_dve, 4 * n + 2 * b + 2)
            for w in range(2):
                for h in range(NH):
                    parts = ((0, 0),) if w == 0 else ((1, 0), (2, 1))
                    for k, (r, t) in enumerate(parts):
                        last = pe.matmul(A[:, 1, (NH * w + h) * HB:(NH * w + h + 1) * HB],
                                         pt[:, r, P * h:P * h + P], v8[:, 2 * b + t, h, :],
                                         start=k == 0, stop=k == len(parts) - 1)
            last.then_inc(pv_psum, 1)

        def pe_al(pe, n):
            pe.wait_ge(aloc_done, 2 * n + 2)
            pe.wait_ge(pt_out_dve, 4 * n + 4)
            for t in range(TILES):
                last = pe.transpose(A[:, 0, P * t:P * t + P], aloc[:, t, :], ident[:, :])
            last.then_inc(al_psum, 1)

        def pe_wo(pe, n, l):
            pe.wait_ge(al_lo, n + 1)
            pe.wait_ge(lin_lo, n + 1)
            pe.wait_ge(wo_ready, l + 1)
            pe.wait_ge(exp_done, 2 * n + 2)
            for t in range(TILES):
                product(pe, A[:, (2, 3, 0, 1)[t], 0:D], lambda a, c: at[:, a, c, P * t:P * t + P],
                        lambda b, c: wo[:, b, c, :]).then_inc(wo_psum, 1)

        def pe_h(pe, n, m, l, first=False):
            if m == 0:
                pe.wait_ge(xt_lo[1], 2 * n + 2)
                pe.wait_ge(w1_ready, l + 1)
            if m >= 2:
                pe.wait_ge(gelu_done, FC * n + m - 1)
            product(pe, F[:, m % 2, :], lambda a, c: w1[:, a, c, P * m:P * m + P],
                    lambda b, c: xt[1][:, b, c, :]).then_inc(h_psum, 1)

        def pe_y(pe, n, t, l):
            if t == 0:
                pe.wait_ge(h_lo, H_LO_0 + FC * n + FC)
                pe.wait_ge(w2_ready, l + 1)
            if t < 2:
                pe.wait_ge(gelu_done, FC * n + FC - 1 + t)
            else:
                pe.wait_ge(res2, RES2_0 + 4 * n + t - 1)
            passes = [(c, a, b) for c in range(FC) for a, b in PASSES]
            for k, (c, a, b) in enumerate(passes):
                last = pe.matmul(F[:, t % 2, 0:D], ht[:, a, c, P * t:P * t + P], w2[:, b, c, :],
                                 start=k == 0, stop=k == len(passes) - 1)
            last.then_inc(y_psum, 1)

        @block.tensor
        def _(pe):
            pe.wait_ge(const_ready, 1)
            pe.wait_ge(zero_ready, 1)

            def top_k():
                bank = F[:, 1, :]
                pe.wait_ge(top_step, 5)
                pe.matmul(bank[0:PRIMS, 0:2], ones64[:, 0:PRIMS], lexp[:, :], start=True, stop=True).then_inc(top_sum, 1)
                pe.wait_ge(top_step, 7)
                both = chosen[:, :, :].rearrange("i f k -> i (f k)")
                pe.matmul(bank[0:1, 64:64 + 2 * TOPK], own[:, :], both, start=True, stop=True).then_inc(top_idx, 1)
                pe.wait_ge(top_w, 1)
                pe.wait_ge(index_ready, 1)
                for j in range(2):
                    for f in range(2):
                        last = pe.matmul(bank[:, 128 + 32 * j + 16 * f:144 + 32 * j + 16 * f], lw_wide[:, f, :],
                                         chosen[:, f, :].rearrange("i (k j) -> i j k", j=2)[:, j, :], start=True, stop=True)
                last.then_inc(top_wcol_psum, 1)

            pe_xt(pe, 0, 0)
            for i in range(2):
                pe_qk(pe, 0, 0, i)

            def context():
                pe.wait_ge(wv_loaded, 16)
                pe.wait_ge(res1, 16 * DEPTH)
                for k in range(4):
                    for j in (2 * k, 2 * k + 1):
                        for c in range(DC):
                            last = pe.transpose(A[:, WVT_BANKS[k], (j % 2) * D + P * c:(j % 2) * D + P * c + P],
                                                wv_raw[:, c, P * j:P * j + P], ident[:, :])
                    last.then_inc(wvt_psum, 1)

            def value_output():
                pe.wait_ge(wvt_out, 4)
                pe.wait_ge(wout_loaded, 16)
                for c in range(DC):
                    for j in range(FC):
                        last = pe.matmul(A[:, 4 + c, 0:D], wvt[:, j, P * c:P * c + P], wout_raw[:, j, :],
                                         start=j == 0, stop=j == FC - 1)
                    last.then_inc(wvo_psum, 1)
                pe.wait_ge(ctx_loaded, 16)
                for c in range(DC):
                    for s in range(2):
                        for b in range(4):
                            last = pe.transpose(A[:, 2 * c + s, P * b:P * b + NKV],
                                                ctx_raw[:, 4 * s + b, P * c:P * c + P], ident[0:NKV, 0:NKV])
                        last.then_inc(ctxt_psum, 1)

            def turn(f, kk, j):
                g, r, raw = PAIRS * f + kk, j % 2, j % 4
                pe.wait_ge((small_loaded, big_loaded)[f][raw], 32 * (PAIRS // 4) * f + 8 * (kk + (4 - raw)))
                if not (type(kk) is int and kk < 2):
                    pe.wait_ge((small_lo, big_lo)[f], g - 1)
                if f == 0:
                    for c in range(DC):
                        last = pe.transpose(A[:, 4 + r, P * c:P * c + P], small_raw[:, raw, P * c:P * c + P], ident[:, :])
                else:
                    for m in range(FC):
                        last = pe.transpose((F, A)[r][:, 4 * r + m // 4, P * (m % 4):P * (m % 4) + P],
                                            big_raw[:, raw, P * m:P * m + P], ident[:, :])
                last.then_inc(at_psum, 1)

            def multiply(f, kk, j, first, final):
                g, r = PAIRS * f + kk, j % 2
                pe.wait_ge(small_hi, g + 1)
                pe.wait_ge(big_hi, g + 1)
                for k, (a, b) in enumerate(PASSES):
                    if k == 1:
                        pe.wait_ge((small_lo, big_lo)[f], g + 1)
                    if k == 2:
                        pe.wait_ge((big_lo, small_lo)[f], g + 1)
                    if f == 0:
                        for c in range(DC):
                            for s in range(2):
                                last = pe.matmul(A[:, 2 * c + s, :], small[r][a][:, P * c:P * c + P],
                                                 big[r][b][:, 512 * s:512 * s + 512], start=first and k == 0,
                                                 stop=final and k == 2, skip_group_check=True)
                    else:
                        for m in range(FC):
                            last = pe.matmul(A[:, m // 2, D * (m % 2):D * (m % 2) + D], big[r][a][:, P * m:P * m + P],
                                             small[r][b], start=first and k == 0 and m % 2 == 0,
                                             stop=final and k == 2, skip_group_check=True)
                last.then_inc(pair_done, 1)

            def compose(f):
                with pe.Fori(0, ITEMS - 1) as i:
                    for j in range(4):
                        turn(f, 4 * i + 3 + j, 3 + j)
                        multiply(f, 4 * i + 2 + j, 2 + j, False, False)
                turn(f, PAIRS - 1, PAIRS - 1)
                multiply(f, PAIRS - 2, PAIRS - 2, False, False)
                if f == 0:
                    pe.wait_ge(res2, RES2_0 + 16 * DEPTH)
                    turn(1, 0, 0)
                else:
                    pe.wait_ge(big_lo, 2 * PAIRS - 1)
                    f_xt(0)
                multiply(f, PAIRS - 1, PAIRS - 1, False, True)

            def step(l, p, last, mlp=True):
                n = 4 * l + p + 1
                attn = not (last and p == ITEMS - 1)
                nxt = not (last and p >= ITEMS - 2)
                la = l + 1 if p == ITEMS - 1 else l

                def h(*chunks):
                    for m in chunks if mlp else ():
                        pe_h(pe, n - 1, m, l)

                def y(t):
                    if mlp:
                        pe_y(pe, n - 1, t, l)

                if attn:
                    for t in range(TILES):
                        if mlp:
                            pe.wait_ge(res1, 4 * n + t - 3)
                        pe_tok(pe, n, t)
                if not attn:
                    context()
                if mlp:
                    pe.wait_ge(res2, RES2_0 + 4 * (n - 1))
                    pe_xt(pe, 1, n - 1)
                if attn:
                    pe_s(pe, n, 0)
                else:
                    value_output()
                h(0, 1, 2)
                if attn:
                    pe_qnt(pe, n)
                h(3)
                if attn:
                    pe_ctx(pe, n, 0)
                h(4, 5)
                if attn:
                    pe_ctx(pe, n, 1)
                else:
                    pe.wait_ge(wvo_out, 2)
                    turn(0, 0, 0)
                    turn(0, 1, 1)
                h(6, 7)
                if attn:
                    pe_lin(pe, n)
                else:
                    pe.wait_ge(ctxt_out, 4)
                    multiply(0, 0, 0, True, False)
                y(0)
                y(1)
                if attn:
                    pe_pt(pe, n, 0)
                    pe_s(pe, n, 1)
                    pe_pv(pe, n, 0)
                y(2)
                y(3)
                if attn:
                    pe_pt(pe, n, 1)
                if nxt:
                    pe.wait_ge(exp_done, 2 * n + 2)
                    pe_xt(pe, 0, n + 1)
                if attn:
                    pe_pv(pe, n, 1)
                if nxt:
                    pe_qk(pe, n + 1, l + 1 if p >= ITEMS - 2 else l, 0)
                if attn:
                    pe_al(pe, n)
                if nxt:
                    pe_qk(pe, n + 1, l + 1 if p >= ITEMS - 2 else l, 1)
                if attn:
                    pe_wo(pe, n, la)

            step(0, -1, False, mlp=False)
            top_k()
            pe.wait_ge(b1_loaded, 16)
            pe.transpose(F[:, 0, 0:DEPTH * FC], b1_rows[:, :], ident[0:DEPTH * FC, 0:DEPTH * FC]).then_inc(b1_psum, 1)
            pe.wait_ge(b1_ready, 1)
            pe.wait_ge(top_wcol, 1)

            with pe.Fori(0, DEPTH - 1) as l:
                for p in range(ITEMS):
                    step(l, p, False)
            for p in range(ITEMS):
                step(DEPTH - 1, p, True)

            def f_xt(p):
                pe.wait_ge(t_norm, ITEMS + p + 1)
                if p >= 2:
                    pe.wait_ge(f_xt_lo, 2 * p)
                for c in range(DC):
                    for t in range(TILES):
                        last = pe.transpose(f_xt_bank(p, c)[:, P * t:P * t + P],
                                            x[:, TILES * p + t, P * c:P * c + P], ident[:, :])
                    last.then_inc(f_xt_psum, 1)

            turn(0, 2, 2)
            multiply(0, 1, 1, False, False)
            compose(0)
            pe.wait_ge(pair_done, PAIRS)
            pe.wait_ge(ctxt_ready, 1)
            pe.wait_ge(wvo_out, 2)
            for u in range(2 * ITEMS):
                if 2 <= u < 6:
                    pe.wait_ge(comp_lo, u - 1)
                if u >= 6:
                    pe.wait_ge(cross_added, u - 5)
                for t in range(2):
                    for c in range(DC):
                        rows = ctxt[:, c, u, :] if t == 0 else ctxt[:, c, u, NKV:NKV + 1].broadcast_to([P, P])
                        last = pe.matmul(A[:, CROSS_BANKS[u], D * t:D * t + D], rows, wvo[:, c, :],
                                         start=c == 0, stop=c == DC - 1)
                last.then_inc(cross_psum, 1)
            pe.wait_ge(cross_added, 2 * ITEMS)
            turn(1, 1, 1)
            multiply(1, 0, 0, True, False)
            turn(1, 2, 2)
            multiply(1, 1, 1, False, False)
            compose(1)

            def f_h(p, m):
                if m == 0:
                    pe.wait_ge(f_xt_lo, 2 * p + 2)
                if FC * p + m >= 2:
                    pe.wait_ge(f_gelu, FC * p + m - 1)
                product(pe, F[:, m % 2, :], lambda a, c: w1[:, a, c, P * m:P * m + P],
                        lambda b, c: xt[(p + 1) % 2][:, b, c, :]).then_inc(f_h_psum, 1)

            def f_y(p):
                pe.wait_ge(f_h_lo, FC * p + FC)
                if p == 0:
                    pe.wait_ge(comp_lo, 8)
                for t in range(TILES):
                    if p:
                        pe.wait_ge(f_res, TILES * (p - 1) + t + 1)
                    passes = [(c, a, b) for c in range(FC) for a, b in PASSES]
                    for k, (c, a, b) in enumerate(passes):
                        last = pe.matmul(A[:, t, 0:D], f_ht(p, a, c)[:, P * t:P * t + P], w2[:, b, c, :],
                                         start=k == 0, stop=k == len(passes) - 1)
                    last.then_inc(f_y_psum, 1)

            for p in range(ITEMS):
                for m in range(FC):
                    if m == 4 and p + 1 < ITEMS:
                        f_xt(p + 1)
                    f_h(p, m)
                if p:
                    f_y(p - 1)
            f_y(ITEMS - 1)


_INS = ['x', 'L0_attn_Wq', 'L0_attn_Wk', 'L0_attn_Wv', 'L0_attn_Wo', 'L0_attn_bo', 'L0_attn_ln1_g', 'L0_attn_ln1_b',
        'L0_attn_W1', 'L0_attn_b1', 'L0_attn_W2', 'L0_attn_b2', 'L0_attn_ln2_g', 'L0_attn_ln2_b',
        'ctx_1024', 'L0_xattn_Wkv', 'L0_xattn_Wout', 'L0_xattn_bout', 'L0_ffn_fc1_A', 'L0_ffn_fc1_B', 'L0_ffn_fc2_A',
        'L0_ffn_fc2_B', 'L0_ffn_fc1_logits', 'L0_ffn_fc2_logits']
_OUTS = [((8, 256, 256), 'float32')]


def kernel(**inputs):
    import numpy as _np
    import concourse.bacc as _bacc
    from concourse import mybir as _mybir
    from concourse.bass_utils import run_bass_kernel_spmd as _run

    nc = _bacc.Bacc("TRN2", target_bir_lowering=False, num_devices=1)
    arrays, args = {}, []
    for name in _INS:
        a = _np.ascontiguousarray(inputs[name])
        arrays[f"in_{name}_dram"] = a
        args.append(nc.dram_tensor(f"in_{name}_dram", a.shape, _mybir.dt.from_np(a.dtype), kind="ExternalInput").ap())
    for i, (shape, dtype) in enumerate(_OUTS):
        dt = _mybir.dt.from_np(_np.dtype(dtype))
        args.append(nc.dram_tensor(f"out_{i}_dram", shape, dt, kind="ExternalOutput").ap())
    build(nc, *args)
    r = _run(nc, [arrays], core_ids=[0])
    got = tuple(r.results[0][f"out_{i}_dram"] for i in range(len(_OUTS)))
    return got[0]
```
